# Optimizing a Trainium2 kernel written in Bass

```python
import numpy as np
import jax
import jax.numpy as jnp

def _softmax(x, axis=-1):
    return jax.nn.softmax(x, axis=axis)

def _gelu(x):
    return jax.nn.gelu(x, approximate=True)

def _silu(x):
    return jax.nn.silu(x)

def _sigmoid(x):
    return jax.nn.sigmoid(x)

def _layernorm(x, axis=-1, eps=1e-05):
    m = jnp.mean(x, axis=axis, keepdims=True)
    v = jnp.var(x, axis=axis, keepdims=True)
    return (x - m) / jnp.sqrt(v + eps)

def _scatter_add(tgt, idx, src, axis=0):
    return tgt.at[idx].add(src)

def _segment_sum(src, seg, n):
    return jax.ops.segment_sum(src, seg, n)
kernel_name = 'mk_prb_d2_jaxref_r8_63bffe'

def setup_inputs(seed: int=0):
    np.random.seed(seed)
    _w = jnp.asarray

    def _L0_attn_setup():
        import jax, jax.numpy as jnp
        import numpy as np
        D_MODEL = 128
        N_HEADS = 16
        HEAD_DIM = D_MODEL // N_HEADS
        WINDOW = 128
        LOCAL_BLOCK = 32
        LATENT_TOKENS = 64
        LATENT_D = 32
        LATENT_HEADS = 4
        LATENT_HD = LATENT_D // LATENT_HEADS
        NEG = -1000000000.0

        def _local_attention(q, k, v):
            B, H, S, hd = q.shape
            bs = min(S, max(WINDOW, LOCAL_BLOCK))
            nb = S // bs
            w = WINDOW
            L = bs + w - 1
            k_pad = jnp.pad(k, ((0, 0), (0, 0), (w - 1, 0), (0, 0)))
            v_pad = jnp.pad(v, ((0, 0), (0, 0), (w - 1, 0), (0, 0)))
            starts = jnp.arange(nb) * bs
            idx = starts[:, None] + jnp.arange(L)[None, :]
            kb = k_pad[:, :, idx]
            vb = v_pad[:, :, idx]
            qb = q.reshape(B, H, nb, bs, hd)
            q_pos = starts[:, None] + jnp.arange(bs)[None, :]
            k_gpos = starts[:, None] + jnp.arange(L)[None, :] - (w - 1)
            dist = q_pos[:, :, None] - k_gpos[:, None, :]
            allowed = (dist > 0) & (dist <= w) & (k_gpos[:, None, :] >= 0)
            scale = 1.0 / np.sqrt(hd)
            scores = jnp.einsum('bhnqd,bhnkd->bhnqk', qb, kb) * scale
            scores = jnp.where(allowed, scores, NEG)
            attn = jax.nn.softmax(scores, axis=-1)
            attn = jnp.where(allowed.any(-1)[None, None, :, :, None], attn, 0.0)
            out = jnp.einsum('bhnqk,bhnkd->bhnqd', attn, vb)
            return out.reshape(B, H, S, hd)
        key = jax.random.key(seed)
        ks = jax.random.split(key, 14)
        B, S = (2, 512)
        s = 0.02
        f32 = jnp.float32
        return {'x': jax.random.normal(ks[0], (B, S, D_MODEL), f32), 'qkv_w': jax.random.normal(ks[1], (D_MODEL, 3 * D_MODEL), f32) * s, 'qkv_b': jnp.zeros((3 * D_MODEL,), f32), 'rq_w': jax.random.normal(ks[2], (D_MODEL, LATENT_D), f32) * s, 'rq_b': jnp.zeros((LATENT_D,), f32), 'rkv_w': jax.random.normal(ks[3], (D_MODEL, 2 * LATENT_D), f32) * s, 'rkv_b': jnp.zeros((2 * LATENT_D,), f32), 'rout_w': jax.random.normal(ks[4], (LATENT_D, D_MODEL), f32) * s, 'rout_b': jnp.zeros((D_MODEL,), f32), 'out_w': jax.random.normal(ks[5], (D_MODEL, D_MODEL), f32) * s, 'out_b': jnp.zeros((D_MODEL,), f32), 'gl_w': jax.random.normal(ks[6], (HEAD_DIM, 1), f32) * s, 'gr_w': jax.random.normal(ks[7], (HEAD_DIM, 1), f32) * s}
    _L0_attn_in = _L0_attn_setup()

    def _L0_ffn_setup():
        import jax, jax.numpy as jnp
        import numpy as np
        LN_EPS = 0.001
        EPS = 1e-05
        QB = 128.0

        def ste_round(x):
            return x + jax.lax.stop_gradient(jnp.round(x) - x)
        key = jax.random.key(seed)
        k1, k2 = jax.random.split(key)
        x = jax.random.normal(k1, (4, 1024, 128), dtype=jnp.float32)
        weight = jax.random.normal(k2, (128, 128), dtype=jnp.float32) * 0.02
        ln_gamma = jnp.ones((128,), dtype=jnp.float32)
        ln_beta = jnp.zeros((128,), dtype=jnp.float32)
        return {'x': x, 'weight': weight, 'ln_gamma': ln_gamma, 'ln_beta': ln_beta}
    _L0_ffn_in = _L0_ffn_setup()

    def _L1_attn_setup():
        import jax, jax.numpy as jnp
        import numpy as np
        B, T, C, H = (4, 128, 128, 16)
        D = C // H

        def _expmap0_split(u):
            mink = -u[..., :1] ** 2 + jnp.sum(u[..., 1:] ** 2, axis=-1, keepdims=True)
            nomin = jnp.sqrt(jnp.maximum(mink, 1e-08))
            time = jnp.cosh(nomin)
            space = jnp.sinh(nomin) * u[..., 1:] / nomin
            return (time, space)
        key = jax.random.key(seed)
        ks = jax.random.split(key, 6)
        s = 1.0 / np.sqrt(C)
        return {'x': jax.random.normal(ks[0], (B, T, C), jnp.float32), 'W_qkv': jax.random.normal(ks[1], (C, 3 * C), jnp.float32) * s, 'b_qkv': jnp.zeros((3 * C,), jnp.float32), 'W_out': jax.random.normal(ks[2], (C, C), jnp.float32) * s, 'b_out': jnp.zeros((C,), jnp.float32), 'w_sur': jax.random.normal(ks[3], (C,), jnp.float32) * s, 'b_sur': jnp.zeros((), jnp.float32), 'threshold': jnp.float32(0.5)}
    _L1_attn_in = _L1_attn_setup()

    def _L1_ffn_setup():
        import jax, jax.numpy as jnp
        import numpy as np
        D_IN, D_HID = (128, 512)

        def _ternary(key, shape):
            return jax.random.randint(key, shape, -1, 2).astype(jnp.float32)

        def _tlin(x, w, s):
            return jnp.einsum('bsi,oi->bso', x, w) * s
        key = jax.random.key(seed)
        ks = jax.random.split(key, 12)
        inv = lambda fan: 1.0 / np.sqrt(fan).astype(np.float32)
        return {'x': jax.random.normal(ks[0], (4, 256, D_IN), dtype=jnp.float32), 'w1_w': _ternary(ks[1], (D_HID, D_IN)), 'w1_s': jax.random.uniform(ks[2], (D_HID,), dtype=jnp.float32) * inv(D_IN), 'w2_w': _ternary(ks[3], (D_HID, D_IN)), 'w2_s': jax.random.uniform(ks[4], (D_HID,), dtype=jnp.float32) * inv(D_IN), 'h1_w': _ternary(ks[5], (D_HID, D_HID)), 'h1_s': jax.random.uniform(ks[6], (D_HID,), dtype=jnp.float32) * inv(D_HID), 'h2_w': _ternary(ks[7], (D_HID, D_HID)), 'h2_s': jax.random.uniform(ks[8], (D_HID,), dtype=jnp.float32) * inv(D_HID), 'w3_w': _ternary(ks[9], (D_IN, D_HID)), 'w3_s': jax.random.uniform(ks[10], (D_IN,), dtype=jnp.float32) * inv(D_HID)}
    _L1_ffn_in = _L1_ffn_setup()
    _d = {'L0_attn_x': _L0_attn_in['x'], 'L0_attn_qkv_w': _L0_attn_in['qkv_w'], 'L0_attn_qkv_b': _L0_attn_in['qkv_b'], 'L0_attn_rq_w': _L0_attn_in['rq_w'], 'L0_attn_rq_b': _L0_attn_in['rq_b'], 'L0_attn_rkv_w': _L0_attn_in['rkv_w'], 'L0_attn_rkv_b': _L0_attn_in['rkv_b'], 'L0_attn_rout_w': _L0_attn_in['rout_w'], 'L0_attn_rout_b': _L0_attn_in['rout_b'], 'L0_attn_out_w': _L0_attn_in['out_w'], 'L0_attn_out_b': _L0_attn_in['out_b'], 'L0_attn_gl_w': _L0_attn_in['gl_w'], 'L0_attn_gr_w': _L0_attn_in['gr_w'], 'L0_ffn_weight': _L0_ffn_in['weight'], 'L0_ffn_ln_gamma': _L0_ffn_in['ln_gamma'], 'L0_ffn_ln_beta': _L0_ffn_in['ln_beta'], 'L1_attn_W_qkv': _L1_attn_in['W_qkv'], 'L1_attn_b_qkv': _L1_attn_in['b_qkv'], 'L1_attn_W_out': _L1_attn_in['W_out'], 'L1_attn_b_out': _L1_attn_in['b_out'], 'L1_attn_w_sur': _L1_attn_in['w_sur'], 'L1_attn_b_sur': _L1_attn_in['b_sur'], 'L1_attn_threshold': _L1_attn_in['threshold'], 'L1_ffn_w1_w': _L1_ffn_in['w1_w'], 'L1_ffn_w1_s': _L1_ffn_in['w1_s'], 'L1_ffn_w2_w': _L1_ffn_in['w2_w'], 'L1_ffn_w2_s': _L1_ffn_in['w2_s'], 'L1_ffn_h1_w': _L1_ffn_in['h1_w'], 'L1_ffn_h1_s': _L1_ffn_in['h1_s'], 'L1_ffn_h2_w': _L1_ffn_in['h2_w'], 'L1_ffn_h2_s': _L1_ffn_in['h2_s'], 'L1_ffn_w3_w': _L1_ffn_in['w3_w'], 'L1_ffn_w3_s': _L1_ffn_in['w3_s']}
    _x0 = _d['L0_attn_x']
    _d['L0_attn_x'] = jax.random.normal(jax.random.fold_in(jax.random.key(seed), 1), (32, 256, 128), dtype=_x0.dtype)
    del _x0
    return _d

def reference(L0_attn_x, L0_attn_qkv_w, L0_attn_qkv_b, L0_attn_rq_w, L0_attn_rq_b, L0_attn_rkv_w, L0_attn_rkv_b, L0_attn_rout_w, L0_attn_rout_b, L0_attn_out_w, L0_attn_out_b, L0_attn_gl_w, L0_attn_gr_w, L0_ffn_weight, L0_ffn_ln_gamma, L0_ffn_ln_beta, L1_attn_W_qkv, L1_attn_b_qkv, L1_attn_W_out, L1_attn_b_out, L1_attn_w_sur, L1_attn_b_sur, L1_attn_threshold, L1_ffn_w1_w, L1_ffn_w1_s, L1_ffn_w2_w, L1_ffn_w2_s, L1_ffn_h1_w, L1_ffn_h1_s, L1_ffn_h2_w, L1_ffn_h2_s, L1_ffn_w3_w, L1_ffn_w3_s):

    def _L0_attn_ref(x, qkv_w, qkv_b, rq_w, rq_b, rkv_w, rkv_b, rout_w, rout_b, out_w, out_b, gl_w, gr_w):
        import jax, jax.numpy as jnp
        import numpy as np
        D_MODEL = 128
        N_HEADS = 16
        HEAD_DIM = D_MODEL // N_HEADS
        WINDOW = 128
        LOCAL_BLOCK = 32
        LATENT_TOKENS = 64
        LATENT_D = 32
        LATENT_HEADS = 4
        LATENT_HD = LATENT_D // LATENT_HEADS
        NEG = -1000000000.0

        def _local_attention(q, k, v):
            B, H, S, hd = q.shape
            bs = min(S, max(WINDOW, LOCAL_BLOCK))
            nb = S // bs
            w = WINDOW
            L = bs + w - 1
            k_pad = jnp.pad(k, ((0, 0), (0, 0), (w - 1, 0), (0, 0)))
            v_pad = jnp.pad(v, ((0, 0), (0, 0), (w - 1, 0), (0, 0)))
            starts = jnp.arange(nb) * bs
            idx = starts[:, None] + jnp.arange(L)[None, :]
            kb = k_pad[:, :, idx]
            vb = v_pad[:, :, idx]
            qb = q.reshape(B, H, nb, bs, hd)
            q_pos = starts[:, None] + jnp.arange(bs)[None, :]
            k_gpos = starts[:, None] + jnp.arange(L)[None, :] - (w - 1)
            dist = q_pos[:, :, None] - k_gpos[:, None, :]
            allowed = (dist > 0) & (dist <= w) & (k_gpos[:, None, :] >= 0)
            scale = 1.0 / np.sqrt(hd)
            scores = jnp.einsum('bhnqd,bhnkd->bhnqk', qb, kb) * scale
            scores = jnp.where(allowed, scores, NEG)
            attn = jax.nn.softmax(scores, axis=-1)
            attn = jnp.where(allowed.any(-1)[None, None, :, :, None], attn, 0.0)
            out = jnp.einsum('bhnqk,bhnkd->bhnqd', attn, vb)
            return out.reshape(B, H, S, hd)
        B, S, D = x.shape
        qkv = x @ qkv_w + qkv_b
        q, k, v = jnp.split(qkv, 3, axis=-1)

        def heads(t):
            return t.reshape(B, S, N_HEADS, HEAD_DIM).transpose(0, 2, 1, 3)
        local = _local_attention(heads(q), heads(k), heads(v))
        chunk = -(-S // min(LATENT_TOKENS, S))
        nlat = S // chunk
        pooled = x.reshape(B, nlat, chunk, D).mean(axis=2)
        chunk_ids = jnp.arange(S) // chunk
        rq = (x @ rq_w + rq_b).reshape(B, S, LATENT_HEADS, LATENT_HD).transpose(0, 2, 1, 3)
        rkv = pooled @ rkv_w + rkv_b
        rk, rv = jnp.split(rkv, 2, axis=-1)
        rk = rk.reshape(B, nlat, LATENT_HEADS, LATENT_HD).transpose(0, 2, 1, 3)
        rv = rv.reshape(B, nlat, LATENT_HEADS, LATENT_HD).transpose(0, 2, 1, 3)
        lscale = 1.0 / np.sqrt(LATENT_HD)
        lscores = jnp.einsum('bhsd,bhld->bhsl', rq, rk) * lscale
        lat_allowed = jnp.arange(nlat)[None, :] < chunk_ids[:, None]
        lscores = jnp.where(lat_allowed[None, None], lscores, NEG)
        lattn = jax.nn.softmax(lscores, axis=-1)
        lattn = jnp.where(lat_allowed.any(-1)[None, None, :, None], lattn, 0.0)
        lat_out = jnp.einsum('bhsl,bhld->bhsd', lattn, rv)
        lat_out = lat_out.transpose(0, 2, 1, 3).reshape(B, S, LATENT_D)
        remote = lat_out @ rout_w + rout_b
        remote_h = remote.reshape(B, S, N_HEADS, HEAD_DIM).transpose(0, 2, 1, 3)
        gate = jax.nn.sigmoid(local @ gl_w + remote_h @ gr_w)
        mixed = gate * local + (1.0 - gate) * remote_h
        mixed = mixed.transpose(0, 2, 1, 3).reshape(B, S, D)
        return mixed @ out_w + out_b

    def _L0_ffn_ref(x, weight, ln_gamma, ln_beta):
        import jax, jax.numpy as jnp
        import numpy as np
        LN_EPS = 0.001
        EPS = 1e-05
        QB = 128.0

        def ste_round(x):
            return x + jax.lax.stop_gradient(jnp.round(x) - x)
        mu = jnp.mean(x, axis=-1, keepdims=True)
        var = jnp.var(x, axis=-1, keepdims=True)
        xn = (x - mu) * jax.lax.rsqrt(var + LN_EPS) * ln_gamma + ln_beta
        beta = jnp.mean(jnp.abs(weight))
        w_q = jnp.clip(ste_round(weight / (beta + EPS)), -1.0, 1.0)
        gamma = jnp.max(jnp.abs(xn))
        xq = jnp.clip(xn * QB / gamma, -QB + EPS, QB - EPS)
        y = jnp.einsum('bsd,du->bsu', xq, w_q)
        return y * (gamma * beta / QB)

    def _L1_attn_ref(x, W_qkv, b_qkv, W_out, b_out, w_sur, b_sur, threshold):
        import jax, jax.numpy as jnp
        import numpy as np
        B, T, C, H = (4, 128, 128, 16)
        D = C // H

        def _expmap0_split(u):
            mink = -u[..., :1] ** 2 + jnp.sum(u[..., 1:] ** 2, axis=-1, keepdims=True)
            nomin = jnp.sqrt(jnp.maximum(mink, 1e-08))
            time = jnp.cosh(nomin)
            space = jnp.sinh(nomin) * u[..., 1:] / nomin
            return (time, space)
        Bx, Tx, Cx = x.shape
        importance = jax.nn.sigmoid(jnp.einsum('btc,c->bt', x, w_sur) + b_sur)
        spikes = (importance > threshold).astype(x.dtype)
        spike_mask = spikes[:, None, :, None]
        qkv = x @ W_qkv + b_qkv
        qkv = qkv.reshape(Bx, Tx, 3, H, D).transpose(2, 0, 3, 1, 4)
        q, k, v = (qkv[0], qkv[1], qkv[2])
        tq, sq = _expmap0_split(q)
        tk, sk = _expmap0_split(k)
        neg_inner = jnp.einsum('bhie,bhje->bhij', tq, tk) - jnp.einsum('bhid,bhjd->bhij', sq, sk)
        dist = jnp.arccosh(jnp.maximum(neg_inner, 1.0 + 1e-07))
        scores = -dist ** 2 / np.sqrt(D)
        causal = jnp.tril(jnp.ones((Tx, Tx), dtype=bool))
        scores = jnp.where(causal[None, None], scores, -jnp.inf)
        attn = jax.nn.softmax(scores, axis=-1) * spike_mask
        y = jnp.einsum('bhij,bhjd->bhid', attn, v)
        y = y.transpose(0, 2, 1, 3).reshape(Bx, Tx, Cx)
        return y @ W_out + b_out

    def _L1_ffn_ref(x, w1_w, w1_s, w2_w, w2_s, h1_w, h1_s, h2_w, h2_s, w3_w, w3_s):
        import jax, jax.numpy as jnp
        import numpy as np
        D_IN, D_HID = (128, 512)

        def _ternary(key, shape):
            return jax.random.randint(key, shape, -1, 2).astype(jnp.float32)

        def _tlin(x, w, s):
            return jnp.einsum('bsi,oi->bso', x, w) * s
        h = jax.nn.silu(_tlin(x, w1_w, w1_s)) * _tlin(x, w2_w, w2_s)
        h = jax.nn.gelu(_tlin(h, h1_w, h1_s), approximate=False)
        h = jax.nn.gelu(_tlin(h, h2_w, h2_s), approximate=False)
        return _tlin(h, w3_w, w3_s)
    x = L0_attn_x
    xn = _layernorm(x, axis=-1)
    x = x + _L0_attn_ref(xn, L0_attn_qkv_w, L0_attn_qkv_b, L0_attn_rq_w, L0_attn_rq_b, L0_attn_rkv_w, L0_attn_rkv_b, L0_attn_rout_w, L0_attn_rout_b, L0_attn_out_w, L0_attn_out_b, L0_attn_gl_w, L0_attn_gr_w) + _L0_ffn_ref(xn, L0_ffn_weight, L0_ffn_ln_gamma, L0_ffn_ln_beta)
    xn = _layernorm(x, axis=-1)
    x = x + _L1_attn_ref(xn, L1_attn_W_qkv, L1_attn_b_qkv, L1_attn_W_out, L1_attn_b_out, L1_attn_w_sur, L1_attn_b_sur, L1_attn_threshold) + _L1_ffn_ref(xn, L1_ffn_w1_w, L1_ffn_w1_s, L1_ffn_w2_w, L1_ffn_w2_s, L1_ffn_h1_w, L1_ffn_h1_s, L1_ffn_h2_w, L1_ffn_h2_s, L1_ffn_w3_w, L1_ffn_w3_s)
    return x

_drawn_inputs = setup_inputs


def setup_inputs(seed=0):
    import zlib

    import numpy as np

    out = dict(_drawn_inputs(seed))
    spreads = {'L0_attn_qkv_b': (0.0, 0.1),
     'L0_attn_rq_b': (0.0, 0.1),
     'L0_attn_rkv_b': (0.0, 0.1),
     'L0_attn_rout_b': (0.0, 0.1),
     'L0_attn_out_b': (0.0, 0.1),
     'L0_ffn_ln_gamma': (1.0, 0.2),
     'L0_ffn_ln_beta': (0.0, 0.1),
     'L1_attn_b_qkv': (0.0, 0.1),
     'L1_attn_b_out': (0.0, 0.1)}
    factors = {}
    for name, (base, spread) in spreads.items():
        noise = np.random.default_rng([zlib.crc32(name.encode()), seed]).standard_normal(out[name].shape)
        drawn = base * np.exp(spread * noise) if base else spread * noise
        out[name] = jnp.asarray(drawn.astype(out[name].dtype))
    for name, factor in factors.items():
        out[name] = (out[name] * factor).astype(out[name].dtype)
    return out
```

```python
from contextlib import ExitStack

import numpy as np

import concourse.bass as bass
from concourse import mybir

F32 = mybir.dt.float32
BF16 = mybir.dt.bfloat16
I32 = mybir.dt.int32
ALU = mybir.AluOpType
ACT = mybir.ActivationFunctionType
AX_X = mybir.AxisListType.X

P = 128
NB, T, D = 32, 256, 128
BLK = T // P
H, HD = 16, 8
HP = H // 2
NLAT, LH, LD = 64, 4, 32
POOL = T // NLAT
HID = 512
HC = HID // P
BANK = 512
SLOTS = [(0, 0), (0, 1), (0, 2), (1, 0), (1, 1), (1, 2), (2, 0), (2, 1)]
MLO = 32
NM = H + LH
BIG = 1e30
SCALE = float(1.0 / np.sqrt(HD))
LN_EPS, FFN_LN_EPS, FFN_EPS, QB = 1e-5, 1e-3, 1e-5, 128.0
MIN_COSH = float(np.float32(1.0 + 1e-7))
PRE = 8
PRE_CHUNKS = NB * T // (P * PRE)
SCOLS = H * T + H * P
UNIT = 2 * BANK
UNITS = SCOLS // UNIT


def shape_constants():
    bf = np.dtype("bfloat16")
    q, k = np.arange(P)[:, None], np.arange(P)[None, :]
    c = {}
    c["ident"] = np.eye(P, dtype=np.float32)
    c["ident_bf"] = np.eye(P, dtype=bf)
    own = (k < q)
    first = own | ((q == 0) & (k == 0))
    prev = (k >= q) & (k >= 1)
    neg = lambda ok: np.where(ok, 0.0, -BIG)
    c["win0"] = np.tile(neg(first), (1, 4)).astype(bf)
    c["win1"] = np.tile(np.concatenate([neg(prev), neg(own)], 1), (1, 2)).astype(bf)
    c["cau0"] = np.tile(-neg(k <= q), (1, 4)).astype(bf)
    c["cau1"] = np.tile(np.concatenate([np.zeros((P, P)), -neg(k <= q)], 1), (1, 2)).astype(bf)
    lat = np.arange(NLAT)[None, :]
    blocks = []
    for b in range(BLK):
        chunk = (b * P + q) // POOL
        blocks.append(np.tile(neg((lat < chunk) | ((chunk == 0) & (lat == 0))), (1, LH)))
    c["winl"] = np.concatenate(blocks, 1).astype(bf)
    ok = (np.arange(P)[:, None] % NLAT) < np.arange(T)[None, :] // POOL
    c["winl_t"] = np.tile(neg(ok), (1, LH // 2)).astype(bf)
    sel = np.zeros((P, H + LH // 2, P), np.float32)
    for h in range(H):
        sel[h, h, :] = 1
        sel[MLO + h, h, :] = 1
    for p in range(LH // 2):
        for e in range(2):
            sel[H + 2 * p + e, H + p, e * NLAT:(e + 1) * NLAT] = 1
            sel[MLO + H + 2 * p + e, H + p, e * NLAT:(e + 1) * NLAT] = 1
    c["sel"] = sel.astype(bf)
    rows = np.arange(P)[:, None, None] // NLAT
    heads = 2 * np.arange(LH // 2)[None, :, None] + rows
    c["lat_cols"] = (heads == (np.arange(LD) // (LD // LH))[None, None, :]).astype(np.float32)
    ones = np.zeros((P, LH // 2, 2 * LD), np.float32)
    ones[:, :, LD:LD + LH] = heads == np.arange(LH)[None, None, :]
    c["lat_ones"] = ones
    c["lat_rows"] = (np.arange(LD)[:, None] // (LD // LH) == np.arange(LH)[None, :]).astype(np.float32)
    return c


class Signal:

    def __init__(self, sem, per=1, step=1, start=0):
        self.sem, self.per, self.step, self.start = sem, per, step, start

    def at(self, i, n=None):
        n = self.per if n is None else n
        return i * (self.per * self.step) + (n * self.step + self.start)


def bc(ap, shape):
    return ap.to_broadcast(list(shape))


def build(nc, A, out):
    ctx = ExitStack()
    with ctx:
        def sb(name, shape, dt=F32):
            return ctx.enter_context(nc.sbuf_tensor(name, list(shape), dt))

        def sem(name):
            return ctx.enter_context(nc.semaphore(name))

        ahead = []

        def sig(name, per=1, step=1, start=0):
            s = Signal(sem(name), per, step, start)
            if start:
                ahead.append(s)
            return s

        ident, ident_bf = sb("ident", [P, P]), sb("ident_bf", [P, P], BF16)
        win0, win1 = sb("win0", [P, BANK], BF16), sb("win1", [P, BANK], BF16)
        cau0, cau1 = sb("cau0", [P, BANK], BF16), sb("cau1", [P, BANK], BF16)
        winl, winl_t = sb("winl", [P, BANK], BF16), sb("winl_t", [P, BANK], BF16)
        sel = sb("sel", [P, H + LH // 2, P], BF16)
        lat_cols, lat_rows = sb("lat_cols", [P, LH // 2, LD]), sb("lat_rows", [LD, LH])
        w_qkv0, b_qk0, b_v0 = sb("w_qkv0", [P, 3 * D]), sb("b_qk0", [P, 2]), sb("b_v0", [P, D])
        w_rq, b_rq = sb("w_rq", [P, LD]), sb("b_rq", [LD, 1])
        w_rkv, b_rk, b_rv = sb("w_rkv", [P, 2 * LD]), sb("b_rk", [LD, 1]), sb("b_rv", [P, LD])
        w_rout, b_rout = sb("w_rout", [LD, D]), sb("b_rout", [P, D])
        w_out0, b_out0 = sb("w_out0", [P, D]), sb("b_out0", [P, D])
        gate_l, gate_r = sb("gate_l", [P, HD]), sb("gate_r", [P, HD])
        w_tern, w_qs = sb("w_tern", [P, D]), sb("w_qs", [P, D])
        gam_row, bet_row = sb("gam_row", [P, D]), sb("bet_row", [P, D])
        gam_col, bet_col = sb("gam_col", [P, 1]), sb("bet_col", [P, 1])
        w_qkv1, b_qk1, b_v1 = sb("w_qkv1", [P, 3 * D]), sb("b_qk1", [P, 2 * D]), sb("b_v1", [P, D])
        w_out1, b_out1 = sb("w_out1", [P, D]), sb("b_out1", [P, D])
        w_sur, b_sur, thresh = sb("w_sur", [P, D]), sb("b_sur", [P, 1]), sb("thresh", [P, 1])
        w1t, w2t = sb("w1t", [P, HID]), sb("w2t", [P, HID])
        h1t, h2t = sb("h1t", [P, HC, HID]), sb("h2t", [P, HC, HID])
        s1, s2, g1, g2 = (sb(n, [P, HC]) for n in ("s1", "s2", "g1", "g2"))
        w3t, s3 = sb("w3t", [P, HC, D]), sb("s3", [P, D])
        mhalf = sb("mhalf", [P, 2 * PRE])
        minus1 = sb("minus1", [P, 1])
        ksign = sb("ksign", [P, BLK * 2 * H])

        zc, zs = sb("zc", [P, SCOLS]), sb("zs", [P, SCOLS])
        px = zc[:, 0:2 * PRE * D].rearrange("p (b n d) -> p b n d", b=2, d=D)
        pn = zs[:, 0:PRE * D].rearrange("p (n d) -> p n d", d=D)
        pf = zs[:, PRE * D:2 * PRE * D].rearrange("p (n d) -> p n d", d=D)
        pst, pmv = sb("pst", [P, PRE, 6]), sb("pmv", [P, PRE, 2])
        pve, prs = sb("pve", [P, PRE]), sb("prs", [P, PRE])
        pmax = sb("pmax", [P, PRE_CHUNKS])
        gcol, gall = sb("gcol", [P, 1]), sb("gall", [P, 1])
        thr, nthr = sb("thr", [P, 1]), sb("nthr", [P, 1])
        wcol, wall = sb("wcol", [P, 1]), sb("wall", [P, 1])
        beta, rbeta = sb("beta", [P, 1]), sb("rbeta", [P, 1])
        wn, wr = sb("wn", [P, D]), sb("wr", [P, D])

        x = sb("x", [P, BLK, D])
        xres = sb("xres", [P, BLK, D])
        st, mv = sb("st", [P, BLK, 6]), sb("mv", [P, BLK, 2])
        ve, rs = sb("ve", [P, BLK]), sb("rs", [P, BLK])
        ve2, rs2 = sb("ve2", [P, BLK]), sb("rs2", [P, BLK])
        xn, xf = sb("xn", [P, BLK, D]), sb("xf", [P, BLK, D])
        xn_t, xq_t = sb("xn_t", [P, T]), sb("xq_t", [P, T])
        pooled = sb("pooled", [P, 2, NLAT])
        qk_t = sb("qk_t", [P, 2 * T])
        resid = sb("resid", [P, 2 * T])
        parts = sb("parts", [P, 3, 2 * T], BF16)
        q_st = sb("q_st", [P, HP, 2, T], BF16)
        k_st = sb("k_st", [P, HP, T], BF16)
        v_st = sb("v_st", [P, BLK, H, 32])
        rq_t, rk_t, rk_m = sb("rq_t", [LD, T]), sb("rk_t", [LD, NLAT]), sb("rk_m", [LD, LH, NLAT])
        rv, rv_st = sb("rv", [P, LD]), sb("rv_st", [P, LH // 2, 2 * LD])
        nmax, nmax2 = sb("nmax", [P, BLK, NM]), sb("nmax2", [P, BLK, P], BF16)
        m_t = sb("m_t", [P, T], BF16)
        prob = sb("prob", [P, SCOLS])
        prob_l = sb("prob_l", [P, LH // 2, T])
        o_t = sb("o_t", [P, 4, T])
        lo_t = sb("lo_t", [2 * LD, T])
        rsum, rrec = sb("rsum", [P, BLK * H]), sb("rrec", [P, BLK * H])
        lsum, lrec = sb("lsum", [P, BLK, LH]), sb("lrec", [P, BLK, LH])
        local, lat = sb("local", [P, BLK, D]), sb("lat", [P, BLK, LD])
        lat_t = sb("lat_t", [LD, T])
        remote = sb("remote", [P, BLK, D])
        gl, gr = sb("gl", [P, BLK, D]), sb("gr", [P, BLK, D])
        glog, gexp, gate = (sb(n, [P, BLK * H]) for n in ("glog", "gexp", "gate"))
        mixed, mix_t = sb("mixed", [P, BLK, D]), sb("mix_t", [P, T])
        x1 = sb("x1", [P, BLK, D])

        st1, mv1 = sb("st1", [P, BLK, 6]), sb("mv1", [P, BLK, 2])
        ve1, rs1 = sb("ve1", [P, BLK]), sb("rs1", [P, BLK])
        x1res = sb("x1res", [P, BLK, D])
        xn1, xs1 = sb("xn1", [P, BLK, D]), sb("xs1", [P, BLK, D])
        imp, eimp, spike = sb("imp", [P, BLK]), sb("eimp", [P, BLK]), sb("spike", [P, BLK])
        xn1_t = sb("xn1_t", [P, T])
        u_qk, u_sq = sb("u_qk", [P, BLK, 2 * D]), sb("u_sq", [P, BLK, 2 * D])
        NV = BLK * 2 * H
        mink, lnw, nom, rnom, epos, eneg = (sb(n, [P, NV]) for n in ("mink", "lnw", "nom", "rnom", "epos", "eneg"))
        ctime, sfac, wsmall, poly, small = (sb(n, [P, NV]) for n in ("ctime", "sfac", "wsmall", "poly", "small"))
        emb = sb("emb", [P, BLK, 2 * D])
        zmin, zsq, zsr, zd = (sb(n, [P, BLK * H]) for n in ("zmin", "zsq", "zsr", "zd"))
        y1, y_t = sb("y1", [P, BLK, D]), sb("y_t", [P, T])
        sil = sb("sil", [P, T])
        hid1, hid2, hid3 = (sb(n, [P, HC, T]) for n in ("hid1", "hid2", "hid3"))
        xout = sb("xout", [P, BLK, D])

        scr = nc.dram_tensor("scr", [2, 3, P, 2 * T], BF16, kind="Internal").ap()

        pu = ctx.enter_context(nc.psum_tensor("pu", [P, 2, UNIT], F32))
        pav = ctx.enter_context(nc.psum_tensor("pav", [P, 2 * BANK], F32))
        pm = ctx.enter_context(nc.psum_tensor("pm", [P, 2, BANK], F32))
        UNIT_USES = [(n, u) for n in ("max0", "exp0", "min1", "cosh1", "sub1") for u in range(UNITS)]
        MISC_USES = ["xT", "qk", "v", "rqkv", "lmax", "mT", "lexp", "lo", "loT", "latT", "rem", "mixT", "y0",
                     "x1T", "qkv1a", "qkv1b", "embT", "mT1", "yT", "f1_0", "f1_1", "f1_2", "f1_3",
                     "f2_0", "f2_1", "f3_0", "f3_1", "y1"]
        AV_USES = ["av0", "avT0", "av1", "avT1"]
        assert len(UNIT_USES) % 2 == 0 and len(MISC_USES) % 2 == 0
        unit_full = [sig(f"unit_full{k}", len(UNIT_USES) // 2) for k in range(2)]
        unit_free = [sig(f"unit_free{k}", len(UNIT_USES) // 2, start=1) for k in range(2)]
        misc_full = [sig(f"misc_full{k}", len(MISC_USES) // 2) for k in range(2)]
        misc_free = [sig(f"misc_free{k}", len(MISC_USES) // 2, start=1) for k in range(2)]
        av_full, av_free = sig("av_full", len(AV_USES)), sig("av_free", len(AV_USES), start=1)

        class Use:

            def __init__(self, ap, full, free, n):
                self.ap, self.full_sig, self.free_sig, self.n = ap, full, free, n
                self.full, self.free = full.sem, free.sem

            def wait_free(self, pe, i):
                pe.wait_ge(self.free, self.free_sig.at(i, self.n))

            def wait_full(self, eng, i):
                eng.wait_ge(self.full, self.full_sig.at(i, self.n + 1))

            def wait_drained(self, eng, i):
                eng.wait_ge(self.free, self.free_sig.at(i, self.n + 1))

        def unit(name, u):
            n = UNIT_USES.index((name, u))
            return Use(pu[:, n % 2, :], unit_full[n % 2], unit_free[n % 2], n // 2)

        def misc(name):
            n = MISC_USES.index(name)
            return Use(pm[:, n % 2, :], misc_full[n % 2], misc_free[n % 2], n // 2)

        def avuse(name):
            return Use(pav[:, :], av_full, av_free, AV_USES.index(name))

        loads = []
        consts_in, passed = sem("consts_in"), sem("passed")
        zeros_set = sem("zeros_set")
        pre_in, pre_used = [sem("pre_in0"), sem("pre_in1")], sem("pre_used")
        pre_var, pre_rstd = sem("pre_var"), sem("pre_rstd")
        cols_ready, all_ready = sem("cols_ready"), sem("all_ready")
        weights_ready = sem("weights_ready")
        pre_link = sem("pre_link")

        x_in = sig("x_in", 1, 16)
        var0, rstd0, var0b, rstd0b = sig("var0"), sig("rstd0"), sig("var0b"), sig("rstd0b")
        xn_ready, xres_ready, xf_ready = sig("xn_ready", start=1), sig("xres_ready", start=1), sig("xf_ready")
        xnT_ready, xq_ready = sig("xnT_ready"), sig("xq_ready")
        pooled_ready = sig("pooled_ready")
        qkT_ready = [sig("qkT_ready0"), sig("qkT_ready1")]
        hi_ready = [sig("hi_ready0"), sig("hi_ready1")]
        parts_ready = [sig("parts_ready0"), sig("parts_ready1")]
        scr_written = [sig("scr_written0", 1, 16), sig("scr_written1", 1, 16)]
        NST = 3 * len(SLOTS)
        stacked = [sig("stacked0", NST, 16), sig("stacked1", NST, 16)]
        v_ready = [sig("v_ready0"), sig("v_ready1")]
        rq_ready, rk_ready, rv_ready = sig("rq_ready"), sig("rk_ready"), sig("rv_ready")
        nmax_ready = [sig("nmax_ready0"), sig("nmax_ready1")]
        mT_ready = [sig("mT_ready0"), sig("mT_ready1")]
        masked0 = sig("masked0", UNITS + 1)
        o_ready = [sig("o_ready0"), sig("o_ready1")]
        lo_ready, lat_ready, latT_ready = sig("lo_ready"), sig("lat_ready"), sig("latT_ready")
        local_ready, remote_ready = sig("local_ready"), sig("remote_ready")
        gsum_ready, glog_ready, gexp_ready, gate_ready = (sig(n) for n in ("gsum_ready", "glog_ready", "gexp_ready", "gate_ready"))
        mixed_ready, mixT_ready, x1_ready = sig("mixed_ready"), sig("mixT_ready"), sig("x1_ready")

        var1, rstd1, xn1_ready, x1res_ready = (sig(n) for n in ("var1", "rstd1", "xn1_ready", "x1res_ready"))
        imp_ready, eimp_ready, xn1T_ready = sig("imp_ready"), sig("eimp_ready"), sig("xn1T_ready")
        u_ready, usq_ready, mink_ready, exps_ready = (sig(n) for n in ("u_ready", "usq_ready", "mink_ready", "exps_ready"))
        emb_ready = sig("emb_ready")
        zmin_ready, zsq_ready, zsr_ready, zsum_ready, zln_ready = (sig(n) for n in ("zmin_ready", "zsq_ready", "zsr_ready", "zsum_ready", "zln_ready"))
        cosh_in, sqrt_done, sum_done, ln_done, sq_done, sub_done, exp1_done = (
            sig(n, UNITS) for n in ("cosh_in", "sqrt_done", "sum_done", "ln_done", "sq_done", "sub_done", "exp1_done"))
        masked1 = sig("masked1", UNITS)
        y_ready, yT_ready = sig("y_ready"), sig("yT_ready")
        sil_ready, hid1_ready = sig("sil_ready", HC), sig("hid1_ready", HC)
        hid2_ready, hid3_ready = sig("hid2_ready"), sig("hid3_ready")
        out_done = sig("out_done", 1, 16, start=1)
        DVE_LINKS, ACT_LINKS, POOL_LINKS = 44, 9, 3
        dve_link, act_link, pool_link = sig("dve_link", DVE_LINKS), sig("act_link", ACT_LINKS), sig("pool_link", POOL_LINKS)

        class Links:

            def __init__(self, eng, counter, i):
                self.eng, self.counter, self.i, self.n = eng, counter, i, 0

            def __call__(self, ins, after=None):
                self.n += 1
                ins.then_inc(self.counter.sem, 1)
                self.eng.wait_ge(self.counter.sem, self.counter.at(self.i, self.n))
                if after:
                    after(self.eng)

            def end(self):
                assert self.n == self.counter.per, (self.counter.sem, self.n)

        def apart(eng):
            eng.sem_inc(passed, 1)

        block = ctx.enter_context(nc.Block())

        def row(ap, n=P):
            return ap.rearrange("(o n) -> o n", o=1).to_broadcast([n, ap.shape[0]])

        def col(ap):
            return ap.rearrange("(p o) -> p o", o=1)

        for name, dst in (("ident", ident), ("ident_bf", ident_bf), ("win0", win0), ("win1", win1), ("cau0", cau0),
                          ("cau1", cau1), ("winl", winl), ("winl_t", winl_t), ("sel", sel), ("lat_cols", lat_cols), ("lat_rows", lat_rows),
                          ("lat_ones", rv_st)):
            loads.append((dst[:], A[name]))
        loads += [
            (w_qkv0[:], A["L0_attn_qkv_w"]), (b_qk0[:], A["b_qk0_cols"]),
            (b_v0[:], row(A["L0_attn_qkv_b"][2 * D:3 * D])), (w_rq[:], A["L0_attn_rq_w"]), (b_rq[:], col(A["L0_attn_rq_b"])),
            (w_rkv[:], A["L0_attn_rkv_w"]), (b_rk[:], col(A["L0_attn_rkv_b"][0:LD])), (b_rv[:], row(A["L0_attn_rkv_b"][LD:2 * LD])),
            (w_rout[:], A["L0_attn_rout_w"]), (b_rout[:], row(A["L0_attn_rout_b"])), (w_out0[:], A["L0_attn_out_w"]),
            (b_out0[:], row(A["L0_attn_out_b"])), (gate_l[:], row(A["L0_attn_gl_w"].rearrange("a o -> (a o)"))),
            (gate_r[:], row(A["L0_attn_gr_w"].rearrange("a o -> (a o)"))), (w_tern[:], A["L0_ffn_weight"]),
            (gam_row[:], row(A["L0_ffn_ln_gamma"])), (bet_row[:], row(A["L0_ffn_ln_beta"])),
            (gam_col[:], col(A["L0_ffn_ln_gamma"])), (bet_col[:], col(A["L0_ffn_ln_beta"])),
            (w_qkv1[:], A["L1_attn_W_qkv"]), (b_qk1[:], row(A["L1_attn_b_qkv"][0:2 * D])), (b_v1[:], row(A["L1_attn_b_qkv"][2 * D:3 * D])),
            (w_out1[:], A["L1_attn_W_out"]), (b_out1[:], row(A["L1_attn_b_out"])), (w_sur[:], row(A["L1_attn_w_sur"])),
            (b_sur[:], row(A["L1_attn_b_sur"])), (thresh[:], row(A["L1_attn_threshold"])),
            (w1t[:], A["w1t"]), (w2t[:], A["w2t"]), (h1t[:], A["h1t"].rearrange("(c p) n -> p c n", p=P)),
            (h2t[:], A["h2t"].rearrange("(c p) n -> p c n", p=P)), (w3t[:], A["w3t"].rearrange("(c p) n -> p c n", p=P)),
            (s3[:], row(A["L1_ffn_w3_s"])),
        ]
        for dst, name in ((s1, "L1_ffn_w1_s"), (s2, "L1_ffn_w2_s"), (g1, "L1_ffn_h1_s"), (g2, "L1_ffn_h2_s")):
            loads.append((dst[:], A[name + "_cols"]))

        x_seq = A["L0_attn_x"].rearrange("b (k p) d -> b p k d", p=P)
        out_seq = out.rearrange("b (k p) d -> b p k d", p=P)
        x_chunk = A["L0_attn_x"].rearrange("b t d -> (b t) d").rearrange("(c n p) d -> c p n d", p=P, n=PRE)

        @block.sync
        def _(sp):
            for s in ahead:
                sp.sem_inc(s.sem, s.start)
            for dst, src in loads:
                sp.dma_start(dst, src).then_inc(consts_in, 16)
            with sp.Fori(0, PRE_CHUNKS // 2) as c:
                for k in range(2):
                    sp.wait_ge(pre_used, c * 2 + k + 1)
                    sp.dma_start(px[:, k], x_chunk[bass.ds(c * 2 + k, 1)].rearrange("o p n d -> p (o n) d")).then_inc(pre_in[k], 16)

            def load_x(i):
                sp.wait_ge(xn_ready.sem, xn_ready.at(i, 0))
                sp.wait_ge(xres_ready.sem, xres_ready.at(i, 0))
                sp.dma_start(x[:], x_seq[bass.ds(i, 1)].rearrange("o p k d -> p (o k) d")).then_inc(x_in.sem, 16)

            def stack(layer, i):
                sp.wait_ge(parts_ready[layer].sem, parts_ready[layer].at(i))
                sp.dma_start(scr[layer].rearrange("a p t -> p a t"), parts[:]).then_inc(scr_written[layer].sem, 16)
                sp.wait_ge(scr_written[layer].sem, scr_written[layer].at(i))
                for s, (a, b) in enumerate(SLOTS):
                    for e in range(2):
                        r = 2 * HD * s + HD * e
                        sp.dma_start(q_st[r:r + HD, :, e, :],
                                     scr[layer, a].rearrange("(p e d) t -> e d p t", e=2, d=HD)[e, :, :, 0:T]).then_inc(stacked[layer].sem, 16)
                    sp.dma_start(k_st[2 * HD * s:2 * HD * (s + 1), :, :],
                                 scr[layer, b].rearrange("(p r) t -> r p t", r=2 * HD)[:, :, T:2 * T]).then_inc(stacked[layer].sem, 16)

            def sequence(i, last):
                stack(0, i)
                if not last:
                    load_x(i + 1)
                stack(1, i)
                misc("y1").wait_drained(sp, i)
                sp.dma_start(out_seq[bass.ds(i, 1)].rearrange("o p k d -> p (o k) d"), xout[:]).then_inc(out_done.sem, 16)

            sp.wait_ge(zeros_set, 2)
            load_x(0)
            with sp.Fori(0, NB - 1) as i:
                sequence(i, False)
            sequence(NB - 1, True)
            sp.wait_ge(out_done.sem, out_done.at(NB - 1))

        @block.vector
        def _(dve):
            V = nc.vector
            n_pre = [0]

            def pre(ins):
                n_pre[0] += 1
                ins.then_inc(pre_link, 1)
                dve.wait_ge(pre_link, n_pre[0])

            dve.sem_inc(pre_used, 2)
            V.memset(mhalf[:], -0.5)
            V.memset(minus1[:], -1.0)
            V.memset(ksign[:].rearrange("p (k s h) -> p k s h", k=BLK, s=2)[:, :, 0, :], 1.0)
            V.memset(ksign[:].rearrange("p (k s h) -> p k s h", k=BLK, s=2)[:, :, 1, :], -1.0)
            V.memset(q_st[:].bitcast(I32) if False else q_st[:], 0.0)
            V.memset(nmax2[:], 0.0)
            V.memset(v_st[:], 0.0).then_inc(zeros_set, 1)
            dve.wait_ge(zeros_set, 1)
            V.memset(v_st[:, :, :, HD:HD + 1], 1.0).then_inc(zeros_set, 1)
            dve.wait_ge(consts_in, 16 * len(loads))
            V.tensor_reduce(out=wcol[:], in_=w_tern[:], axis=AX_X, op=ALU.add, apply_absolute_value=True).then_inc(cols_ready, 1)
            V.tensor_tensor(w3t[:], w3t[:], bc(s3[:].unsqueeze(1), [P, HC, D]), ALU.mult)

            PRE_LINKS = 16
            with dve.Fori(0, PRE_CHUNKS // 2) as c:
                links = 0

                def link(ins, after=None):
                    nonlocal links
                    links += 1
                    ins.then_inc(pre_link, 1)
                    dve.wait_ge(pre_link, c * PRE_LINKS + links)
                    if after:
                        after(dve)

                for k in range(2):
                    dve.wait_ge(pre_in[k], c * 16 + 16)

                    def norm(dst, src, eps, step):
                        for n in range(PRE):
                            last = V.bn_stats(pst[:, n, :], src[:, n, :])
                        link(last, apart)
                        for n in range(PRE):
                            last = V.bn_aggr(pmv[:, n, :], pst[:, n, :])
                        link(last)
                        V.tensor_scalar(pve[:], pmv[:, :, 1], eps, None, ALU.add).then_inc(pre_var, 1)
                        dve.wait_ge(pre_rstd, c * 4 + 2 * k + step)
                        for n in range(PRE):
                            last = V.tensor_scalar(dst[:, n, :], src[:, n, :], pmv[:, n, 0:1], prs[:, n:n + 1], ALU.subtract, ALU.mult)
                        return last

                    ins = norm(pn, px[:, k], LN_EPS, 1)
                    ins.then_inc(pre_used, 1)
                    dve.wait_ge(pre_used, c * 2 + k + 3)
                    link(norm(pf, pn, FFN_LN_EPS, 2))
                    link(V.tensor_tensor(pf, pf, bc(gam_row[:].unsqueeze(1), [P, PRE, D]), ALU.mult))
                    link(V.tensor_tensor(pf, pf, bc(bet_row[:].unsqueeze(1), [P, PRE, D]), ALU.add))
                    link(V.tensor_reduce(out=pmax[:, bass.ds(c * 2 + k, 1)], in_=pf.rearrange("p n d -> p (n d)"), axis=AX_X, op=ALU.max,
                                         apply_absolute_value=True))
                assert links == PRE_LINKS, links
            n_pre[0] = PRE_LINKS * (PRE_CHUNKS // 2)
            V.tensor_reduce(out=gcol[:], in_=pmax[:], axis=AX_X, op=ALU.max).then_inc(cols_ready, 1)
            dve.wait_ge(all_ready, 2)
            lim = float(np.float32(QB - FFN_EPS)) / QB
            V.tensor_scalar(thr[:], gall[:], lim, None, ALU.mult)
            V.tensor_scalar(nthr[:], gall[:], -lim, None, ALU.mult)
            pre(V.tensor_scalar(beta[:], wall[:], 1.0 / (D * D), None, ALU.mult))
            pre(V.tensor_scalar(rbeta[:], beta[:], FFN_EPS, None, ALU.add))
            pre(V.reciprocal(rbeta[:], rbeta[:]))
            pre(V.tensor_scalar(wn[:], w_tern[:], rbeta[:], None, ALU.mult))
            pre(V.tensor_scalar(wr[:], wn[:], 4.0, -4.0, ALU.min, ALU.max))
            magic = 1.5 * 2.0 ** 23
            pre(V.tensor_scalar(wr[:], wr[:], magic, None, ALU.add))
            pre(V.tensor_scalar(wr[:], wr[:], -magic, None, ALU.add))
            pre(V.tensor_scalar(wr[:], wr[:], 1.0, -1.0, ALU.min, ALU.max))
            V.tensor_scalar(w_qs[:], wr[:], beta[:], None, ALU.mult).then_inc(weights_ready, 1)

            def moments(dst_st, dst_mv, dst_ve, src, eps, ready, link):
                for k in range(BLK):
                    last = V.bn_stats(dst_st[:, k, :], src[:, k, :])
                link(last, apart)
                for k in range(BLK):
                    last = V.bn_aggr(dst_mv[:, k, :], dst_st[:, k, :])
                link(last)
                V.tensor_scalar(dst_ve[:], dst_mv[:, :, 1], eps, None, ALU.add).then_inc(ready.sem, 1)

            def normed(dst, src, mvs, rstd, ready, i):
                dve.wait_ge(ready.sem, ready.at(i))
                for k in range(BLK):
                    last = V.tensor_scalar(dst[:, k, :], src[:, k, :], mvs[:, k, 0:1], rstd[:, k:k + 1], ALU.subtract, ALU.mult)
                return last

            def split(layer, i, link):
                dve.wait_ge(hi_ready[layer].sem, hi_ready[layer].at(i))
                link(V.tensor_tensor(resid[:], qk_t[:], parts[:, 0, :], ALU.subtract))
                link(V.tensor_copy(parts[:, 1, :], resid[:]))
                V.tensor_tensor(parts[:, 2, :], resid[:], parts[:, 1, :], ALU.subtract).then_inc(parts_ready[layer].sem, 1)

            def values(dst_use, psum4, bias, ready):
                V.tensor_tensor(v_st[:, :, :, 0:HD], psum4, bc(bias[:].rearrange("p (h d) -> p h d", d=HD).unsqueeze(1), [P, BLK, H, HD]), ALU.add)

            def maxima_low(n, layer, link):
                link(V.tensor_copy(nmax2[:, :, 0:n], nmax[:, :, 0:n]))
                V.tensor_tensor(nmax2[:, :, MLO:MLO + n], nmax[:, :, 0:n], nmax2[:, :, 0:n], ALU.subtract).then_inc(nmax_ready[layer].sem, 1)

            def head_norm(use, dst, i, link, extra=None):
                use.wait_full(dve, i)
                t = use.ap.rearrange("p (n c) -> p n c", c=32)
                link(V.tensor_scalar(rsum[:].unsqueeze(2), t[:, :, HD:HD + 1], 0.5, None, ALU.max))
                link(V.reciprocal(rrec[:], rsum[:]))
                if extra is not None:
                    r3 = rrec[:].rearrange("p (k h) -> p k h", k=BLK)
                    link(V.tensor_tensor(r3, r3, bc(extra[:].unsqueeze(2), [P, BLK, H]), ALU.mult))
                return V.tensor_tensor(dst[:].rearrange("p k (h d) -> p (k h) d", d=HD), t[:, :, 0:HD],
                                       bc(rrec[:].unsqueeze(2), [P, BLK * H, HD]), ALU.mult)

            def layer0(i, link):
                dve.wait_ge(x_in.sem, x_in.at(i))
                moments(st, mv, ve, x, LN_EPS, var0, link)
                normed(xn, x, mv, rs, rstd0, i).then_inc(xn_ready.sem, 1)
                dve.wait_ge(xn_ready.sem, xn_ready.at(i))
                moments(st, mv, ve2, xn, FFN_LN_EPS, var0b, link)
                normed(xf, xn, mv, rs2, rstd0b, i).then_inc(xf_ready.sem, 1)
                misc("xT").wait_drained(dve, i)
                V.tensor_scalar(xq_t[:], xq_t[:], thr[:], nthr[:], ALU.min, ALU.max).then_inc(xq_ready.sem, 1)
                link(V.tensor_reduce(out=pooled[:, 0, :], in_=xn_t[:].rearrange("p (l c) -> p l c", c=POOL), axis=AX_X, op=ALU.add))
                V.tensor_copy(pooled[:, 1, :], pooled[:, 0, :]).then_inc(pooled_ready.sem, 1)
                u = misc("v")
                u.wait_full(dve, i)
                V.tensor_tensor(v_st[:, :, :, 0:HD], u.ap[:, 0:T].rearrange("p (k h d) -> p k h d", k=BLK, d=HD),
                                bc(b_v0[:].rearrange("p (h d) -> p h d", d=HD).unsqueeze(1), [P, BLK, H, HD]), ALU.add).then_inc(u.free, 1)
                split(0, i, link)
                u = misc("rqkv")
                u.wait_full(dve, i)
                V.tensor_scalar(rq_t[:], u.ap[0:LD, 0:T], b_rq[:], None, ALU.add).then_inc(rq_ready.sem, 1)
                V.tensor_scalar(rk_t[:], u.ap[0:LD, T:T + NLAT], 1.0 / POOL, b_rk[:], ALU.mult, ALU.add)
                last = V.scalar_tensor_tensor(rv[:], u.ap[:, T + NLAT:T + NLAT + LD], 1.0 / POOL, b_rv[:], ALU.mult, ALU.add)
                last.then_inc(u.free, 1)
                u.wait_drained(dve, i)
                V.tensor_tensor(rk_m[:], bc(rk_t[:].unsqueeze(1), [LD, LH, NLAT]), bc(lat_rows[:].unsqueeze(2), [LD, LH, NLAT]), ALU.mult).then_inc(rk_ready.sem, 1)
                V.tensor_tensor(rv_st[:, :, 0:LD], bc(rv[:].unsqueeze(1), [P, LH // 2, LD]), lat_cols[:], ALU.mult).then_inc(rv_ready.sem, 1)
                for n in range(UNITS):
                    u = unit("max0", n)
                    u.wait_full(dve, i)
                    if n < 2:
                        V.tensor_reduce(out=nmax[:, 0, 8 * n:8 * n + 8], in_=u.ap.rearrange("p (h k) -> p h k", k=P), axis=AX_X, op=ALU.max,
                                        negate=True).then_inc(u.free, 1)
                    else:
                        V.tensor_reduce(out=nmax[:, 1, 4 * n - 8:4 * n - 4], in_=u.ap.rearrange("p (h k) -> p h k", k=T), axis=AX_X, op=ALU.max,
                                        negate=True).then_inc(u.free, 1)
                u = misc("lmax")
                u.wait_full(dve, i)
                link(V.tensor_reduce(out=nmax[:, :, H:NM], in_=u.ap.rearrange("p (k h l) -> p k h l", k=BLK, l=NLAT), axis=AX_X, op=ALU.max, negate=True))
                V.tensor_copy(nmax2[:, :, 0:NM], nmax[:]).then_inc(u.free, 1)
                u.wait_drained(dve, i)
                V.tensor_tensor(nmax2[:, :, MLO:MLO + NM], nmax[:], nmax2[:, :, 0:NM], ALU.subtract).then_inc(nmax_ready[0].sem, 1)
                u = misc("lo")
                u.wait_full(dve, i)
                V.tensor_copy(lo_t[:], u.ap[0:2 * LD, 0:T]).then_inc(u.free, 1)
                u = misc("loT")
                u.wait_full(dve, i)
                t = u.ap[:, 0:2 * 2 * LD].rearrange("p (k c) -> p k c", k=BLK)
                link(V.tensor_scalar(lsum[:], t[:, :, LD:LD + LH], 0.5, None, ALU.max))
                link(V.reciprocal(lrec[:], lsum[:]))
                last = V.tensor_tensor(lat[:].rearrange("p k (h d) -> p k h d", h=LH), t[:, :, 0:LD].rearrange("p k (h d) -> p k h d", h=LH),
                                       bc(lrec[:].unsqueeze(3), [P, BLK, LH, LD // LH]), ALU.mult)
                last.then_inc(u.free, 1)
                u = misc("rem")
                u.wait_full(dve, i)
                V.tensor_tensor(remote[:], u.ap[:, 0:T].rearrange("p (k d) -> p k d", k=BLK), bc(b_rout[:].unsqueeze(1), [P, BLK, D]), ALU.add).then_inc(u.free, 1)
                u = avuse("avT0")
                head_norm(u, local, i, link).then_inc(u.free, 1)
                dve.wait_ge(gsum_ready.sem, gsum_ready.at(i))
                V.tensor_reduce(out=glog[:], in_=gl[:].rearrange("p k (h d) -> p (k h) d", d=HD), axis=AX_X, op=ALU.add).then_inc(glog_ready.sem, 1)
                dve.wait_ge(gexp_ready.sem, gexp_ready.at(i))
                link(V.tensor_scalar(gexp[:], gexp[:], 1.0, None, ALU.add))
                V.reciprocal(gate[:], gexp[:]).then_inc(gate_ready.sem, 1)
                u = misc("y0")
                u.wait_full(dve, i)
                V.tensor_tensor(x1[:], u.ap[:, 0:T].rearrange("p (k d) -> p k d", k=BLK), xres[:], ALU.add).then_inc(u.free, 1)
                u.wait_drained(dve, i)

            def layer1(i, link):
                moments(st1, mv1, ve1, x1, LN_EPS, var1, link)
                normed(xn1, x1, mv1, rs1, rstd1, i).then_inc(xn1_ready.sem, 1)
                V.tensor_tensor(x1res[:], x1[:], bc(b_out1[:].unsqueeze(1), [P, BLK, D]), ALU.add)
                dve.wait_ge(xn1_ready.sem, xn1_ready.at(i))
                link(V.tensor_tensor(xs1[:], xn1[:], bc(w_sur[:].unsqueeze(1), [P, BLK, D]), ALU.mult))
                link(V.tensor_reduce(out=imp[:], in_=xs1[:], axis=AX_X, op=ALU.add))
                V.tensor_scalar(imp[:], imp[:], b_sur[:], None, ALU.add).then_inc(imp_ready.sem, 1)
                for k, name in enumerate(("qkv1a", "qkv1b")):
                    u = misc(name)
                    u.wait_full(dve, i)
                    V.tensor_tensor(v_st[:, k, :, 0:HD], u.ap[:, 2 * D:3 * D].rearrange("p (h d) -> p h d", d=HD),
                                    b_v1[:].rearrange("p (h d) -> p h d", d=HD), ALU.add)
                    V.tensor_tensor(u_qk[:, k, :], u.ap[:, 0:2 * D], b_qk1[:], ALU.add).then_inc(u.free, 1)
                u.wait_drained(dve, i)
                link(V.tensor_tensor(u_sq[:], u_qk[:], u_qk[:], ALU.mult))
                sq = u_sq[:].rearrange("p k (h d) -> p (k h) d", d=HD)
                link(V.tensor_reduce(out=mink[:], in_=sq[:, :, 1:HD], axis=AX_X, op=ALU.add))
                link(V.tensor_tensor(mink[:], mink[:], sq[:, :, 0], ALU.subtract))
                V.tensor_scalar(mink[:], mink[:], 1e-8, None, ALU.max).then_inc(mink_ready.sem, 1)
                dve.wait_ge(mink_ready.sem, mink_ready.at(i))
                V.tensor_scalar(small[:].bitcast(I32), mink[:], 1.0, None, ALU.is_le)
                link(V.tensor_scalar(wsmall[:], mink[:], 1.0, None, ALU.min))
                link(V.tensor_scalar(poly[:], wsmall[:], 1.0 / 110, 1.0, ALU.mult, ALU.add))
                for d in (72, 42, 20, 6):
                    link(V.scalar_tensor_tensor(poly[:], poly[:], 1.0 / d, wsmall[:], ALU.mult, ALU.mult))
                    link(V.tensor_scalar(poly[:], poly[:], 1.0, None, ALU.add))
                dve.wait_ge(eimp_ready.sem, eimp_ready.at(i))
                link(V.tensor_scalar(eimp[:], eimp[:], 1.0, None, ALU.add))
                link(V.reciprocal(eimp[:], eimp[:]))
                V.tensor_scalar(spike[:], eimp[:], thresh[:], None, ALU.is_gt)
                dve.wait_ge(exps_ready.sem, exps_ready.at(i))
                V.tensor_tensor(ctime[:], epos[:], eneg[:], ALU.add)
                link(V.tensor_tensor(sfac[:], epos[:], eneg[:], ALU.subtract))
                link(V.scalar_tensor_tensor(sfac[:], sfac[:], 0.5, rnom[:], ALU.mult, ALU.mult), apart)
                link(V.copy_predicated(sfac[:], small[:].bitcast(I32), poly[:]))
                link(V.tensor_tensor(sfac[:], sfac[:], ksign[:], ALU.mult))
                e3 = emb[:].rearrange("p k (h d) -> p (k h) d", d=HD)
                link(V.tensor_tensor(e3, u_qk[:].rearrange("p k (h d) -> p (k h) d", d=HD), bc(sfac[:].unsqueeze(2), [P, NV, HD]), ALU.mult))
                V.tensor_scalar(e3[:, :, 0:1], ctime[:].unsqueeze(2), 0.5, None, ALU.mult).then_inc(emb_ready.sem, 1)
                split(1, i, link)
                for n in range(UNITS):
                    u = unit("min1", n)
                    u.wait_full(dve, i)
                    if n < 2:
                        V.tensor_reduce(out=zmin[:, 8 * n:8 * n + 8], in_=u.ap.rearrange("p (h k) -> p h k", k=P), axis=AX_X, op=ALU.min).then_inc(u.free, 1)
                    else:
                        last = V.tensor_reduce(out=zmin[:, H + 4 * n - 8:H + 4 * n - 4], in_=u.ap.rearrange("p (h k) -> p h k", k=T), axis=AX_X, op=ALU.min)
                        last.then_inc(u.free, 1)
                u.wait_drained(dve, i)
                V.tensor_scalar(zmin[:], zmin[:], MIN_COSH, None, ALU.max).then_inc(zmin_ready.sem, 1)
                for n in range(UNITS):
                    u = unit("cosh1", n)
                    u.wait_full(dve, i)
                    V.tensor_scalar(zc[:, n * UNIT:(n + 1) * UNIT], u.ap, MIN_COSH, None, ALU.max).then_inc(u.free, 1)
                dve.wait_ge(zsr_ready.sem, zsr_ready.at(i))
                V.tensor_tensor(zmin[:], zmin[:], zsr[:], ALU.add).then_inc(zsum_ready.sem, 1)
                for n in range(UNITS):
                    c = slice(n * UNIT, (n + 1) * UNIT)
                    dve.wait_ge(sqrt_done.sem, sqrt_done.at(i, n + 1))
                    V.tensor_tensor(zc[:, c], zc[:, c], zs[:, c], ALU.add).then_inc(sum_done.sem, 1)
                dve.wait_ge(zln_ready.sem, zln_ready.at(i))
                z3 = zd[:].rearrange("p (k h) -> p k h", k=BLK)
                link(V.scalar_tensor_tensor(nmax[:, :, 0:H], z3, -1.0, z3, ALU.mult, ALU.mult))
                maxima_low(H, 1, link)
                for n in range(UNITS):
                    c = slice(n * UNIT, (n + 1) * UNIT)
                    dve.wait_ge(sq_done.sem, sq_done.at(i, n + 1))
                    u = unit("sub1", n)
                    u.wait_full(dve, i)
                    V.tensor_tensor(zc[:, c], zs[:, c], u.ap, ALU.add).then_inc(u.free, 1)
                u = avuse("avT1")
                ins = head_norm(u, y1, i, link, spike)
                ins.then_inc(u.free, 1)
                for c in range(HC):
                    u = misc(f"f1_{c}")
                    dve.wait_ge(sil_ready.sem, sil_ready.at(i, c + 1))
                    V.scalar_tensor_tensor(hid1[:, c, :], u.ap[:, T:2 * T], s2[:, c:c + 1], sil[:], ALU.mult, ALU.mult).then_inc(u.free, 1)
                u = misc("y1")
                u.wait_full(dve, i)
                dve.wait_ge(out_done.sem, out_done.at(i, 0))
                V.tensor_tensor(xout[:], u.ap[:, 0:T].rearrange("p (k d) -> p k d", k=BLK), x1res[:], ALU.add).then_inc(u.free, 1)

            with dve.Fori(0, NB) as i:
                link = Links(dve, dve_link, i)
                layer0(i, link)
                layer1(i, link)
                link.end()

        @block.gpsimd
        def _(pool):
            G = nc.gpsimd
            RMAX, RADD = bass.bass_isa.ReduceOp.max, bass.bass_isa.ReduceOp.add
            pool.wait_ge(cols_ready, 1)
            G.partition_all_reduce(wall[:], wcol[:], P, RADD).then_inc(all_ready, 1)
            with pool.Fori(0, 2 * PRE_CHUNKS) as c:
                pool.wait_ge(pre_var, c + 1)
                G.tensor_tensor(prs[:], pve[:], mhalf[:, 0:PRE], ALU.pow).then_inc(pre_rstd, 1)
            pool.wait_ge(cols_ready, 2)
            G.partition_all_reduce(gall[:], gcol[:], P, RMAX).then_inc(all_ready, 1)

            def power(dst, src, var, done, i):
                pool.wait_ge(var.sem, var.at(i))
                G.tensor_tensor(dst[:], src[:], mhalf[:, 0:BLK], ALU.pow).then_inc(done.sem, 1)

            def layer0(i, link):
                pool.wait_ge(x_in.sem, x_in.at(i))
                G.tensor_tensor(xres[:], x[:], bc(b_out0[:].unsqueeze(1), [P, BLK, D]), ALU.add).then_inc(xres_ready.sem, 1)
                power(rs, ve, var0, rstd0, i)
                power(rs2, ve2, var0b, rstd0b, i)
                for n in range(UNITS):
                    unit("exp0", n).wait_drained(pool, i)
                    apart(pool)
                    c = prob[:, n * UNIT:(n + 1) * UNIT]
                    if n < 4:
                        t = c.rearrange("p (h q) -> p h q", q=T)
                        G.affine_select(out=t[:, :, 0:P], in_=t[:, :, 0:P], compare_op=ALU.is_gt, fill=0.0, base=0,
                                        pattern=[[0, 4], [1, P]], channel_multiplier=-1)
                        G.affine_select(out=t[:, :, P:T], in_=t[:, :, P:T], compare_op=ALU.is_ge, fill=0.0, base=0,
                                        pattern=[[0, 4], [-1, P]], channel_multiplier=1).then_inc(masked0.sem, 1)
                    else:
                        t = c.rearrange("p (h q) -> p h q", q=P)
                        G.affine_select(out=t, in_=t, compare_op=ALU.is_gt, fill=0.0, base=0,
                                        pattern=[[0, 8], [1, P]], channel_multiplier=-1).then_inc(masked0.sem, 1)
                pool.wait_ge(masked0.sem, masked0.at(i, UNITS))
                apart(pool)
                edge = prob[:, 0:H * T].rearrange("p (h q) -> p h q", q=T)[:, :, P:P + 1]
                G.affine_select(out=edge, in_=edge, compare_op=ALU.is_gt, fill=0.0, base=0, pattern=[[0, H], [0, 1]],
                                channel_multiplier=1).then_inc(masked0.sem, 1)
                misc("rem").wait_drained(pool, i)
                d4 = lambda a: a[:].rearrange("p k (h d) -> p (k h) d", d=HD)
                G.tensor_tensor(d4(gr), d4(remote), bc(gate_r[:].unsqueeze(1), [P, BLK * H, HD]), ALU.mult)
                avuse("avT0").wait_drained(pool, i)
                link(G.tensor_tensor(d4(gl), d4(local), bc(gate_l[:].unsqueeze(1), [P, BLK * H, HD]), ALU.mult))
                G.tensor_tensor(gl[:], gl[:], gr[:], ALU.add).then_inc(gsum_ready.sem, 1)
                pool.wait_ge(gate_ready.sem, gate_ready.at(i))
                link(G.tensor_tensor(gr[:], local[:], remote[:], ALU.subtract))
                link(G.tensor_tensor(d4(gr), d4(gr), bc(gate[:].unsqueeze(2), [P, BLK * H, HD]), ALU.mult))
                G.tensor_tensor(mixed[:], gr[:], remote[:], ALU.add).then_inc(mixed_ready.sem, 1)

            def layer1(i, link):
                power(rs1, ve1, var1, rstd1, i)
                for n in range(UNITS):
                    c = slice(n * UNIT, (n + 1) * UNIT)
                    pool.wait_ge(ln_done.sem, ln_done.at(i, n + 1))
                    G.tensor_tensor(zs[:, c], zs[:, c], zs[:, c], ALU.mult).then_inc(sq_done.sem, 1)
                for n in range(UNITS):
                    pool.wait_ge(exp1_done.sem, exp1_done.at(i, n + 1))
                    apart(pool)
                    c = prob[:, n * UNIT:(n + 1) * UNIT]
                    t = c.rearrange("p (h q) -> p h q", q=T)[:, :, 0:P] if n < 4 else c.rearrange("p (h q) -> p h q", q=P)
                    G.affine_select(out=t, in_=t, compare_op=ALU.is_ge, fill=0.0, base=0, pattern=[[0, 4 if n < 4 else 8], [1, P]],
                                    channel_multiplier=-1).then_inc(masked1.sem, 1)

            with pool.Fori(0, NB) as i:
                link = Links(pool, pool_link, i)
                layer0(i, link)
                layer1(i, link)
                link.end()

        @block.scalar
        def _(act):
            S = nc.scalar
            act.wait_ge(weights_ready, 1)

            def layer0(i, link):
                u = misc("xT")
                u.wait_full(act, i)
                S.activation(xn_t[:], u.ap[:, 0:T], ACT.Copy).then_inc(xnT_ready.sem, 1)
                S.activation(xq_t[:], u.ap[:, T:2 * T], ACT.Identity, bias=bet_col[:], scale=gam_col[:]).then_inc(u.free, 1)
                u = misc("qk")
                u.wait_full(act, i)
                S.activation(qk_t[:, 0:T], u.ap[:, 0:T], ACT.Identity, bias=b_qk0[:, 0:1])
                S.activation(qk_t[:, T:2 * T], u.ap[:, T:2 * T], ACT.Identity, bias=b_qk0[:, 1:2]).then_inc(u.free, 1)
                u.wait_drained(act, i)
                S.activation(parts[:, 0, :], qk_t[:], ACT.Copy).then_inc(hi_ready[0].sem, 1)
                u = misc("mT")
                u.wait_full(act, i)
                S.activation(m_t[:], u.ap.bitcast(BF16)[:, 0:T], ACT.Copy).then_inc(u.free, 1)
                u = misc("lexp")
                u.wait_full(act, i)
                S.activation(prob_l[:].rearrange("p a q -> p (a q)"), u.ap, ACT.Exp, scale=SCALE).then_inc(u.free, 1)
                for n in range(UNITS):
                    u = unit("exp0", n)
                    u.wait_full(act, i)
                    S.activation(prob[:, n * UNIT:(n + 1) * UNIT], u.ap, ACT.Exp, scale=SCALE).then_inc(u.free, 1)
                u = misc("latT")
                u.wait_full(act, i)
                S.activation(lat_t[:], u.ap[0:LD, 0:T], ACT.Copy).then_inc(u.free, 1)
                u = avuse("av0")
                u.wait_full(act, i)
                S.activation(o_t[:].rearrange("p v t -> p (v t)"), u.ap, ACT.Copy).then_inc(u.free, 1)
                act.wait_ge(glog_ready.sem, glog_ready.at(i))
                S.activation(gexp[:], glog[:], ACT.Exp, scale=-1.0).then_inc(gexp_ready.sem, 1)
                u = misc("mixT")
                u.wait_full(act, i)
                S.activation(mix_t[:], u.ap[:, 0:T], ACT.Copy).then_inc(u.free, 1)

            def layer1(i, link):
                u = misc("x1T")
                u.wait_full(act, i)
                S.activation(xn1_t[:], u.ap[:, 0:T], ACT.Copy).then_inc(u.free, 1)
                act.wait_ge(imp_ready.sem, imp_ready.at(i))
                S.activation(eimp[:], imp[:], ACT.Exp, scale=-1.0).then_inc(eimp_ready.sem, 1)
                act.wait_ge(mink_ready.sem, mink_ready.at(i))
                link(S.activation(lnw[:], mink[:], ACT.Ln))
                S.activation(rnom[:], lnw[:], ACT.Exp, scale=-0.5)
                link(S.activation(nom[:], lnw[:], ACT.Exp, scale=0.5))
                S.activation(epos[:], nom[:], ACT.Exp)
                S.activation(eneg[:], nom[:], ACT.Exp, scale=-1.0).then_inc(exps_ready.sem, 1)
                u = misc("embT")
                u.wait_full(act, i)
                S.activation(qk_t[:], u.ap, ACT.Copy).then_inc(u.free, 1)
                u.wait_drained(act, i)
                S.activation(parts[:, 0, :], qk_t[:], ACT.Copy).then_inc(hi_ready[1].sem, 1)
                act.wait_ge(zmin_ready.sem, zmin_ready.at(i))
                link(S.activation(zsq[:], zmin[:], ACT.Square))
                S.activation(zsr[:], zsq[:], ACT.Sqrt, bias=minus1[:]).then_inc(zsr_ready.sem, 1)
                for n in range(UNITS):
                    c = slice(n * UNIT, (n + 1) * UNIT)
                    u = unit("cosh1", n)
                    u.wait_drained(act, i)
                    link(S.activation(zs[:, c], zc[:, c], ACT.Square))
                    S.activation(zs[:, c], zs[:, c], ACT.Sqrt, bias=minus1[:]).then_inc(sqrt_done.sem, 1)
                act.wait_ge(zsum_ready.sem, zsum_ready.at(i))
                S.activation(zd[:], zmin[:], ACT.Ln).then_inc(zln_ready.sem, 1)
                for n in range(UNITS):
                    c = slice(n * UNIT, (n + 1) * UNIT)
                    act.wait_ge(sum_done.sem, sum_done.at(i, n + 1))
                    S.activation(zs[:, c], zc[:, c], ACT.Ln).then_inc(ln_done.sem, 1)
                u = misc("mT1")
                u.wait_full(act, i)
                S.activation(m_t[:], u.ap.bitcast(BF16)[:, 0:T], ACT.Copy).then_inc(u.free, 1)
                for n in range(UNITS):
                    c = slice(n * UNIT, (n + 1) * UNIT)
                    u = unit("sub1", n)
                    u.wait_drained(act, i)
                    S.activation(prob[:, c], zc[:, c], ACT.Exp, scale=-SCALE).then_inc(exp1_done.sem, 1)
                u = avuse("av1")
                u.wait_full(act, i)
                S.activation(o_t[:].rearrange("p v t -> p (v t)"), u.ap, ACT.Copy).then_inc(u.free, 1)
                u = misc("yT")
                u.wait_full(act, i)
                S.activation(y_t[:], u.ap[:, 0:T], ACT.Copy).then_inc(u.free, 1)
                for c in range(HC):
                    u = misc(f"f1_{c}")
                    u.wait_full(act, i)
                    if c:
                        prev = misc(f"f1_{c - 1}")
                        prev.wait_drained(act, i)
                    S.activation(sil[:], u.ap[:, 0:T], ACT.Silu, scale=s1[:, c:c + 1]).then_inc(sil_ready.sem, 1)
                for name, dst, g in (("f2", hid2, g1), ("f3", hid3, g2)):
                    for a in range(2):
                        u = misc(f"{name}_{a}")
                        u.wait_full(act, i)
                        for c in range(2):
                            o = 2 * a + c
                            last = S.activation(dst[:, o, :], u.ap[:, c * T:(c + 1) * T], ACT.Gelu, scale=g[:, o:o + 1])
                        last.then_inc(u.free, 1)

            with act.Fori(0, NB) as i:
                link = Links(act, act_link, i)
                layer0(i, link)
                layer1(i, link)
                link.end()

        @block.tensor
        def _(pe):
            PE = nc.tensor
            pe.wait_ge(weights_ready, 1)

            def scores_by_query(name, masks, i):
                for n in range(UNITS):
                    u = unit(name, n)
                    u.wait_free(pe, i)
                    per = 4 if n < 2 else 2
                    width = BANK // per
                    q = slice(0, P) if n < 2 else slice(P, T)
                    for b in range(2):
                        bank = u.ap[:, b * BANK:(b + 1) * BANK]
                        for s in range(per):
                            h = (8 * n if n < 2 else 4 * (n - 2)) + per * b + s
                            PE.matmul(bank[:, s * width:(s + 1) * width], q_st[:, h // 2, h % 2, q], k_st[:, h // 2, 0:width],
                                      start=(s == 0), stop=False)
                        last = PE.matmul(bank, ident_bf[:], masks[0 if n < 2 else 1][:], start=False, stop=True)
                    last.then_inc(u.full, 1)

            def heads_of(n, b):
                if n < 4:
                    return [2 * n + b], slice(0, P), slice(0, T), 2 * T
                return [4 * (n - 4) + 2 * b, 4 * (n - 4) + 2 * b + 1], slice(P, T), slice(P, T), 2 * P

            def scores_by_key(name, shifted, i):
                for n in range(UNITS):
                    u = unit(name, n)
                    u.wait_free(pe, i)
                    for b in range(2):
                        pairs, keys, queries, width = heads_of(n, b)
                        for s, hp in enumerate(pairs):
                            o = b * BANK + s * width
                            last = PE.matmul(u.ap[:, o:o + width], k_st[:, hp, keys], q_st[:, hp, :, queries],
                                             start=(s == 0), stop=not shifted and s == len(pairs) - 1)
                            if shifted:
                                for e in range(2):
                                    w = width // 2
                                    last = PE.matmul(u.ap[:, o + e * w:o + (e + 1) * w], sel[:, 2 * hp + e, :], m_t[:, queries],
                                                     start=False, stop=(e == 1 and s == len(pairs) - 1))
                    last.then_inc(u.full, 1)

            def shifts_by_key(name, i):
                for n in range(UNITS):
                    u = unit(name, n)
                    u.wait_free(pe, i)
                    for b in range(2):
                        pairs, _, queries, width = heads_of(n, b)
                        for s, hp in enumerate(pairs):
                            for e in range(2):
                                o, w = b * BANK + s * width, width // 2
                                last = PE.matmul(u.ap[:, o + e * w:o + (e + 1) * w], sel[:, 2 * hp + e, :], m_t[:, queries],
                                                 start=(s == 0 and e == 0), stop=(e == 1 and s == len(pairs) - 1))
                    last.then_inc(u.full, 1)

            def attend(use, use_t, o_sig, i):
                use.wait_free(pe, i)
                for v in range(4):
                    for g in range(4):
                        h = 4 * v + g
                        PE.matmul(use.ap[32 * g:32 * g + 32, v * T:(v + 1) * T], v_st[:, 0, h, :], prob[:, h * T:(h + 1) * T], start=True, stop=False)
                    for g in range(4):
                        h = 4 * v + g
                        last = PE.matmul(use.ap[32 * g:32 * g + 32, v * T + P:(v + 1) * T], v_st[:, 1, h, :],
                                         prob[:, H * T + h * P:H * T + (h + 1) * P], start=False, stop=True)
                last.then_inc(use.full, 1)
                use_t.wait_free(pe, i)
                for k in range(BLK):
                    for v in range(4):
                        last = PE.transpose(use_t.ap[:, k * BANK + v * P:k * BANK + (v + 1) * P], o_t[:, v, k * P:(k + 1) * P], ident[:])
                last.then_inc(use_t.full, 1)

            def transposed(u, srcs, i, identity=None):
                u.wait_free(pe, i)
                for n, src in enumerate(srcs):
                    last = PE.transpose(u.ap[:, n * P:(n + 1) * P], src, ident[:])
                last.then_inc(u.full, 1)

            def maxima_t(name, layer, i):
                u = misc(name)
                pe.wait_ge(nmax_ready[layer].sem, nmax_ready[layer].at(i))
                u.wait_free(pe, i)
                for k in range(BLK):
                    last = PE.transpose(u.ap.bitcast(BF16)[:, k * P:(k + 1) * P], nmax2[:, k, :], ident_bf[:])
                last.then_inc(u.full, 1)

            def layer0(i):
                pe.wait_ge(xf_ready.sem, xf_ready.at(i))
                transposed(misc("xT"), [xn[:, 0, :], xn[:, 1, :], xf[:, 0, :], xf[:, 1, :]], i)
                pe.wait_ge(xnT_ready.sem, xnT_ready.at(i))
                u = misc("qk")
                u.wait_free(pe, i)
                PE.matmul(u.ap[:, 0:T], w_qkv0[:, 0:D], xn_t[:], start=True, stop=True)
                PE.matmul(u.ap[:, T:2 * T], w_qkv0[:, D:2 * D], xn_t[:], start=True, stop=True).then_inc(u.full, 1)
                u = misc("v")
                u.wait_free(pe, i)
                for k in range(BLK):
                    last = PE.matmul(u.ap[:, k * P:(k + 1) * P], xn_t[:, k * P:(k + 1) * P], w_qkv0[:, 2 * D:3 * D], start=True, stop=True)
                last.then_inc(u.full, 1)
                u = misc("rqkv")
                u.wait_free(pe, i)
                pe.wait_ge(pooled_ready.sem, pooled_ready.at(i))
                PE.matmul(u.ap[0:LD, 0:T], w_rq[:], xn_t[:], start=True, stop=True)
                PE.matmul(u.ap[0:LD, T:T + NLAT], w_rkv[:, 0:LD], pooled[:, 0, :], start=True, stop=True)
                PE.matmul(u.ap[:, T + NLAT:T + NLAT + LD], pooled[:].rearrange("p a l -> p (a l)"), w_rkv[:, LD:2 * LD], start=True, stop=True).then_inc(u.full, 1)
                pe.wait_ge(stacked[0].sem, stacked[0].at(i))
                scores_by_query("max0", (win0, win1), i)
                u = misc("lmax")
                u.wait_free(pe, i)
                pe.wait_ge(rk_ready.sem, rk_ready.at(i))
                for k in range(BLK):
                    PE.matmul(u.ap[:, k * T:(k + 1) * T], rq_t[:, k * P:(k + 1) * P], rk_m[:].rearrange("p h l -> p (h l)"), start=(k == 0), stop=False)
                PE.matmul(u.ap, ident_bf[:], winl[:], start=False, stop=True).then_inc(u.full, 1)
                maxima_t("mT", 0, i)
                misc("mT").wait_drained(pe, i)
                u = misc("lexp")
                u.wait_free(pe, i)
                for p in range(LH // 2):
                    PE.matmul(u.ap[:, p * T:(p + 1) * T], rk_m[:, 2 * p:2 * p + 2, :].rearrange("p h l -> p (h l)"), rq_t[:], start=(p == 0), stop=False)
                    PE.matmul(u.ap[:, p * T:(p + 1) * T], sel[:, H + p, :], m_t[:], start=False, stop=False)
                last = PE.matmul(u.ap, ident_bf[:], winl_t[:], start=False, stop=True)
                last.then_inc(u.full, 1)
                scores_by_key("exp0", True, i)
                u = misc("lo")
                u.wait_free(pe, i)
                misc("lexp").wait_drained(pe, i)
                pe.wait_ge(rv_ready.sem, rv_ready.at(i))
                for p in range(LH // 2):
                    last = PE.matmul(u.ap[0:2 * LD, 0:T], rv_st[:, p, :], prob_l[:, p, :], start=(p == 0), stop=(p == LH // 2 - 1))
                last.then_inc(u.full, 1)
                u.wait_drained(pe, i)
                u = misc("loT")
                u.wait_free(pe, i)
                apart(pe)
                for k in range(BLK):
                    last = PE.transpose(u.ap[:, k * 2 * LD:(k + 1) * 2 * LD], lo_t[:, k * P:(k + 1) * P], ident[0:2 * LD, 0:2 * LD])
                last.then_inc(u.full, 1)
                u.wait_drained(pe, i)
                u = misc("latT")
                u.wait_free(pe, i)
                for k in range(BLK):
                    last = PE.transpose(u.ap[0:LD, k * P:(k + 1) * P], lat[:, k, :], ident[:])
                last.then_inc(u.full, 1)
                u.wait_drained(pe, i)
                u = misc("rem")
                u.wait_free(pe, i)
                for k in range(BLK):
                    last = PE.matmul(u.ap[:, k * D:(k + 1) * D], lat_t[:, k * P:(k + 1) * P], w_rout[:], start=True, stop=True)
                last.then_inc(u.full, 1)
                pe.wait_ge(masked0.sem, masked0.at(i))
                attend(avuse("av0"), avuse("avT0"), o_ready[0], i)
                pe.wait_ge(mixed_ready.sem, mixed_ready.at(i))
                transposed(misc("mixT"), [mixed[:, 0, :], mixed[:, 1, :]], i)
                misc("mixT").wait_drained(pe, i)
                u = misc("y0")
                u.wait_free(pe, i)
                pe.wait_ge(xq_ready.sem, xq_ready.at(i))
                for k in range(BLK):
                    c = slice(k * P, (k + 1) * P)
                    PE.matmul(u.ap[:, c], mix_t[:, c], w_out0[:], start=True, stop=False)
                    last = PE.matmul(u.ap[:, c], xq_t[:, c], w_qs[:], start=False, stop=True)
                last.then_inc(u.full, 1)

            def layer1(i):
                pe.wait_ge(xn1_ready.sem, xn1_ready.at(i))
                transposed(misc("x1T"), [xn1[:, 0, :], xn1[:, 1, :]], i)
                misc("x1T").wait_drained(pe, i)
                for k, name in enumerate(("qkv1a", "qkv1b")):
                    u = misc(name)
                    u.wait_free(pe, i)
                    PE.matmul(u.ap[:, 0:3 * D], xn1_t[:, k * P:(k + 1) * P], w_qkv1[:], start=True, stop=True).then_inc(u.full, 1)
                pe.wait_ge(emb_ready.sem, emb_ready.at(i))
                transposed(misc("embT"), [emb[:, 0, 0:D], emb[:, 1, 0:D], emb[:, 0, D:2 * D], emb[:, 1, D:2 * D]], i)
                pe.wait_ge(stacked[1].sem, stacked[1].at(i))
                scores_by_query("min1", (cau0, cau1), i)
                scores_by_key("cosh1", False, i)
                maxima_t("mT1", 1, i)
                misc("mT1").wait_drained(pe, i)
                shifts_by_key("sub1", i)
                pe.wait_ge(masked1.sem, masked1.at(i))
                attend(avuse("av1"), avuse("avT1"), o_ready[1], i)
                avuse("avT1").wait_drained(pe, i)
                transposed(misc("yT"), [y1[:, 0, :], y1[:, 1, :]], i)
                for c in range(HC):
                    u = misc(f"f1_{c}")
                    u.wait_free(pe, i)
                    PE.matmul(u.ap[:, 0:T], w1t[:, c * P:(c + 1) * P], xn1_t[:], start=True, stop=True)
                    PE.matmul(u.ap[:, T:2 * T], w2t[:, c * P:(c + 1) * P], xn1_t[:], start=True, stop=True).then_inc(u.full, 1)
                for name, w, src, prior in (("f2", h1t, hid1, ("f1_2", "f1_3")), ("f3", h2t, hid2, ("f2_0", "f2_1"))):
                    for p in prior:
                        misc(p).wait_drained(pe, i)
                    for a in range(2):
                        u = misc(f"{name}_{a}")
                        u.wait_free(pe, i)
                        for c in range(2):
                            o = 2 * a + c
                            for k in range(HC):
                                last = PE.matmul(u.ap[:, c * T:(c + 1) * T], w[:, k, o * P:(o + 1) * P], src[:, k, :], start=(k == 0), stop=(k == HC - 1))
                        last.then_inc(u.full, 1)
                misc("f3_0").wait_drained(pe, i)
                misc("f3_1").wait_drained(pe, i)
                misc("yT").wait_drained(pe, i)
                u = misc("y1")
                u.wait_free(pe, i)
                for k in range(BLK):
                    c = slice(k * P, (k + 1) * P)
                    PE.matmul(u.ap[:, c], y_t[:, c], w_out1[:], start=True, stop=False)
                    for n in range(HC):
                        last = PE.matmul(u.ap[:, c], hid3[:, n, c], w3t[:, n, :], start=False, stop=(n == HC - 1))
                last.then_inc(u.full, 1)

            with pe.Fori(0, NB) as i:
                layer0(i)
                layer1(i)


_IN = ["L0_attn_x", "L0_attn_qkv_w", "L0_attn_qkv_b", "L0_attn_rq_w", "L0_attn_rq_b", "L0_attn_rkv_w", "L0_attn_rkv_b", "L0_attn_rout_w",
       "L0_attn_rout_b", "L0_attn_out_w", "L0_attn_out_b", "L0_attn_gl_w", "L0_attn_gr_w", "L0_ffn_weight", "L0_ffn_ln_gamma",
       "L0_ffn_ln_beta", "L1_attn_W_qkv", "L1_attn_b_qkv", "L1_attn_W_out", "L1_attn_b_out", "L1_attn_w_sur", "L1_attn_b_sur",
       "L1_attn_threshold", "L1_ffn_w1_s", "L1_ffn_w2_s", "L1_ffn_h1_s", "L1_ffn_h2_s", "L1_ffn_w3_s"]
_COLUMNS = ("L1_ffn_w1_s", "L1_ffn_w2_s", "L1_ffn_h1_s", "L1_ffn_h2_s")
_TRANSPOSED = {"w1t": "L1_ffn_w1_w", "w2t": "L1_ffn_w2_w", "h1t": "L1_ffn_h1_w", "h2t": "L1_ffn_h2_w", "w3t": "L1_ffn_w3_w"}


def kernel(**inputs):
    import concourse.bacc as bacc
    from concourse.bass_utils import run_bass_kernel_spmd

    nc = bacc.Bacc("TRN2", target_bir_lowering=False, num_devices=1)
    arrays, A = {}, {}
    laid = {n: np.ascontiguousarray(inputs[n]).reshape(inputs[n].shape or (1,)) for n in _IN}
    laid |= {n: np.ascontiguousarray(np.asarray(inputs[src]).T) for n, src in _TRANSPOSED.items()}
    laid["b_qk0_cols"] = np.ascontiguousarray(np.asarray(inputs["L0_attn_qkv_b"])[:2 * D].reshape(2, P).T)
    laid |= {n + "_cols": np.ascontiguousarray(laid.pop(n).reshape(HC, P).T) for n in _IN if n in _COLUMNS}
    laid |= shape_constants()
    for name, a in laid.items():
        arrays[f"in_{name}"] = a
        A[name] = nc.dram_tensor(f"in_{name}", list(a.shape), mybir.dt.from_np(a.dtype), kind="ExternalInput").ap()
    out = nc.dram_tensor("out_0", [NB, T, D], F32, kind="ExternalOutput").ap()
    build(nc, A, out)
    r = run_bass_kernel_spmd(nc, [arrays], core_ids=[0])
    return r.results[0]["out_0"]
```

```python
from contextlib import ExitStack

import numpy as np

import concourse.bass as bass
from concourse import mybir

F32 = mybir.dt.float32
BF16 = mybir.dt.bfloat16
I32 = mybir.dt.int32
ALU = mybir.AluOpType
ACT = mybir.ActivationFunctionType
AX_X = mybir.AxisListType.X

P = 128
NB, T, D = 32, 256, 128
BLK = T // P
H, HD = 16, 8
HP = H // 2
NLAT, LH, LD = 64, 4, 32
POOL = T // NLAT
HID = 512
HC = HID // P
BANK = 512
SLOTS = [(0, 0), (0, 1), (0, 2), (1, 0), (1, 1), (1, 2), (2, 0), (2, 1)]
MLO = 32
NM = H + LH
BIG = 1e30
SCALE = float(1.0 / np.sqrt(HD))
LN_EPS, FFN_LN_EPS, FFN_EPS, QB = 1e-5, 1e-3, 1e-5, 128.0
MIN_COSH = float(np.float32(1.0 + 1e-7))
PRE = 8
PRE_CHUNKS = NB * T // (P * PRE)
SCOLS = H * T + H * P
UNIT = 2 * BANK
UNITS = SCOLS // UNIT


def shape_constants():
    bf = np.dtype("bfloat16")
    q, k = np.arange(P)[:, None], np.arange(P)[None, :]
    c = {}
    c["ident"] = np.eye(P, dtype=np.float32)
    c["ident_bf"] = np.eye(P, dtype=bf)
    own = (k < q)
    first = own | ((q == 0) & (k == 0))
    prev = (k >= q) & (k >= 1)
    neg = lambda ok: np.where(ok, 0.0, -BIG)
    c["win0"] = np.tile(neg(first), (1, 4)).astype(bf)
    c["win1"] = np.concatenate([neg(prev), neg(own)], 1).astype(bf)
    c["cau0"] = np.tile(-neg(k <= q), (1, 4)).astype(bf)
    c["cau1"] = np.concatenate([np.zeros((P, P)), -neg(k <= q)], 1).astype(bf)
    lat = np.arange(NLAT)[None, :]
    blocks = []
    for b in range(BLK):
        chunk = (b * P + q) // POOL
        blocks.append(np.tile(neg((lat < chunk) | ((chunk == 0) & (lat == 0))), (1, LH)))
    c["winl"] = np.concatenate(blocks, 1).astype(bf)
    ok = (np.arange(P)[:, None] % NLAT) < np.arange(T)[None, :] // POOL
    c["winl_t"] = neg(ok).astype(bf)
    sel = np.zeros((P, H + LH // 2, P), np.float32)
    for h in range(H):
        sel[h, h, :] = 1
        sel[MLO + h, h, :] = 1
    for p in range(LH // 2):
        for e in range(2):
            sel[H + 2 * p + e, H + p, e * NLAT:(e + 1) * NLAT] = 1
            sel[MLO + H + 2 * p + e, H + p, e * NLAT:(e + 1) * NLAT] = 1
    c["sel"] = sel.astype(bf)
    rows = np.arange(P)[:, None, None] // NLAT
    heads = 2 * np.arange(LH // 2)[None, :, None] + rows
    c["lat_cols"] = (heads == (np.arange(LD) // (LD // LH))[None, None, :]).astype(np.float32)
    ones = np.zeros((P, LH // 2, 2 * LD), np.float32)
    ones[:, :, LD:LD + LH] = heads == np.arange(LH)[None, None, :]
    c["lat_ones"] = ones
    c["lat_rows"] = (np.arange(LD)[:, None] // (LD // LH) == np.arange(LH)[None, :]).astype(np.float32)
    return c


class Sequence:

    def __init__(self, t, lag):
        self.t, self.lag = t, lag

    def index(self):
        return self.t - self.lag


class Signal:

    def __init__(self, sem, per=1, step=1, start=0):
        self.sem, self.per, self.step, self.start = sem, per, step, start

    def at(self, s, n=None):
        n = self.per if n is None else n
        each = self.per * self.step
        return s.t * each + (n * self.step + self.start - s.lag * each)


class Phase:

    def __init__(self, t0, trips, stages):
        self.t0, self.trips, self.stages = t0, trips, stages


LAG = {"first": 0, "middle": 1, "last": 2, "end": 3, "out": 4}


def pipeline_phases():
    deepest = max(LAG.values())
    at_work = lambda t: tuple(n for n, lag in LAG.items() if 0 <= t - lag < NB)
    single = lambda t: Phase(t, 1, at_work(t))
    head, tail = range(deepest + 1), range(NB - 1, NB + deepest)
    return [single(t) for t in head] + [Phase(deepest + 1, NB - deepest - 2, tuple(LAG))] + [single(t) for t in tail]


PHASES = pipeline_phases()


class Run:

    def __init__(self, phase, t):
        self.phase, self.t = phase, t
        self.first, self.middle, self.last, self.end, self.out = (Sequence(t, LAG[n]) if n in phase.stages else None for n in LAG)

    def before(self):
        if self.phase.trips > 1:
            return Run(self.phase, self.t - 1)
        return next(Run(p, self.t - 1) for p in PHASES if p.t0 <= self.t - 1 < p.t0 + p.trips)


class Buffer:

    def __init__(self, ap, uses, full, free):
        self.ap, self.uses, self.full, self.free = ap, uses, full, free

    def use(self, run, name):
        before = 0
        for ph in PHASES:
            names = [n for stage, n in self.uses if stage in ph.stages]
            if ph is run.phase:
                break
            before += ph.trips * len(names)
        return Use(self, run.t * len(names) + (before + names.index(name) - run.phase.t0 * len(names)))


class Use:

    def __init__(self, buffer, count):
        self.ap, self.full, self.free, self.count = buffer.ap, buffer.full, buffer.free, count

    def wait_free(self, pe):
        pe.wait_ge(self.free, self.count + 1)

    def wait_full(self, eng):
        eng.wait_ge(self.full, self.count + 1)

    def wait_drained(self, eng):
        eng.wait_ge(self.free, self.count + 2)


DVE_LINKS = {"first": 7, "middle": 29, "last": 4, "end": 3}


def bc(ap, shape):
    return ap.to_broadcast(list(shape))


def build(nc, A, out):
    ctx = ExitStack()
    with ctx:
        def sb(name, shape, dt=F32):
            return ctx.enter_context(nc.sbuf_tensor(name, list(shape), dt))

        def sem(name):
            return ctx.enter_context(nc.semaphore(name))

        ahead = []

        def sig(name, per=1, step=1, start=0):
            s = Signal(sem(name), per, step, start)
            if start:
                ahead.append(s)
            return s

        ident, ident_bf = sb("ident", [P, P]), sb("ident_bf", [P, P], BF16)
        win0, win1 = sb("win0", [P, BANK], BF16), sb("win1", [P, T], BF16)
        cau0, cau1 = sb("cau0", [P, BANK], BF16), sb("cau1", [P, T], BF16)
        winl, winl_t = sb("winl", [P, BANK], BF16), sb("winl_t", [P, T], BF16)
        sel = sb("sel", [P, H + LH // 2, P], BF16)
        lat_cols, lat_rows = sb("lat_cols", [P, LH // 2, LD]), sb("lat_rows", [LD, LH])
        w_qkv0, b_qk0, b_v0 = sb("w_qkv0", [P, 3 * D]), sb("b_qk0", [P, 2]), sb("b_v0", [P, D])
        w_rq, b_rq = sb("w_rq", [P, LD]), sb("b_rq", [LD, 1])
        w_rkv, b_rk, b_rv = sb("w_rkv", [P, 2 * LD]), sb("b_rk", [LD, 1]), sb("b_rv", [P, LD])
        w_rout, b_rout = sb("w_rout", [LD, D]), sb("b_rout", [P, D])
        w_out0, b_out0 = sb("w_out0", [P, D]), sb("b_out0", [P, D])
        gate_l, gate_r = sb("gate_l", [P, HD]), sb("gate_r", [P, HD])
        w_qs = sb("w_qs", [P, D])
        gam_col, bet_col = sb("gam_col", [P, 1]), sb("bet_col", [P, 1])
        w_qkv1, b_qk1, b_v1 = sb("w_qkv1", [P, 3 * D]), sb("b_qk1", [P, 2 * D]), sb("b_v1", [P, D])
        w_out1, b_out1 = sb("w_out1", [P, D]), sb("b_out1", [P, D])
        w_sur, b_sur, thresh = sb("w_sur", [P, D]), sb("b_sur", [P, 1]), sb("thresh", [P, 1])
        w1t, w2t = sb("w1t", [P, HID]), sb("w2t", [P, HID])
        h1t, h2t = sb("h1t", [P, HC, HID]), sb("h2t", [P, HC, HID])
        s1, s2, g1, g2 = (sb(n, [P, HC]) for n in ("s1", "s2", "g1", "g2"))
        w3t = sb("w3t", [P, HC, D])
        mhalf = sb("mhalf", [P, 2 * PRE])
        minus1 = sb("minus1", [P, 1])
        ksign = sb("ksign", [P, BLK * 2 * H])

        zc, zs = sb("zc", [P, SCOLS]), sb("zs", [P, SCOLS])
        prob0 = sb("prob0", [P, SCOLS])
        w_tern, wn, wr, gam_row, bet_row, s3 = (prob0[:, n * D:(n + 1) * D] for n in range(6))
        px = zc[:, 0:2 * PRE * D].rearrange("p (b n d) -> p b n d", b=2, d=D)
        pn = zs[:, 0:PRE * D].rearrange("p (n d) -> p n d", d=D)
        pf = zs[:, PRE * D:2 * PRE * D].rearrange("p (n d) -> p n d", d=D)
        pst, pmv = sb("pst", [P, PRE, 6]), sb("pmv", [P, PRE, 2])
        pve, prs = sb("pve", [P, PRE]), sb("prs", [P, PRE])
        pmax = sb("pmax", [P, PRE_CHUNKS])
        gcol, gall = sb("gcol", [P, 1]), sb("gall", [P, 1])
        thr, nthr = sb("thr", [P, 1]), sb("nthr", [P, 1])
        wcol, wall = sb("wcol", [P, 1]), sb("wall", [P, 1])
        beta, rbeta = sb("beta", [P, 1]), sb("rbeta", [P, 1])

        x = sb("x", [P, BLK, D])
        xres = sb("xres", [P, BLK, D])
        st, mv = sb("st", [P, BLK, 6]), sb("mv", [P, BLK, 2])
        ve, rs = sb("ve", [P, BLK]), sb("rs", [P, BLK])
        ve2, rs2 = sb("ve2", [P, BLK]), sb("rs2", [P, BLK])
        xn, xf = sb("xn", [P, BLK, D]), sb("xf", [P, BLK, D])
        xn_t, xa_t, xq_t = sb("xn_t", [P, T]), sb("xa_t", [P, T]), sb("xq_t", [P, T])
        pooled = sb("pooled", [P, 2, NLAT])
        qk_t, resid = sb("qk_t", [P, 2 * T]), sb("resid", [P, 2 * T])
        parts = sb("parts", [P, 3, 2 * T], BF16)
        q_st = [sb(f"q_st{n}", [P, HP, 2, T], BF16) for n in range(2)]
        k_st = [sb(f"k_st{n}", [P, HP, T], BF16) for n in range(2)]
        v_st = [sb(f"v_st{n}", [P, BLK, H, 32]) for n in range(2)]
        rq_t, rk_t, rk_m = sb("rq_t", [LD, T]), sb("rk_t", [LD, NLAT]), sb("rk_m", [LD, LH, NLAT])
        rv, rv_st = sb("rv", [P, LD]), sb("rv_st", [P, LH // 2, 2 * LD])

        nmax = [sb("nmax0", [P, BLK, NM]), sb("nmax1", [P, BLK, H])]
        nmax2 = [sb(f"nmax2_{n}", [P, BLK, P], BF16) for n in range(2)]
        m_t = [sb(f"m_t{n}", [P, T], BF16) for n in range(2)]
        prob_l = sb("prob_l", [P, LH // 2, T])
        o_t = sb("o_t", [P, 4, T])
        rsum, rrec = sb("rsum", [P, BLK * H]), sb("rrec", [P, BLK * H])
        lo_t = sb("lo_t", [2 * LD, T])
        lsum, lrec = sb("lsum", [P, BLK, LH]), sb("lrec", [P, BLK, LH])
        local, lat = sb("local", [P, BLK, D]), sb("lat", [P, BLK, LD])
        lat_t = sb("lat_t", [LD, T])
        remote = sb("remote", [P, BLK, D])
        gl, gr = sb("gl", [P, BLK, D]), sb("gr", [P, BLK, D])
        glog, gexp, gate = (sb(n, [P, BLK * H]) for n in ("glog", "gexp", "gate"))
        mixed, out_t = gr, sb("out_t", [P, T])
        x1 = sb("x1", [P, BLK, D])
        st1, mv1 = sb("st1", [P, BLK, 6]), sb("mv1", [P, BLK, 2])
        ve1, rs1 = sb("ve1", [P, BLK]), sb("rs1", [P, BLK])
        xn1 = sb("xn1", [P, BLK, D])
        xs1 = resid[:, 0:BLK * D].rearrange("p (k d) -> p k d", k=BLK)
        imp, eimp = sb("imp", [P, BLK]), sb("eimp", [P, BLK])
        xn1_t = sb("xn1_t", [P, T])
        u_qk, u_sq = sb("u_qk", [P, BLK, 2 * D]), resid[:].rearrange("p (k d) -> p k d", k=BLK)
        v_new = sb("v_new", [P, BLK, D])
        NV = BLK * 2 * H
        mink, lnw, nom, rnom, epos, eneg = (sb(n, [P, NV]) for n in ("mink", "lnw", "nom", "rnom", "epos", "eneg"))
        ctime, sfac, wsmall, poly, small = (sb(n, [P, NV]) for n in ("ctime", "sfac", "wsmall", "poly", "small"))
        emb = sb("emb", [P, BLK, 2 * D])

        x1res, spike = sb("x1res", [P, BLK, D]), sb("spike", [P, BLK])
        zmin, zsq, zsr, zd = (sb(n, [P, BLK * H]) for n in ("zmin", "zsq", "zsr", "zd"))
        prob1 = zs
        y1 = local
        hid1, hid2, hid3 = (sb(n, [P, HC, T]) for n in ("hid1", "hid2", "hid3"))
        xatt, xold = sb("xatt", [P, BLK, D]), sb("xold", [P, BLK, D])

        scr = nc.dram_tensor("scr", [2, 2, P, len(SLOTS), T], BF16, kind="Internal").ap()

        pu = ctx.enter_context(nc.psum_tensor("pu", [P, 2, UNIT], F32))
        pav = ctx.enter_context(nc.psum_tensor("pav", [P, 2 * BANK], F32))
        pm = ctx.enter_context(nc.psum_tensor("pm", [P, 2, BANK], F32))
        F, M, L, E, O = "first", "middle", "last", "end", "out"
        MAX, MIN, EXP, COSH, SUB = ([f"{n}{u}" for u in range(UNITS)] for n in ("max", "min", "exp", "cosh", "sub"))
        uses = lambda stage, names: [(stage, n) for n in names]
        UNIT_USES = [uses(M, MAX[0::2]) + uses(L, MIN[0::2]) + uses(M, EXP[0::2]) + uses(L, SUB[0::3]),
                     uses(M, MAX[1::2]) + uses(L, MIN[1::2]) + uses(L, COSH) + uses(L, SUB[1::3])]
        MISC_ORDER = [(M, "lmax"), (M, "mT"), (F, "xT"), (E, "yT"), (F, "qk"), (E, "y1"), (M, "lexp"), (M, "lo"), (M, "loT"), (M, "latT"),
                      (M, "rem"), (E, "f2_0"), (E, "f2_1"), (L, "f1_0"), (L, "f1_1"), (L, "f1_2"), (L, "f1_3"), (M, "mixT"), (M, "y0"),
                      (F, "rqkv"), (F, "v"), (L, "mT1"), (M, "x1T"), (M, "qkv1a"), (M, "qkv1b"), (O, "yffn"), (E, "f3_0"), (M, "embT"),
                      (E, "f3_1")]
        MISC_USES = [MISC_ORDER[0::2], MISC_ORDER[1::2]]
        AV_USES = uses(E, ["av1", "avT1"]) + uses(M, EXP[1::2]) + uses(M, ["av0", "avT0"]) + uses(L, SUB[2::3])

        def buffer(name, ap, users):
            one = Buffer(ap, users, sem(name + "_full"), sig(name + "_free", start=1).sem)
            return {n: one for _, n in users}

        score_banks = buffer("unit0", pu[:, 0, :], UNIT_USES[0]) | buffer("unit1", pu[:, 1, :], UNIT_USES[1]) | buffer("av", pav[:, :], AV_USES)
        misc_banks = buffer("misc0", pm[:, 0, :], MISC_USES[0]) | buffer("misc1", pm[:, 1, :], MISC_USES[1])
        unit = avuse = lambda run, n: score_banks[n].use(run, n)
        misc = lambda run, n: misc_banks[n].use(run, n)

        loads = []
        consts_in, passed = sem("consts_in"), sem("passed")
        zeros_set = sem("zeros_set")
        pre_in, pre_used = [sem("pre_in0"), sem("pre_in1")], sem("pre_used")
        pre_var, pre_rstd = sem("pre_var"), sem("pre_rstd")
        cols_ready, all_ready = sem("cols_ready"), sem("all_ready")
        weights_ready = sem("weights_ready")
        pre_link = sem("pre_link")

        x_in = sig("x_in", 1, 16)
        var0, rstd0, var0b, rstd0b = sig("var0"), sig("rstd0"), sig("var0b"), sig("rstd0b")
        xn_ready, xres_ready, xf_ready = sig("xn_ready", start=1), sig("xres_ready", start=1), sig("xf_ready")
        xq_ready = sig("xq_ready", start=1)
        pooled_ready = sig("pooled_ready")
        hi_ready = [sig("hi_ready0"), sig("hi_ready1")]
        parts_ready = [sig("parts_ready0"), sig("parts_ready1")]
        scr_written = [sig("scr_written0", 6, 16), sig("scr_written1", 6, 16)]
        stacked = [sig("stacked0", 3, 16, start=1), sig("stacked1", 3, 16, start=1)]
        rq_ready, rk_ready, rv_ready = sig("rq_ready"), sig("rk_ready"), sig("rv_ready")
        nmax_ready = [sig("nmax_ready0"), sig("nmax_ready1")]
        masked0 = sig("masked0", UNITS + 1)
        gsum_ready, glog_ready, gexp_ready, gate_ready = (sig(n) for n in ("gsum_ready", "glog_ready", "gexp_ready", "gate_ready"))
        mixed_ready = sig("mixed_ready")

        var1, rstd1, xn1_ready, x1res_ready = sig("var1"), sig("rstd1"), sig("xn1_ready"), sig("x1res_ready")
        imp_ready, eimp_ready = sig("imp_ready"), sig("eimp_ready")
        mink_ready, exps_ready, emb_ready = (sig(n) for n in ("mink_ready", "exps_ready", "emb_ready"))
        v1_ready, spike_ready = sig("v1_ready"), sig("spike_ready")
        zmin_ready, zsr_ready, zsum_ready, zln_ready = (sig(n) for n in ("zmin_ready", "zsr_ready", "zsum_ready", "zln_ready"))
        sqrt_done, sum_done, ln_done, exp1_done, masked1 = (
            sig(n, UNITS) for n in ("sqrt_done", "sum_done", "ln_done", "exp1_done", "masked1"))
        SQUARED_BY_POOL = (1, 4)
        squared = [sig("squared_act", UNITS - len(SQUARED_BY_POOL)), sig("squared_pool", len(SQUARED_BY_POOL))]
        hid2_ready, hid3_ready, xold_ready = sig("hid2_ready"), sig("hid3_ready"), sig("xold_ready")
        sq_done = [sig(f"sq_done{k}", UNITS // 2) for k in range(2)]
        sil_ready = sig("sil_ready", HC)
        out_done = sig("out_done", 1, 16, start=1)
        dve_link = {F: sig("dve_first", DVE_LINKS[F]), M: sig("dve_middle", DVE_LINKS[M]), L: sig("dve_last", DVE_LINKS[L]), E: sig("dve_end", DVE_LINKS[E])}
        act_link = {M: sig("act_middle", 2), L: sig("act_last", 1)}
        pool_link = {M: sig("pool_middle", 3)}

        class Links:

            def __init__(self, eng, counter, seq):
                self.eng, self.counter, self.seq, self.n = eng, counter, seq, 0

            def __call__(self, ins, after=None):
                self.n += 1
                ins.then_inc(self.counter.sem, 1)
                self.eng.wait_ge(self.counter.sem, self.counter.at(self.seq, self.n))
                if after:
                    after(self.eng)

            def end(self):
                assert self.n == self.counter.per, (self.counter.sem, self.n)

        def links_of(eng, counters, run):
            seqs = {F: run.first, M: run.middle, L: run.last, E: run.end, O: run.out}
            return {n: Links(eng, c, seqs[n]) for n, c in counters.items() if seqs[n] is not None}

        def apart(eng):
            eng.sem_inc(passed, 1)

        def phases(eng, iteration):
            for phase in PHASES:
                if phase.trips == 1:
                    iteration(Run(phase, phase.t0))
                else:
                    with eng.Fori(phase.t0, phase.t0 + phase.trips) as t:
                        iteration(Run(phase, t))

        block = ctx.enter_context(nc.Block())

        def row(ap, n=P):
            return ap.rearrange("(o n) -> o n", o=1).to_broadcast([n, ap.shape[0]])

        def col(ap):
            return ap.rearrange("(p o) -> p o", o=1)

        for name, dst in (("ident", ident), ("ident_bf", ident_bf), ("win0", win0), ("win1", win1), ("cau0", cau0),
                          ("cau1", cau1), ("winl", winl), ("winl_t", winl_t), ("sel", sel), ("lat_cols", lat_cols), ("lat_rows", lat_rows),
                          ("lat_ones", rv_st)):
            loads.append((dst[:], A[name]))
        loads += [
            (w_qkv0[:], A["L0_attn_qkv_w"]), (b_qk0[:], A["b_qk0_cols"]),
            (b_v0[:], row(A["L0_attn_qkv_b"][2 * D:3 * D])), (w_rq[:], A["L0_attn_rq_w"]), (b_rq[:], col(A["L0_attn_rq_b"])),
            (w_rkv[:], A["L0_attn_rkv_w"]), (b_rk[:], col(A["L0_attn_rkv_b"][0:LD])), (b_rv[:], row(A["L0_attn_rkv_b"][LD:2 * LD])),
            (w_rout[:], A["L0_attn_rout_w"]), (b_rout[:], row(A["L0_attn_rout_b"])), (w_out0[:], A["L0_attn_out_w"]),
            (b_out0[:], row(A["L0_attn_out_b"])), (gate_l[:], row(A["L0_attn_gl_w"].rearrange("a o -> (a o)"))),
            (gate_r[:], row(A["L0_attn_gr_w"].rearrange("a o -> (a o)"))), (w_tern, A["L0_ffn_weight"]),
            (gam_row, row(A["L0_ffn_ln_gamma"])), (bet_row, row(A["L0_ffn_ln_beta"])),
            (gam_col[:], col(A["L0_ffn_ln_gamma"])), (bet_col[:], col(A["L0_ffn_ln_beta"])),
            (w_qkv1[:], A["L1_attn_W_qkv"]), (b_qk1[:], row(A["L1_attn_b_qkv"][0:2 * D])), (b_v1[:], row(A["L1_attn_b_qkv"][2 * D:3 * D])),
            (w_out1[:], A["L1_attn_W_out"]), (b_out1[:], row(A["L1_attn_b_out"])), (w_sur[:], row(A["L1_attn_w_sur"])),
            (b_sur[:], row(A["L1_attn_b_sur"])), (thresh[:], row(A["L1_attn_threshold"])),
            (w1t[:], A["w1t"]), (w2t[:], A["w2t"]), (h1t[:], A["h1t"].rearrange("(c p) n -> p c n", p=P)),
            (h2t[:], A["h2t"].rearrange("(c p) n -> p c n", p=P)), (w3t[:], A["w3t"].rearrange("(c p) n -> p c n", p=P)),
            (s3, row(A["L1_ffn_w3_s"])),
        ]
        for dst, name in ((s1, "L1_ffn_w1_s"), (s2, "L1_ffn_w2_s"), (g1, "L1_ffn_h1_s"), (g2, "L1_ffn_h2_s")):
            loads.append((dst[:], A[name + "_cols"]))

        x_seq = A["L0_attn_x"].rearrange("b (k p) d -> b p k d", p=P)
        out_seq = out.rearrange("b (k p) d -> b p k d", p=P)
        x_chunk = A["L0_attn_x"].rearrange("b t d -> (b t) d").rearrange("(c n p) d -> c p n d", p=P, n=PRE)

        @block.sync
        def _(sp):
            for s in ahead:
                sp.sem_inc(s.sem, s.start)
            for dst, src in loads:
                sp.dma_start(dst, src).then_inc(consts_in, 16)
            with sp.Fori(0, PRE_CHUNKS // 2) as c:
                for k in range(2):
                    sp.wait_ge(pre_used, c * 2 + k + 1)
                    sp.dma_start(px[:, k], x_chunk[bass.ds(c * 2 + k, 1)].rearrange("o p n d -> p (o n) d")).then_inc(pre_in[k], 16)

            def stack(layer, s, run):
                sp.wait_ge(stacked[layer].sem, stacked[layer].at(s, 0))
                apart(sp)
                sp.wait_ge(parts_ready[layer].sem, parts_ready[layer].at(s))
                apart(sp)
                for side, cols in enumerate((slice(0, T), slice(T, 2 * T))):
                    for part in range(3):
                        slots = [n for n, pair in enumerate(SLOTS) if pair[side] == part]
                        step = slots[1] - slots[0]
                        sp.dma_start(scr[layer, side, :, slots[0]:slots[-1] + 1:step, :],
                                     bc(parts[:, part:part + 1, cols], [P, len(slots), T])).then_inc(scr_written[layer].sem, 16)
                sp.wait_ge(scr_written[layer].sem, scr_written[layer].at(s))
                apart(sp)
                if layer == 0 and run.middle is not None:
                    unit(run, f"exp{UNITS - 1}").wait_full(sp)
                    apart(sp)
                if layer == 1 and run.last is not None:
                    unit(run, f"cosh{UNITS - 1}").wait_full(sp)
                    apart(sp)
                half = P // 2
                for e in range(2):
                    sp.dma_start(q_st[layer][e * half:(e + 1) * half, :, e, :],
                                 scr[layer, 0].rearrange("(p e d) s t -> e (d s) p t", e=2, d=HD)[e]).then_inc(stacked[layer].sem, 16)
                sp.dma_start(k_st[layer][:], scr[layer, 1].rearrange("(p r) s t -> (r s) p t", p=HP)).then_inc(stacked[layer].sem, 16)

            def load_x(i):
                sp.dma_start(x[:], x_seq[bass.ds(i, 1)].rearrange("o p k d -> p (o k) d")).then_inc(x_in.sem, 16)

            def iteration(run):
                f, m, o = run.first, run.middle, run.out
                if f:
                    stack(0, f, run)
                    if run.phase.trips > 1 or run.t + 1 < NB:
                        sp.wait_ge(xn_ready.sem, xn_ready.at(f))
                        apart(sp)
                        sp.wait_ge(xres_ready.sem, xres_ready.at(f))
                        apart(sp)
                        load_x(f.index() + 1)
                if o:
                    misc(run, "yffn").wait_drained(sp)
                    apart(sp)
                    sp.dma_start(out_seq[bass.ds(o.index(), 1)].rearrange("o p k d -> p (o k) d"), xold[:]).then_inc(out_done.sem, 16)
                if m:
                    stack(1, m, run)

            sp.wait_ge(zeros_set, 2)
            load_x(0)
            phases(sp, iteration)
            sp.wait_ge(out_done.sem, out_done.at(Sequence(NB - 1, 0)))

        @block.vector
        def _(dve):
            V = nc.vector
            n_pre = [0]

            def pre(ins):
                n_pre[0] += 1
                ins.then_inc(pre_link, 1)
                dve.wait_ge(pre_link, n_pre[0])

            dve.sem_inc(pre_used, 2)
            V.memset(mhalf[:], -0.5)
            V.memset(minus1[:], -1.0)
            V.memset(ksign[:].rearrange("p (k s h) -> p k s h", k=BLK, s=2)[:, :, 0, :], 1.0)
            V.memset(ksign[:].rearrange("p (k s h) -> p k s h", k=BLK, s=2)[:, :, 1, :], -1.0)
            for n in range(2):
                V.memset(q_st[n][:], 0.0)
                V.memset(nmax2[n][:], 0.0)
                last = V.memset(v_st[n][:], 0.0)
            last.then_inc(zeros_set, 1)
            dve.wait_ge(zeros_set, 1)
            for n in range(2):
                last = V.memset(v_st[n][:, :, :, HD:HD + 1], 1.0)
            last.then_inc(zeros_set, 1)
            dve.wait_ge(consts_in, 16 * len(loads))
            V.tensor_reduce(out=wcol[:], in_=w_tern, axis=AX_X, op=ALU.add, apply_absolute_value=True).then_inc(cols_ready, 1)
            V.tensor_tensor(w3t[:], w3t[:], bc(s3.unsqueeze(1), [P, HC, D]), ALU.mult)

            PRE_LINKS = 16
            with dve.Fori(0, PRE_CHUNKS // 2) as c:
                links = 0

                def link(ins, after=None):
                    nonlocal links
                    links += 1
                    ins.then_inc(pre_link, 1)
                    dve.wait_ge(pre_link, c * PRE_LINKS + links)
                    if after:
                        after(dve)

                for k in range(2):
                    dve.wait_ge(pre_in[k], c * 16 + 16)

                    def norm(dst, src, eps, step):
                        for n in range(PRE):
                            last = V.bn_stats(pst[:, n, :], src[:, n, :])
                        link(last, apart)
                        for n in range(PRE):
                            last = V.bn_aggr(pmv[:, n, :], pst[:, n, :])
                        link(last)
                        V.tensor_scalar(pve[:], pmv[:, :, 1], eps, None, ALU.add).then_inc(pre_var, 1)
                        dve.wait_ge(pre_rstd, c * 4 + 2 * k + step)
                        for n in range(PRE):
                            last = V.tensor_scalar(dst[:, n, :], src[:, n, :], pmv[:, n, 0:1], prs[:, n:n + 1], ALU.subtract, ALU.mult)
                        return last

                    ins = norm(pn, px[:, k], LN_EPS, 1)
                    ins.then_inc(pre_used, 1)
                    dve.wait_ge(pre_used, c * 2 + k + 3)
                    link(norm(pf, pn, FFN_LN_EPS, 2))
                    link(V.tensor_tensor(pf, pf, bc(gam_row.unsqueeze(1), [P, PRE, D]), ALU.mult))
                    link(V.tensor_tensor(pf, pf, bc(bet_row.unsqueeze(1), [P, PRE, D]), ALU.add))
                    link(V.tensor_reduce(out=pmax[:, bass.ds(c * 2 + k, 1)], in_=pf.rearrange("p n d -> p (n d)"), axis=AX_X, op=ALU.max,
                                         apply_absolute_value=True))
                assert links == PRE_LINKS, links
            n_pre[0] = PRE_LINKS * (PRE_CHUNKS // 2)
            V.tensor_reduce(out=gcol[:], in_=pmax[:], axis=AX_X, op=ALU.max).then_inc(cols_ready, 1)
            dve.wait_ge(all_ready, 2)
            lim = float(np.float32(QB - FFN_EPS)) / QB
            V.tensor_scalar(thr[:], gall[:], lim, None, ALU.mult)
            V.tensor_scalar(nthr[:], gall[:], -lim, None, ALU.mult)
            pre(V.tensor_scalar(beta[:], wall[:], 1.0 / (D * D), None, ALU.mult))
            pre(V.tensor_scalar(rbeta[:], beta[:], FFN_EPS, None, ALU.add))
            pre(V.reciprocal(rbeta[:], rbeta[:]))
            pre(V.tensor_scalar(wn, w_tern, rbeta[:], None, ALU.mult))
            pre(V.tensor_scalar(wr, wn, 4.0, -4.0, ALU.min, ALU.max))
            magic = 1.5 * 2.0 ** 23
            pre(V.tensor_scalar(wr, wr, magic, None, ALU.add))
            pre(V.tensor_scalar(wr, wr, -magic, None, ALU.add))
            pre(V.tensor_scalar(wr, wr, 1.0, -1.0, ALU.min, ALU.max))
            V.tensor_scalar(w_qs[:], wr, beta[:], None, ALU.mult).then_inc(weights_ready, 1)

            def moments(dst_st, dst_mv, dst_ve, src, eps, ready, link):
                for k in range(BLK):
                    last = V.bn_stats(dst_st[:, k, :], src[:, k, :])
                link(last, apart)
                for k in range(BLK):
                    last = V.bn_aggr(dst_mv[:, k, :], dst_st[:, k, :])
                link(last)
                V.tensor_scalar(dst_ve[:], dst_mv[:, :, 1], eps, None, ALU.add).then_inc(ready.sem, 1)

            def normed(dst, src, mvs, rstd, ready, s):
                dve.wait_ge(ready.sem, ready.at(s))
                for k in range(BLK):
                    last = V.tensor_scalar(dst[:, k, :], src[:, k, :], mvs[:, k, 0:1], rstd[:, k:k + 1], ALU.subtract, ALU.mult)
                return last

            def split(layer, s, link):
                dve.wait_ge(hi_ready[layer].sem, hi_ready[layer].at(s))
                link(V.tensor_tensor(resid[:], qk_t[:], parts[:, 0, :], ALU.subtract))
                link(V.tensor_copy(parts[:, 1, :], resid[:]))
                V.tensor_tensor(parts[:, 2, :], resid[:], parts[:, 1, :], ALU.subtract).then_inc(parts_ready[layer].sem, 1)

            def head_norm(layer, use, dst, link, extra=None):
                use.wait_full(dve)
                t = use.ap.rearrange("p (n c) -> p n c", c=32)
                total, rec = rsum, rrec
                link(V.tensor_scalar(total[:].unsqueeze(2), t[:, :, HD:HD + 1], 0.5, None, ALU.max))
                link(V.reciprocal(rec[:], total[:]))
                if extra is not None:
                    r3 = rec[:].rearrange("p (k h) -> p k h", k=BLK)
                    link(V.tensor_tensor(r3, r3, bc(extra[:].unsqueeze(2), [P, BLK, H]), ALU.mult))
                V.tensor_tensor(dst[:].rearrange("p k (h d) -> p (k h) d", d=HD), t[:, :, 0:HD],
                                bc(rec[:].unsqueeze(2), [P, BLK * H, HD]), ALU.mult).then_inc(use.free, 1)

            def heads_reduced(u, n, blocks, op, negate):
                heads, width = (8, P) if n < 2 else (4, T)
                h = 8 * n if n < 2 else 4 * (n - 2)
                dst = blocks[0 if n < 2 else 1][:, h:h + heads]
                u.wait_full(dve)
                V.tensor_reduce(out=dst, in_=u.ap.rearrange("p (h k) -> p h k", k=width), axis=AX_X, op=op, negate=negate).then_inc(u.free, 1)

            def clip_input(f):
                V.tensor_scalar(xq_t[:], xa_t[:], thr[:], nthr[:], ALU.min, ALU.max).then_inc(xq_ready.sem, 1)

            def pool_tokens(run, f, link):
                misc(run, "xT").wait_drained(dve)
                link(V.tensor_reduce(out=pooled[:, 0, :], in_=xn_t[:].rearrange("p (l c) -> p l c", c=POOL), axis=AX_X, op=ALU.add))
                V.tensor_copy(pooled[:, 1, :], pooled[:, 0, :]).then_inc(pooled_ready.sem, 1)

            def latent_projections(run, f):
                u = misc(run, "rqkv")
                u.wait_full(dve)
                V.tensor_scalar(rq_t[:], u.ap[0:LD, 0:T], b_rq[:], None, ALU.add).then_inc(rq_ready.sem, 1)
                V.tensor_scalar(rk_t[:], u.ap[0:LD, T:T + NLAT], 1.0 / POOL, b_rk[:], ALU.mult, ALU.add)
                last = V.scalar_tensor_tensor(rv[:], u.ap[:, T + NLAT:T + NLAT + LD], 1.0 / POOL, b_rv[:], ALU.mult, ALU.add)
                last.then_inc(u.free, 1)
                u.wait_drained(dve)
                V.tensor_tensor(rk_m[:], bc(rk_t[:].unsqueeze(1), [LD, LH, NLAT]), bc(lat_rows[:].unsqueeze(2), [LD, LH, NLAT]), ALU.mult).then_inc(rk_ready.sem, 1)
                V.tensor_tensor(rv_st[:, :, 0:LD], bc(rv[:].unsqueeze(1), [P, LH // 2, LD]), lat_cols[:], ALU.mult).then_inc(rv_ready.sem, 1)

            def values0(run, f):
                u = misc(run, "v")
                u.wait_full(dve)
                V.tensor_tensor(v_st[0][:, :, :, 0:HD], u.ap[:, 0:T].rearrange("p (k h d) -> p k h d", k=BLK, d=HD),
                                bc(b_v0[:].rearrange("p (h d) -> p h d", d=HD).unsqueeze(1), [P, BLK, H, HD]), ALU.add).then_inc(u.free, 1)

            def latent_maxima(run, m, link):
                u = misc(run, "lmax")
                u.wait_full(dve)
                V.tensor_reduce(out=nmax[0][:, :, H:NM], in_=u.ap.rearrange("p (k h l) -> p k h l", k=BLK, l=NLAT), axis=AX_X, op=ALU.max,
                                negate=True).then_inc(u.free, 1)
                u.wait_drained(dve)
                link(V.tensor_copy(nmax2[0][:, :, 0:NM], nmax[0][:]))
                V.tensor_tensor(nmax2[0][:, :, MLO:MLO + NM], nmax[0][:], nmax2[0][:, :, 0:NM], ALU.subtract).then_inc(nmax_ready[0].sem, 1)

            def latent_out(run):
                u = misc(run, "lo")
                u.wait_full(dve)
                V.tensor_copy(lo_t[:], u.ap[0:2 * LD, 0:T]).then_inc(u.free, 1)

            def latent_norm(run, link):
                u = misc(run, "loT")
                u.wait_full(dve)
                t = u.ap[:, 0:2 * 2 * LD].rearrange("p (k c) -> p k c", k=BLK)
                link(V.tensor_scalar(lsum[:], t[:, :, LD:LD + LH], 0.5, None, ALU.max))
                link(V.reciprocal(lrec[:], lsum[:]))
                V.tensor_tensor(lat[:].rearrange("p k (h d) -> p k h d", h=LH), t[:, :, 0:LD].rearrange("p k (h d) -> p k h d", h=LH),
                                bc(lrec[:].unsqueeze(3), [P, BLK, LH, LD // LH]), ALU.mult).then_inc(u.free, 1)

            def remote_bias(run):
                u = misc(run, "rem")
                u.wait_full(dve)
                V.tensor_tensor(remote[:], u.ap[:, 0:T].rearrange("p (k d) -> p k d", k=BLK), bc(b_rout[:].unsqueeze(1), [P, BLK, D]), ALU.add).then_inc(u.free, 1)

            def gate_logits(m):
                dve.wait_ge(gsum_ready.sem, gsum_ready.at(m))
                V.tensor_reduce(out=glog[:], in_=gl[:].rearrange("p k (h d) -> p (k h) d", d=HD), axis=AX_X, op=ALU.add).then_inc(glog_ready.sem, 1)

            def gate_sigmoid(m):
                dve.wait_ge(gexp_ready.sem, gexp_ready.at(m))
                V.tensor_scalar(gate[:], gexp[:], 0.5, 0.5, ALU.mult, ALU.add).then_inc(gate_ready.sem, 1)

            def layer0_out(run, m):
                u = misc(run, "y0")
                u.wait_full(dve)
                if run.last:
                    dve.wait_ge(x1res_ready.sem, x1res_ready.at(run.last))
                V.tensor_tensor(x1[:], u.ap[:, 0:T].rearrange("p (k d) -> p k d", k=BLK), xres[:], ALU.add).then_inc(u.free, 1)
                u.wait_drained(dve)

            def importance(m, link):
                dve.wait_ge(parts_ready[1].sem, parts_ready[1].at(m))
                link(V.tensor_tensor(xs1, xn1[:], bc(w_sur[:].unsqueeze(1), [P, BLK, D]), ALU.mult))
                link(V.tensor_reduce(out=imp[:], in_=xs1, axis=AX_X, op=ALU.add))
                V.tensor_scalar(imp[:], imp[:], b_sur[:], None, ALU.add).then_inc(imp_ready.sem, 1)

            def projections1(run, m, link):
                if run.last:
                    dve.wait_ge(v1_ready.sem, v1_ready.at(run.last))
                for k, name in enumerate(("qkv1a", "qkv1b")):
                    u = misc(run, name)
                    u.wait_full(dve)
                    V.tensor_tensor(v_new[:, k, :], u.ap[:, 2 * D:3 * D], b_v1[:], ALU.add)
                    V.tensor_tensor(u_qk[:, k, :], u.ap[:, 0:2 * D], b_qk1[:], ALU.add).then_inc(u.free, 1)
                u.wait_drained(dve)
                link(V.tensor_tensor(u_sq, u_qk[:], u_qk[:], ALU.mult))
                sq = u_sq.rearrange("p k (h d) -> p (k h) d", d=HD)
                link(V.tensor_reduce(out=mink[:], in_=sq[:, :, 1:HD], axis=AX_X, op=ALU.add))
                link(V.tensor_tensor(mink[:], mink[:], sq[:, :, 0], ALU.subtract))
                V.tensor_scalar(mink[:], mink[:], 1e-8, None, ALU.max).then_inc(mink_ready.sem, 1)

            def sinh_series(m, link):
                dve.wait_ge(mink_ready.sem, mink_ready.at(m))
                V.tensor_scalar(small[:].bitcast(I32), mink[:], 1.0, None, ALU.is_le)
                link(V.tensor_scalar(wsmall[:], mink[:], 1.0, None, ALU.min))
                link(V.tensor_scalar(poly[:], wsmall[:], 1.0 / 110, 1.0, ALU.mult, ALU.add))
                for d in (72, 42, 20, 6):
                    link(V.scalar_tensor_tensor(poly[:], poly[:], 1.0 / d, wsmall[:], ALU.mult, ALU.mult))
                    link(V.tensor_scalar(poly[:], poly[:], 1.0, None, ALU.add))

            def embedding(m, link):
                dve.wait_ge(exps_ready.sem, exps_ready.at(m))
                V.tensor_tensor(ctime[:], epos[:], eneg[:], ALU.add)
                link(V.tensor_tensor(sfac[:], epos[:], eneg[:], ALU.subtract))
                link(V.scalar_tensor_tensor(sfac[:], sfac[:], 0.5, rnom[:], ALU.mult, ALU.mult), apart)
                link(V.copy_predicated(sfac[:], small[:].bitcast(I32), poly[:]))
                link(V.tensor_tensor(sfac[:], sfac[:], ksign[:], ALU.mult))
                e3 = emb[:].rearrange("p k (h d) -> p (k h) d", d=HD)
                link(V.tensor_tensor(e3, u_qk[:].rearrange("p k (h d) -> p (k h) d", d=HD), bc(sfac[:].unsqueeze(2), [P, NV, HD]), ALU.mult))
                V.tensor_scalar(e3[:, :, 0:1], ctime[:].unsqueeze(2), 0.5, None, ALU.mult).then_inc(emb_ready.sem, 1)

            def spikes(l, link):
                dve.wait_ge(eimp_ready.sem, eimp_ready.at(l))
                link(V.tensor_scalar(eimp[:], eimp[:], 1.0, None, ALU.add))
                link(V.reciprocal(eimp[:], eimp[:]))
                V.tensor_scalar(spike[:], eimp[:], thresh[:], None, ALU.is_gt).then_inc(spike_ready.sem, 1)

            def silu_product(run, l, c):
                u = misc(run, f"f1_{c}")
                dve.wait_ge(sil_ready.sem, sil_ready.at(l, c + 1))
                V.scalar_tensor_tensor(hid1[:, c, :], u.ap[:, T:2 * T], s2[:, c:c + 1], hid1[:, c, :], ALU.mult, ALU.mult).then_inc(u.free, 1)

            def clamp_minima(run):
                unit(run, f"min{UNITS - 1}").wait_drained(dve)
                V.tensor_scalar(zmin[:], zmin[:], MIN_COSH, None, ALU.max).then_inc(zmin_ready.sem, 1)

            def clamp_cosh(run, n):
                u = unit(run, f"cosh{n}")
                u.wait_full(dve)
                V.tensor_scalar(zc[:, n * UNIT:(n + 1) * UNIT], u.ap, MIN_COSH, None, ALU.max).then_inc(u.free, 1)

            def sum_minima(l):
                dve.wait_ge(zsr_ready.sem, zsr_ready.at(l))
                V.tensor_tensor(zmin[:], zmin[:], zsr[:], ALU.add).then_inc(zsum_ready.sem, 1)

            def sum_cosh(l, n):
                c = slice(n * UNIT, (n + 1) * UNIT)
                dve.wait_ge(sqrt_done.sem, sqrt_done.at(l, n + 1))
                V.tensor_tensor(zc[:, c], zc[:, c], zs[:, c], ALU.add).then_inc(sum_done.sem, 1)

            def least_squares(l, link):
                dve.wait_ge(zln_ready.sem, zln_ready.at(l))
                z3 = zd[:].rearrange("p (k h) -> p k h", k=BLK)
                link(V.scalar_tensor_tensor(nmax[1][:], z3, -1.0, z3, ALU.mult, ALU.mult))
                link(V.tensor_copy(nmax2[1][:, :, 0:H], nmax[1][:]))
                V.tensor_tensor(nmax2[1][:, :, MLO:MLO + H], nmax[1][:], nmax2[1][:, :, 0:H], ALU.subtract).then_inc(nmax_ready[1].sem, 1)

            def shift(run, l, n):
                c = slice(n * UNIT, (n + 1) * UNIT)
                dve.wait_ge(sq_done[n % 2].sem, sq_done[n % 2].at(l, n // 2 + 1))
                u = unit(run, f"sub{n}")
                u.wait_full(dve)
                V.tensor_tensor(zc[:, c], zs[:, c], u.ap, ALU.add).then_inc(u.free, 1)

            def hidden(run, name, dst, g, a):
                u = misc(run, f"{name}_{a}")
                u.wait_full(dve)
                for c in range(2):
                    o = 2 * a + c
                    last = V.tensor_scalar(dst[:, o, :], u.ap[:, c * T:(c + 1) * T], g[:, o:o + 1], None, ALU.mult)
                last.then_inc(u.free, 1)

            def attention_out(run, e):
                u = misc(run, "y1")
                u.wait_full(dve)
                if run.out:
                    dve.wait_ge(xold_ready.sem, xold_ready.at(run.out))
                V.tensor_tensor(xatt[:], u.ap[:, 0:T].rearrange("p (k d) -> p k d", k=BLK), x1res[:], ALU.add).then_inc(u.free, 1)

            def output(run, o):
                u = misc(run, "yffn")
                dve.wait_ge(xold_ready.sem, xold_ready.at(o))
                u.wait_full(dve)
                V.tensor_tensor(xold[:], u.ap[:, 0:T].rearrange("p (k d) -> p k d", k=BLK), xold[:], ALU.add).then_inc(u.free, 1)

            def iteration(run):
                f, m, l, e, o = run.first, run.middle, run.last, run.end, run.out
                link = links_of(dve, dve_link, run)
                zblocks = [zmin[:, 0:H], zmin[:, H:2 * H]]
                nblocks = [nmax[0][:, 0, 0:H], nmax[0][:, 1, 0:H]]
                for n in range(UNITS):
                    if m:
                        heads_reduced(unit(run, f"max{n}"), n, nblocks, ALU.max, True)
                    if f and n == 1:
                        dve.wait_ge(x_in.sem, x_in.at(f))
                        moments(st, mv, ve, x, LN_EPS, var0, link[F])
                    if f and n == 3:
                        normed(xn, x, mv, rs, rstd0, f).then_inc(xn_ready.sem, 1)
                        dve.wait_ge(xn_ready.sem, xn_ready.at(f))
                        moments(st, mv, ve2, xn, FFN_LN_EPS, var0b, link[F])
                if m:
                    latent_maxima(run, m, link[M])
                if f:
                    normed(xf, xn, mv, rs2, rstd0b, f).then_inc(xf_ready.sem, 1)
                for n in range(UNITS):
                    if l:
                        heads_reduced(unit(run, f"min{n}"), n, zblocks, ALU.min, False)
                    if e and n == 1:
                        head_norm(1, avuse(run, "avT1"), y1, link[E], spike)
                if l:
                    clamp_minima(run)
                if e:
                    attention_out(run, e)
                if l:
                    spikes(l, link[L])
                if f:
                    pool_tokens(run, f, link[F])
                for n in range(UNITS):
                    if l:
                        clamp_cosh(run, n)
                    if m and n == 2:
                        latent_out(run)
                    if m and n == 4:
                        latent_norm(run, link[M])
                if f:
                    split(0, f, link[F])
                if m:
                    remote_bias(run)
                if l:
                    sum_minima(l)
                    for n in range(3):
                        sum_cosh(l, n)
                if e:
                    hidden(run, "f2", hid2, g1, 0)
                if l:
                    sum_cosh(l, 3)
                if m:
                    head_norm(0, avuse(run, "avT0"), local, link[M])
                if e:
                    hidden(run, "f2", hid2, g1, 1)
                if l:
                    sum_cosh(l, 4)
                if m:
                    gate_logits(m)
                if l:
                    sum_cosh(l, 5)
                    silu_product(run, l, 0)
                    silu_product(run, l, 1)
                if m:
                    gate_sigmoid(m)
                if l:
                    silu_product(run, l, 2)
                    silu_product(run, l, 3)
                if m:
                    layer0_out(run, m)
                    moments(st1, mv1, ve1, x1, LN_EPS, var1, link[M])
                if f:
                    misc(run, "xT").wait_drained(dve)
                    clip_input(f)
                    latent_projections(run, f)
                    values0(run, f)
                if l:
                    least_squares(l, link[L])
                if m:
                    normed(xn1, x1, mv1, rs1, rstd1, m).then_inc(xn1_ready.sem, 1)
                if l:
                    shift(run, l, 0)
                if m:
                    projections1(run, m, link[M])
                if l:
                    shift(run, l, 1)
                if m:
                    sinh_series(m, link[M])
                if l:
                    shift(run, l, 2)
                if m:
                    embedding(m, link[M])
                if o:
                    output(run, o)
                if l:
                    shift(run, l, 3)
                if e:
                    hidden(run, "f3", hid3, g2, 0)
                if m:
                    split(1, m, link[M])
                if l:
                    shift(run, l, 4)
                if e:
                    hidden(run, "f3", hid3, g2, 1)
                if l:
                    shift(run, l, 5)
                if m:
                    importance(m, link[M])
                for one in link.values():
                    one.end()

            phases(dve, iteration)

        @block.gpsimd
        def _(pool):
            G = nc.gpsimd
            RMAX, RADD = bass.bass_isa.ReduceOp.max, bass.bass_isa.ReduceOp.add
            pool.wait_ge(cols_ready, 1)
            G.partition_all_reduce(wall[:], wcol[:], P, RADD).then_inc(all_ready, 1)
            with pool.Fori(0, 2 * PRE_CHUNKS) as c:
                pool.wait_ge(pre_var, c + 1)
                G.tensor_tensor(prs[:], pve[:], mhalf[:, 0:PRE], ALU.pow).then_inc(pre_rstd, 1)
            pool.wait_ge(cols_ready, 2)
            G.partition_all_reduce(gall[:], gcol[:], P, RMAX).then_inc(all_ready, 1)

            d4 = lambda a: a[:].rearrange("p k (h d) -> p (k h) d", d=HD)

            def power(dst, src, var, done, s):
                pool.wait_ge(var.sem, var.at(s))
                G.tensor_tensor(dst[:], src[:], mhalf[:, 0:BLK], ALU.pow).then_inc(done.sem, 1)

            def window(run, n):
                unit(run, f"exp{n}").wait_drained(pool)
                apart(pool)
                c = prob0[:, n * UNIT:(n + 1) * UNIT]
                if n < 4:
                    t = c.rearrange("p (h q) -> p h q", q=T)
                    G.affine_select(out=t[:, :, 0:P], in_=t[:, :, 0:P], compare_op=ALU.is_gt, fill=0.0, base=0,
                                    pattern=[[0, 4], [1, P]], channel_multiplier=-1)
                    G.affine_select(out=t[:, :, P:T], in_=t[:, :, P:T], compare_op=ALU.is_ge, fill=0.0, base=0,
                                    pattern=[[0, 4], [-1, P]], channel_multiplier=1).then_inc(masked0.sem, 1)
                else:
                    t = c.rearrange("p (h q) -> p h q", q=P)
                    G.affine_select(out=t, in_=t, compare_op=ALU.is_gt, fill=0.0, base=0,
                                    pattern=[[0, 8], [1, P]], channel_multiplier=-1).then_inc(masked0.sem, 1)

            def window_edge(m):
                pool.wait_ge(masked0.sem, masked0.at(m, UNITS))
                apart(pool)
                edge = prob0[:, 0:H * T].rearrange("p (h q) -> p h q", q=T)[:, :, P:P + 1]
                G.affine_select(out=edge, in_=edge, compare_op=ALU.is_gt, fill=0.0, base=0, pattern=[[0, H], [0, 1]],
                                channel_multiplier=1).then_inc(masked0.sem, 1)

            def gate_products(run, link):
                misc(run, "rem").wait_drained(pool)
                G.tensor_tensor(d4(gr), d4(remote), bc(gate_r[:].unsqueeze(1), [P, BLK * H, HD]), ALU.mult)
                avuse(run, "avT0").wait_drained(pool)
                link(G.tensor_tensor(d4(gl), d4(local), bc(gate_l[:].unsqueeze(1), [P, BLK * H, HD]), ALU.mult))
                G.tensor_tensor(gl[:], gl[:], gr[:], ALU.add).then_inc(gsum_ready.sem, 1)

            def mix(m, link):
                pool.wait_ge(gate_ready.sem, gate_ready.at(m))
                link(G.tensor_tensor(gr[:], local[:], remote[:], ALU.subtract))
                link(G.tensor_tensor(d4(gr), d4(gr), bc(gate[:].unsqueeze(2), [P, BLK * H, HD]), ALU.mult))
                G.tensor_tensor(mixed[:], gr[:], remote[:], ALU.add).then_inc(mixed_ready.sem, 1)

            def square(l, n):
                c = slice(n * UNIT, (n + 1) * UNIT)
                pool.wait_ge(ln_done.sem, ln_done.at(l, n + 1))
                G.tensor_tensor(zs[:, c], zs[:, c], zs[:, c], ALU.mult).then_inc(sq_done[1].sem, 1)

            def square_cosh(run, l, n):
                c = slice(n * UNIT, (n + 1) * UNIT)
                unit(run, f"cosh{n}").wait_drained(pool)
                G.tensor_tensor(zs[:, c], zc[:, c], zc[:, c], ALU.mult).then_inc(squared[1].sem, 1)

            def causal(l, n):
                pool.wait_ge(exp1_done.sem, exp1_done.at(l, n + 1))
                apart(pool)
                c = prob1[:, n * UNIT:(n + 1) * UNIT]
                t = c.rearrange("p (h q) -> p h q", q=T)[:, :, 0:P] if n < 4 else c.rearrange("p (h q) -> p h q", q=P)
                G.affine_select(out=t, in_=t, compare_op=ALU.is_ge, fill=0.0, base=0, pattern=[[0, 4 if n < 4 else 8], [1, P]],
                                channel_multiplier=-1).then_inc(masked1.sem, 1)

            def iteration(run):
                f, m, l, e, o = run.first, run.middle, run.last, run.end, run.out
                link = links_of(pool, pool_link, run)
                if o:
                    pool.wait_ge(out_done.sem, out_done.at(o, 0))
                    apart(pool)
                    G.tensor_copy(xold[:], xatt[:]).then_inc(xold_ready.sem, 1)
                if f:
                    power(rs, ve, var0, rstd0, f)
                    power(rs2, ve2, var0b, rstd0b, f)
                if l:
                    if e:
                        avuse(run, "av1").wait_full(pool)
                    apart(pool)
                    G.tensor_copy(v_st[1][:, :, :, 0:HD], v_new[:].rearrange("p k (h d) -> p k h d", d=HD)).then_inc(v1_ready.sem, 1)
                    if e:
                        misc(run, "y1").wait_drained(pool)
                    G.tensor_tensor(x1res[:], x1[:], bc(b_out1[:].unsqueeze(1), [P, BLK, D]), ALU.add).then_inc(x1res_ready.sem, 1)
                for n in range(UNITS):
                    if m:
                        window(run, n)
                    if l and n in SQUARED_BY_POOL:
                        square_cosh(run, l, n)
                if m:
                    window_edge(m)
                    gate_products(run, link[M])
                    mix(m, link[M])
                if m:
                    power(rs1, ve1, var1, rstd1, m)
                if f:
                    if m:
                        misc(run, "y0").wait_drained(pool)
                    pool.wait_ge(x_in.sem, x_in.at(f))
                    G.tensor_tensor(xres[:], x[:], bc(b_out0[:].unsqueeze(1), [P, BLK, D]), ALU.add).then_inc(xres_ready.sem, 1)
                if l:
                    square(l, 1)
                    square(l, 3)
                    causal(l, 0)
                    square(l, 5)
                    for n in range(1, UNITS):
                        causal(l, n)
                for one in link.values():
                    one.end()

            phases(pool, iteration)

        @block.scalar
        def _(act):
            S = nc.scalar
            act.wait_ge(weights_ready, 1)
            LOG_EXP, SILU = "natural_log_exp_and_others", "silu_and_others"

            def transposes0(run, f):
                u = misc(run, "xT")
                u.wait_full(act)
                S.activation(xn_t[:], u.ap[:, 0:T], ACT.Copy)
                act.wait_ge(xq_ready.sem, xq_ready.at(f, 0))
                S.activation(xa_t[:], u.ap[:, T:2 * T], ACT.Identity, bias=bet_col[:], scale=gam_col[:]).then_inc(u.free, 1)

            def hi_part(layer, other, s):
                if other:
                    act.wait_ge(scr_written[1 - layer].sem, scr_written[1 - layer].at(other))
                S.activation(parts[:, 0, :], qk_t[:], ACT.Copy).then_inc(hi_ready[layer].sem, 1)

            def operands0(run, f):
                u = misc(run, "qk")
                u.wait_full(act)
                if run.last:
                    act.wait_ge(parts_ready[1].sem, parts_ready[1].at(run.last))
                S.activation(qk_t[:, 0:T], u.ap[:, 0:T], ACT.Identity, bias=b_qk0[:, 0:1])
                S.activation(qk_t[:, T:2 * T], u.ap[:, T:2 * T], ACT.Identity, bias=b_qk0[:, 1:2]).then_inc(u.free, 1)
                u.wait_drained(act)
                hi_part(0, run.last, f)

            def copied(u, dst, src):
                u.wait_full(act)
                S.activation(dst, src, ACT.Copy).then_inc(u.free, 1)

            def latent_weights(run):
                u = misc(run, "lexp")
                u.wait_full(act)
                S.activation(prob_l[:].rearrange("p a q -> p (a q)"), u.ap, ACT.Exp, scale=SCALE).then_inc(u.free, 1)

            def weights0(run, n):
                u = unit(run, f"exp{n}")
                u.wait_full(act)
                S.activation(prob0[:, n * UNIT:(n + 1) * UNIT], u.ap, ACT.Exp, scale=SCALE).then_inc(u.free, 1)

            def gate_tanh(m):
                act.wait_ge(glog_ready.sem, glog_ready.at(m))
                S.activation(gexp[:], glog[:], ACT.Tanh, scale=0.5).then_inc(gexp_ready.sem, 1)

            def importance_exp(run, m):
                if run.last:
                    act.wait_ge(spike_ready.sem, spike_ready.at(run.last))
                act.wait_ge(imp_ready.sem, imp_ready.at(m))
                S.activation(eimp[:], imp[:], ACT.Exp, scale=-1.0).then_inc(eimp_ready.sem, 1)

            def norm_exps(m, link):
                act.wait_ge(mink_ready.sem, mink_ready.at(m))
                link(S.activation(lnw[:], mink[:], ACT.Ln))
                S.activation(rnom[:], lnw[:], ACT.Exp, scale=-0.5)
                link(S.activation(nom[:], lnw[:], ACT.Exp, scale=0.5))
                S.activation(epos[:], nom[:], ACT.Exp)
                S.activation(eneg[:], nom[:], ACT.Exp, scale=-1.0).then_inc(exps_ready.sem, 1)

            def operands1(run, m):
                u = misc(run, "embT")
                u.wait_full(act)
                if run.first:
                    act.wait_ge(parts_ready[0].sem, parts_ready[0].at(run.first))
                S.activation(qk_t[:], u.ap, ACT.Copy).then_inc(u.free, 1)
                u.wait_drained(act)
                hi_part(1, run.first, m)

            def silu(run, l, c):
                u = misc(run, f"f1_{c}")
                u.wait_full(act)
                S.activation(hid1[:, c, :], u.ap[:, 0:T], ACT.Silu, scale=s1[:, c:c + 1]).then_inc(sil_ready.sem, 1)

            def gelu(layer, done):
                flat = layer[:].rearrange("p c t -> p (c t)")
                S.activation(flat, flat, ACT.Gelu).then_inc(done.sem, 1)

            def square_cosh(run, n):
                c = slice(n * UNIT, (n + 1) * UNIT)
                unit(run, f"cosh{n}").wait_drained(act)
                S.activation(zs[:, c], zc[:, c], ACT.Square).then_inc(squared[0].sem, 1)

            def minima_root(l, link):
                act.wait_ge(zmin_ready.sem, zmin_ready.at(l))
                link(S.activation(zsq[:], zmin[:], ACT.Square))
                S.activation(zsr[:], zsq[:], ACT.Sqrt, bias=minus1[:]).then_inc(zsr_ready.sem, 1)

            def root(l, n):
                c = slice(n * UNIT, (n + 1) * UNIT)
                by_pool = n in SQUARED_BY_POOL
                earlier = sum((k in SQUARED_BY_POOL) == by_pool for k in range(n + 1))
                act.wait_ge(squared[by_pool].sem, squared[by_pool].at(l, earlier))
                S.activation(zs[:, c], zs[:, c], ACT.Sqrt, bias=minus1[:]).then_inc(sqrt_done.sem, 1)

            def minima_log(l):
                act.wait_ge(zsum_ready.sem, zsum_ready.at(l))
                S.activation(zd[:], zmin[:], ACT.Ln).then_inc(zln_ready.sem, 1)

            def log(l, n):
                c = slice(n * UNIT, (n + 1) * UNIT)
                act.wait_ge(sum_done.sem, sum_done.at(l, n + 1))
                S.activation(zs[:, c], zc[:, c], ACT.Ln).then_inc(ln_done.sem, 1)

            def square_log(l, n):
                c = slice(n * UNIT, (n + 1) * UNIT)
                act.wait_ge(ln_done.sem, ln_done.at(l, n + 1))
                S.activation(zs[:, c], zs[:, c], ACT.Square).then_inc(sq_done[0].sem, 1)

            def weights1(run, n):
                c = slice(n * UNIT, (n + 1) * UNIT)
                unit(run, f"sub{n}").wait_drained(act)
                S.activation(prob1[:, c], zc[:, c], ACT.Exp, scale=-SCALE).then_inc(exp1_done.sem, 1)

            def iteration(run):
                f, m, l, e, o = run.first, run.middle, run.last, run.end, run.out
                link = links_of(act, act_link, run)
                if e:
                    copied(avuse(run, "av1"), o_t[:].rearrange("p v t -> p (v t)"), pav[:, :])
                if m:
                    u = misc(run, "mT")
                    copied(u, m_t[0][:], u.ap.bitcast(BF16)[:, 0:T])
                if f:
                    transposes0(run, f)
                if e:
                    u = misc(run, "yT")
                    copied(u, out_t[:], u.ap[:, 0:T])
                if f:
                    operands0(run, f)
                S.preload_act_table_set(LOG_EXP)
                if m:
                    latent_weights(run)
                for n in range(UNITS + 1):
                    if m and n < UNITS:
                        weights0(run, n)
                    if m and n == UNITS:
                        u = misc(run, "latT")
                        copied(u, lat_t[:], u.ap[0:LD, 0:T])
                    if l and n and n - 1 not in SQUARED_BY_POOL:
                        square_cosh(run, n - 1)
                if l:
                    minima_root(l, link[L])
                    for n in range(4):
                        root(l, n)
                if m:
                    copied(avuse(run, "av0"), o_t[:].rearrange("p v t -> p (v t)"), pav[:, :])
                if l:
                    root(l, 4)
                    root(l, 5)
                S.preload_act_table_set(SILU)
                if l:
                    silu(run, l, 0)
                    silu(run, l, 1)
                if m:
                    gate_tanh(m)
                if l:
                    silu(run, l, 2)
                    silu(run, l, 3)
                if m:
                    u = misc(run, "mixT")
                    copied(u, out_t[:], u.ap[:, 0:T])
                if o:
                    misc(run.before(), "f3_0").wait_drained(act)
                    misc(run.before(), "f3_1").wait_drained(act)
                    gelu(hid3, hid3_ready)
                if e:
                    misc(run, "f2_0").wait_drained(act)
                    misc(run, "f2_1").wait_drained(act)
                    gelu(hid2, hid2_ready)
                S.preload_act_table_set(LOG_EXP)
                if l:
                    minima_log(l)
                    log(l, 0)
                    square_log(l, 0)
                    u = misc(run, "mT1")
                    copied(u, m_t[1][:], u.ap.bitcast(BF16)[:, 0:T])
                if m:
                    u = misc(run, "x1T")
                    copied(u, xn1_t[:], u.ap[:, 0:T])
                if l:
                    log(l, 1)
                    log(l, 2)
                    square_log(l, 2)
                    weights1(run, 0)
                    log(l, 3)
                if m:
                    norm_exps(m, link[M])
                if l:
                    weights1(run, 1)
                    log(l, 4)
                    square_log(l, 4)
                    log(l, 5)
                    weights1(run, 2)
                if m:
                    operands1(run, m)
                if l:
                    for n in range(3, UNITS):
                        weights1(run, n)
                if m:
                    importance_exp(run, m)
                for one in link.values():
                    one.end()

            phases(act, iteration)

        @block.tensor
        def _(pe):
            PE = nc.tensor
            pe.wait_ge(weights_ready, 1)

            def scores_by_query(u, layer, n, masks):
                u.wait_free(pe)
                per = 4 if n < 2 else 2
                width = BANK // per
                q = slice(0, P) if n < 2 else slice(P, T)
                for b in range(2):
                    bank = u.ap[:, b * BANK:(b + 1) * BANK]
                    for s in range(per):
                        h = (8 * n if n < 2 else 4 * (n - 2)) + per * b + s
                        PE.matmul(bank[:, s * width:(s + 1) * width], q_st[layer][:, h // 2, h % 2, q], k_st[layer][:, h // 2, 0:width],
                                  start=(s == 0), stop=False)
                    mask = masks[0 if n < 2 else 1]
                    wide = mask.shape[1]
                    for o in range(0, BANK, wide):
                        last = PE.matmul(bank[:, o:o + wide], ident_bf[:], mask[:], start=False, stop=(o + wide == BANK))
                last.then_inc(u.full, 1)

            def scores_by_key(u, layer, n, scores, shifts):
                u.wait_free(pe)
                for b in range(2):
                    if n < 4:
                        pairs, keys, queries, width = [2 * n + b], slice(0, P), slice(0, T), 2 * T
                    else:
                        pairs, keys, queries, width = [4 * (n - 4) + 2 * b, 4 * (n - 4) + 2 * b + 1], slice(P, T), slice(P, T), 2 * P
                    products = []
                    for s, hp in enumerate(pairs):
                        o, w = b * BANK + s * width, width // 2
                        if scores:
                            products.append((u.ap[:, o:o + width], k_st[layer][:, hp, keys], q_st[layer][:, hp, :, queries]))
                        if shifts:
                            products += [(u.ap[:, o + e * w:o + (e + 1) * w], sel[:, 2 * hp + e, :], m_t[layer][:, queries]) for e in range(2)]
                    for k, (dst, a, b_) in enumerate(products):
                        last = PE.matmul(dst, a, b_, start=(k == 0), stop=(k == len(products) - 1))
                last.then_inc(u.full, 1)

            def attend(use, layer, prob, groups=range(4)):
                if 0 in groups:
                    use.wait_free(pe)
                for v in groups:
                    for g in range(4):
                        h = 4 * v + g
                        PE.matmul(use.ap[32 * g:32 * g + 32, v * T:(v + 1) * T], v_st[layer][:, 0, h, :], prob[:, h * T:(h + 1) * T], start=True, stop=False)
                    for g in range(4):
                        h = 4 * v + g
                        last = PE.matmul(use.ap[32 * g:32 * g + 32, v * T + P:(v + 1) * T], v_st[layer][:, 1, h, :],
                                         prob[:, H * T + h * P:H * T + (h + 1) * P], start=False, stop=True)
                if 3 in groups:
                    last.then_inc(use.full, 1)

            def attended_t(use_t, layer):
                use_t.wait_free(pe)
                for k in range(BLK):
                    for v in range(4):
                        last = PE.transpose(use_t.ap[:, k * BANK + v * P:k * BANK + (v + 1) * P], o_t[:, v, k * P:(k + 1) * P], ident[:])
                last.then_inc(use_t.full, 1)

            def transposed(u, srcs):
                u.wait_free(pe)
                for n, src in enumerate(srcs):
                    last = PE.transpose(u.ap[:, n * P:(n + 1) * P], src, ident[:])
                last.then_inc(u.full, 1)

            def maxima_t(u, layer, s):
                pe.wait_ge(nmax_ready[layer].sem, nmax_ready[layer].at(s))
                u.wait_free(pe)
                for k in range(BLK):
                    last = PE.transpose(u.ap.bitcast(BF16)[:, k * P:(k + 1) * P], nmax2[layer][:, k, :], ident_bf[:])
                last.then_inc(u.full, 1)

            def project0(run):
                u = misc(run, "qk")
                misc(run, "xT").wait_drained(pe)
                u.wait_free(pe)
                PE.matmul(u.ap[:, 0:T], w_qkv0[:, 0:D], xn_t[:], start=True, stop=True)
                PE.matmul(u.ap[:, T:2 * T], w_qkv0[:, D:2 * D], xn_t[:], start=True, stop=True).then_inc(u.full, 1)

            def project_latent(run, f):
                u = misc(run, "rqkv")
                u.wait_free(pe)
                pe.wait_ge(pooled_ready.sem, pooled_ready.at(f))
                PE.matmul(u.ap[0:LD, 0:T], w_rq[:], xn_t[:], start=True, stop=True)
                PE.matmul(u.ap[0:LD, T:T + NLAT], w_rkv[:, 0:LD], pooled[:, 0, :], start=True, stop=True)
                PE.matmul(u.ap[:, T + NLAT:T + NLAT + LD], pooled[:].rearrange("p a l -> p (a l)"), w_rkv[:, LD:2 * LD], start=True, stop=True).then_inc(u.full, 1)

            def project_values0(run):
                u = misc(run, "v")
                u.wait_free(pe)
                for k in range(BLK):
                    last = PE.matmul(u.ap[:, k * P:(k + 1) * P], xn_t[:, k * P:(k + 1) * P], w_qkv0[:, 2 * D:3 * D], start=True, stop=True)
                last.then_inc(u.full, 1)

            def latent_scores(run, m):
                u = misc(run, "lmax")
                u.wait_free(pe)
                pe.wait_ge(rk_ready.sem, rk_ready.at(m))
                for k in range(BLK):
                    PE.matmul(u.ap[:, k * T:(k + 1) * T], rq_t[:, k * P:(k + 1) * P], rk_m[:].rearrange("p h l -> p (h l)"), start=(k == 0), stop=False)
                PE.matmul(u.ap, ident_bf[:], winl[:], start=False, stop=True).then_inc(u.full, 1)

            def latent_scores_t(run):
                u = misc(run, "lexp")
                misc(run, "mT").wait_drained(pe)
                u.wait_free(pe)
                for p in range(LH // 2):
                    PE.matmul(u.ap[:, p * T:(p + 1) * T], rk_m[:, 2 * p:2 * p + 2, :].rearrange("p h l -> p (h l)"), rq_t[:], start=(p == 0), stop=False)
                    PE.matmul(u.ap[:, p * T:(p + 1) * T], sel[:, H + p, :], m_t[0][:], start=False, stop=False)
                    last = PE.matmul(u.ap[:, p * T:(p + 1) * T], ident_bf[:], winl_t[:], start=False, stop=(p == LH // 2 - 1))
                last.then_inc(u.full, 1)

            def latent_attend(run, m):
                u = misc(run, "lo")
                u.wait_free(pe)
                misc(run, "lexp").wait_drained(pe)
                pe.wait_ge(rv_ready.sem, rv_ready.at(m))
                for p in range(LH // 2):
                    last = PE.matmul(u.ap[0:2 * LD, 0:T], rv_st[:, p, :], prob_l[:, p, :], start=(p == 0), stop=(p == LH // 2 - 1))
                last.then_inc(u.full, 1)

            def latent_tokens(run):
                misc(run, "lo").wait_drained(pe)
                u = misc(run, "loT")
                u.wait_free(pe)
                apart(pe)
                for k in range(BLK):
                    last = PE.transpose(u.ap[:, k * 2 * LD:(k + 1) * 2 * LD], lo_t[:, k * P:(k + 1) * P], ident[0:2 * LD, 0:2 * LD])
                last.then_inc(u.full, 1)

            def latent_back(run):
                misc(run, "loT").wait_drained(pe)
                u = misc(run, "latT")
                u.wait_free(pe)
                for k in range(BLK):
                    last = PE.transpose(u.ap[0:LD, k * P:(k + 1) * P], lat[:, k, :], ident[:])
                last.then_inc(u.full, 1)

            def latent_project(run):
                misc(run, "latT").wait_drained(pe)
                u = misc(run, "rem")
                u.wait_free(pe)
                for k in range(BLK):
                    last = PE.matmul(u.ap[:, k * D:(k + 1) * D], lat_t[:, k * P:(k + 1) * P], w_rout[:], start=True, stop=True)
                last.then_inc(u.full, 1)

            def layer0_out(run, m):
                pe.wait_ge(mixed_ready.sem, mixed_ready.at(m))
                transposed(misc(run, "mixT"), [mixed[:, 0, :], mixed[:, 1, :]])
                misc(run, "mixT").wait_drained(pe)
                u = misc(run, "y0")
                u.wait_free(pe)
                pe.wait_ge(xq_ready.sem, xq_ready.at(m))
                for k in range(BLK):
                    c = slice(k * P, (k + 1) * P)
                    PE.matmul(u.ap[:, c], out_t[:, c], w_out0[:], start=True, stop=False)
                    last = PE.matmul(u.ap[:, c], xq_t[:, c], w_qs[:], start=False, stop=True)
                last.then_inc(u.full, 1)

            def project1(run, m):
                pe.wait_ge(xn1_ready.sem, xn1_ready.at(m))
                transposed(misc(run, "x1T"), [xn1[:, 0, :], xn1[:, 1, :]])
                misc(run, "x1T").wait_drained(pe)
                for k, name in enumerate(("qkv1a", "qkv1b")):
                    u = misc(run, name)
                    u.wait_free(pe)
                    PE.matmul(u.ap[:, 0:3 * D], xn1_t[:, k * P:(k + 1) * P], w_qkv1[:], start=True, stop=True).then_inc(u.full, 1)

            def feed1(run, c):
                u = misc(run, f"f1_{c}")
                u.wait_free(pe)
                PE.matmul(u.ap[:, 0:T], w1t[:, c * P:(c + 1) * P], xn1_t[:], start=True, stop=True)
                PE.matmul(u.ap[:, T:2 * T], w2t[:, c * P:(c + 1) * P], xn1_t[:], start=True, stop=True).then_inc(u.full, 1)

            def feed(run, name, a, w, src):
                u = misc(run, f"{name}_{a}")
                u.wait_free(pe)
                for c in range(2):
                    o = 2 * a + c
                    for k in range(HC):
                        last = PE.matmul(u.ap[:, c * T:(c + 1) * T], w[:, k, o * P:(o + 1) * P], src[:, k, :], start=(k == 0), stop=(k == HC - 1))
                last.then_inc(u.full, 1)

            def feed_out(run):
                u = misc(run, "yffn")
                u.wait_free(pe)
                for k in range(BLK):
                    c = slice(k * P, (k + 1) * P)
                    for n in range(HC):
                        last = PE.matmul(u.ap[:, c], hid3[:, n, c], w3t[:, n, :], start=(n == 0), stop=(n == HC - 1))
                last.then_inc(u.full, 1)

            def outputs_t(run):
                avuse(run, "avT1").wait_drained(pe)
                transposed(misc(run, "yT"), [y1[:, 0, :], y1[:, 1, :]])

            def output(run):
                misc(run, "yT").wait_drained(pe)
                u = misc(run, "y1")
                u.wait_free(pe)
                for k in range(BLK):
                    c = slice(k * P, (k + 1) * P)
                    last = PE.matmul(u.ap[:, c], out_t[:, c], w_out1[:], start=True, stop=True)
                last.then_inc(u.full, 1)

            def iteration(run):
                f, m, l, e, o = run.first, run.middle, run.last, run.end, run.out
                maxima = lambda *units: [scores_by_query(unit(run, f"max{n}"), 0, n, (win0, win1)) for n in units if m]
                minima = lambda *units: [scores_by_query(unit(run, f"min{n}"), 1, n, (cau0, cau1)) for n in units if l]
                shifts = lambda *units: [scores_by_key(unit(run, f"sub{n}"), 1, n, False, True) for n in units if l]
                if m:
                    pe.wait_ge(stacked[0].sem, stacked[0].at(m))
                maxima(0, 1)
                if e:
                    pe.wait_ge(v1_ready.sem, v1_ready.at(e))
                    pe.wait_ge(masked1.sem, masked1.at(e))
                for v in range(4):
                    if e:
                        attend(avuse(run, "av1"), 1, prob1, [v])
                    maxima(v + 2)
                if m:
                    latent_scores(run, m)
                if e:
                    attended_t(avuse(run, "avT1"), 1)
                if l:
                    pe.wait_ge(stacked[1].sem, stacked[1].at(l))
                minima(0)
                if m:
                    maxima_t(misc(run, "mT"), 0, m)
                minima(1)
                if f:
                    pe.wait_ge(xf_ready.sem, xf_ready.at(f))
                    transposed(misc(run, "xT"), [xn[:, 0, :], xn[:, 1, :], xf[:, 0, :], xf[:, 1, :]])
                minima(2)
                if e:
                    outputs_t(run)
                minima(3)
                if f:
                    project0(run)
                minima(4)
                if e:
                    output(run)
                minima(5)
                if m:
                    latent_scores_t(run)
                for n in range(UNITS):
                    if m:
                        scores_by_key(unit(run, f"exp{n}"), 0, n, True, True)
                    if l:
                        scores_by_key(unit(run, f"cosh{n}"), 1, n, True, False)
                    if m and n == 1:
                        latent_attend(run, m)
                    if m and n == 3:
                        latent_tokens(run)
                    if m and n == 5:
                        latent_back(run)
                if m:
                    latent_project(run)
                if e:
                    misc(run.before(), "f1_2").wait_drained(pe)
                    misc(run.before(), "f1_3").wait_drained(pe)
                    feed(run, "f2", 0, h1t, hid1)
                if m:
                    pe.wait_ge(masked0.sem, masked0.at(m))
                    attend(avuse(run, "av0"), 0, prob0)
                if e:
                    feed(run, "f2", 1, h1t, hid1)
                if m:
                    attended_t(avuse(run, "avT0"), 0)
                if l:
                    for c in range(HC):
                        feed1(run, c)
                if m:
                    layer0_out(run, m)
                if f:
                    project_latent(run, f)
                    project_values0(run)
                if l:
                    maxima_t(misc(run, "mT1"), 1, l)
                    misc(run, "mT1").wait_drained(pe)
                shifts(0)
                if m:
                    project1(run, m)
                shifts(1, 2)
                if o:
                    pe.wait_ge(hid3_ready.sem, hid3_ready.at(o))
                    feed_out(run)
                shifts(3)
                if e:
                    pe.wait_ge(hid2_ready.sem, hid2_ready.at(e))
                    feed(run, "f3", 0, h2t, hid2)
                if m:
                    pe.wait_ge(emb_ready.sem, emb_ready.at(m))
                    transposed(misc(run, "embT"), [emb[:, 0, 0:D], emb[:, 1, 0:D], emb[:, 0, D:2 * D], emb[:, 1, D:2 * D]])
                shifts(4)
                if e:
                    feed(run, "f3", 1, h2t, hid2)
                shifts(5)

            phases(pe, iteration)


_IN = ["L0_attn_x", "L0_attn_qkv_w", "L0_attn_qkv_b", "L0_attn_rq_w", "L0_attn_rq_b", "L0_attn_rkv_w", "L0_attn_rkv_b", "L0_attn_rout_w",
       "L0_attn_rout_b", "L0_attn_out_w", "L0_attn_out_b", "L0_attn_gl_w", "L0_attn_gr_w", "L0_ffn_weight", "L0_ffn_ln_gamma",
       "L0_ffn_ln_beta", "L1_attn_W_qkv", "L1_attn_b_qkv", "L1_attn_W_out", "L1_attn_b_out", "L1_attn_w_sur", "L1_attn_b_sur",
       "L1_attn_threshold", "L1_ffn_w1_s", "L1_ffn_w2_s", "L1_ffn_h1_s", "L1_ffn_h2_s", "L1_ffn_w3_s"]
_COLUMNS = ("L1_ffn_w1_s", "L1_ffn_w2_s", "L1_ffn_h1_s", "L1_ffn_h2_s")
_TRANSPOSED = {"w1t": "L1_ffn_w1_w", "w2t": "L1_ffn_w2_w", "h1t": "L1_ffn_h1_w", "h2t": "L1_ffn_h2_w", "w3t": "L1_ffn_w3_w"}


def kernel(**inputs):
    import concourse.bacc as bacc
    from concourse.bass_utils import run_bass_kernel_spmd

    nc = bacc.Bacc("TRN2", target_bir_lowering=False, num_devices=1)
    arrays, A = {}, {}
    laid = {n: np.ascontiguousarray(inputs[n]).reshape(inputs[n].shape or (1,)) for n in _IN}
    laid |= {n: np.ascontiguousarray(np.asarray(inputs[src]).T) for n, src in _TRANSPOSED.items()}
    laid["b_qk0_cols"] = np.ascontiguousarray(np.asarray(inputs["L0_attn_qkv_b"])[:2 * D].reshape(2, P).T)
    laid |= {n + "_cols": np.ascontiguousarray(laid.pop(n).reshape(HC, P).T) for n in _IN if n in _COLUMNS}
    laid |= shape_constants()
    for name, a in laid.items():
        arrays[f"in_{name}"] = a
        A[name] = nc.dram_tensor(f"in_{name}", list(a.shape), mybir.dt.from_np(a.dtype), kind="ExternalInput").ap()
    out = nc.dram_tensor("out_0", [NB, T, D], F32, kind="ExternalOutput").ap()
    build(nc, A, out)
    r = run_bass_kernel_spmd(nc, [arrays], core_ids=[0])
    return r.results[0]["out_0"]
```

```python
from contextlib import ExitStack

import numpy as np

import concourse.bass as bass
from concourse import mybir

F32 = mybir.dt.float32
BF16 = mybir.dt.bfloat16
I32 = mybir.dt.int32
ALU = mybir.AluOpType
ACT = mybir.ActivationFunctionType
AX_X = mybir.AxisListType.X

P = 128
NB, T, D = 32, 256, 128
BLK = T // P
H, HD = 16, 8
HP = H // 2
NLAT, LH, LD = 64, 4, 32
POOL = T // NLAT
HID = 512
HC = HID // P
BANK = 512
SLOTS = [(0, 0), (0, 1), (0, 2), (1, 0), (1, 1), (1, 2), (2, 0), (2, 1)]
MLO = 32
NM = H + LH
BIG = 1e30
SCALE = float(1.0 / np.sqrt(HD))
LN_EPS, FFN_LN_EPS, FFN_EPS, QB = 1e-5, 1e-3, 1e-5, 128.0
MIN_COSH = float(np.float32(1.0 + 1e-7))
PRE = 16
PRE_CHUNKS = NB * T // (P * PRE)
SCOLS = H * T + H * P
UNIT = 2 * BANK
UNITS = SCOLS // UNIT


def shape_constants():
    bf = np.dtype("bfloat16")
    q, k = np.arange(P)[:, None], np.arange(P)[None, :]
    c = {}
    c["ident"] = np.eye(P, dtype=np.float32)
    c["ident_bf"] = np.eye(P, dtype=bf)
    own = (k < q)
    first = own | ((q == 0) & (k == 0))
    prev = (k >= q) & (k >= 1)
    neg = lambda ok: np.where(ok, 0.0, -BIG)
    c["win0"] = np.tile(neg(first), (1, 4)).astype(bf)
    c["win1"] = np.concatenate([neg(prev), neg(own)], 1).astype(bf)
    c["cau0"] = np.tile(-neg(k <= q), (1, 4)).astype(bf)
    lat = np.arange(NLAT)[None, :]
    blocks = []
    for b in range(BLK):
        chunk = (b * P + q) // POOL
        blocks.append(np.tile(neg((lat < chunk) | ((chunk == 0) & (lat == 0))), (1, LH)))
    c["winl"] = np.concatenate(blocks, 1).astype(bf)
    ok = (np.arange(P)[:, None] % NLAT) < np.arange(T)[None, :] // POOL
    c["winl_t"] = neg(ok).astype(bf)
    sel = np.zeros((P, H + LH // 2, P), np.float32)
    for h in range(H):
        sel[h, h, :] = 1
        sel[MLO + h, h, :] = 1
    for p in range(LH // 2):
        for e in range(2):
            sel[H + 2 * p + e, H + p, e * NLAT:(e + 1) * NLAT] = 1
            sel[MLO + H + 2 * p + e, H + p, e * NLAT:(e + 1) * NLAT] = 1
    c["sel"] = sel.astype(bf)
    rows = np.arange(P)[:, None, None] // NLAT
    heads = 2 * np.arange(LH // 2)[None, :, None] + rows
    c["lat_cols"] = (heads == (np.arange(LD) // (LD // LH))[None, None, :]).astype(np.float32)
    ones = np.zeros((P, LH // 2, 2 * LD), np.float32)
    ones[:, :, LD:LD + LH] = heads == np.arange(LH)[None, None, :]
    c["lat_ones"] = ones
    c["lat_rows"] = (np.arange(LD)[:, None] // (LD // LH) == np.arange(LH)[None, :]).astype(np.float32)
    return c


class Sequence:

    def __init__(self, t, lag):
        self.t, self.lag = t, lag

    def index(self):
        return self.t - self.lag


class Signal:

    def __init__(self, sem, per=1, step=1, start=0):
        self.sem, self.per, self.step, self.start = sem, per, step, start

    def at(self, s, n=None):
        n = self.per if n is None else n
        each = self.per * self.step
        return s.t * each + (n * self.step + self.start - s.lag * each)


class Phase:

    def __init__(self, t0, trips, stages):
        self.t0, self.trips, self.stages = t0, trips, stages


LAG = {"first": 0, "middle": 1, "last": 2, "end": 3, "out": 4}


def pipeline_phases():
    deepest = max(LAG.values())
    at_work = lambda t: tuple(n for n, lag in LAG.items() if 0 <= t - lag < NB)
    single = lambda t: Phase(t, 1, at_work(t))
    head, tail = range(deepest + 1), range(NB - 1, NB + deepest)
    return [single(t) for t in head] + [Phase(deepest + 1, NB - deepest - 2, tuple(LAG))] + [single(t) for t in tail]


PHASES = pipeline_phases()


class Run:

    def __init__(self, phase, t):
        self.phase, self.t = phase, t
        self.first, self.middle, self.last, self.end, self.out = (Sequence(t, LAG[n]) if n in phase.stages else None for n in LAG)

    def before(self):
        if self.phase.trips > 1:
            return Run(self.phase, self.t - 1)
        return next(Run(p, self.t - 1) for p in PHASES if p.t0 <= self.t - 1 < p.t0 + p.trips)


class Buffer:

    def __init__(self, ap, uses, full, free):
        self.ap, self.uses, self.full, self.free = ap, uses, full, free

    def use(self, run, name):
        before = 0
        for ph in PHASES:
            names = [n for stage, n in self.uses if stage in ph.stages]
            if ph is run.phase:
                break
            before += ph.trips * len(names)
        return Use(self, run.t * len(names) + (before + names.index(name) - run.phase.t0 * len(names)))


def nth(n, units):
    return sum((k in units) == (n in units) for k in range(n + 1))


class Use:

    def __init__(self, buffer, count):
        self.ap, self.full, self.free, self.count = buffer.ap, buffer.full, buffer.free, count

    def wait_free(self, pe):
        pe.wait_ge(self.free, self.count + 1)

    def wait_full(self, eng):
        eng.wait_ge(self.full, self.count + 1)

    def wait_drained(self, eng):
        eng.wait_ge(self.free, self.count + 2)


DVE_LINKS = {"first": 3, "middle": 29, "last": 3, "end": 6}


def bc(ap, shape):
    return ap.to_broadcast(list(shape))


def build(nc, A, out):
    ctx = ExitStack()
    with ctx:
        def sb(name, shape, dt=F32):
            return ctx.enter_context(nc.sbuf_tensor(name, list(shape), dt))

        def sem(name):
            return ctx.enter_context(nc.semaphore(name))

        ahead = []

        def sig(name, per=1, step=1, start=0):
            s = Signal(sem(name), per, step, start)
            if start:
                ahead.append(s)
            return s

        ident, ident_bf = sb("ident", [P, P]), sb("ident_bf", [P, P], BF16)
        win0, win1 = sb("win0", [P, BANK], BF16), sb("win1", [P, T], BF16)
        cau0 = sb("cau0", [P, BANK], BF16)
        winl, winl_t = sb("winl", [P, BANK], BF16), sb("winl_t", [P, T], BF16)
        sel = sb("sel", [P, H + LH // 2, P], BF16)
        lat_cols, lat_rows = sb("lat_cols", [P, LH // 2, LD]), sb("lat_rows", [LD, LH])
        w_qkv0, b_qk0, b_v0 = sb("w_qkv0", [P, 3 * D]), sb("b_qk0", [P, 2]), sb("b_v0", [P, D])
        w_rq, b_rq = sb("w_rq", [P, LD]), sb("b_rq", [LD, 1])
        w_rkv, b_rk, b_rv = sb("w_rkv", [P, 2 * LD]), sb("b_rk", [LD, 1]), sb("b_rv", [P, LD])
        w_rout, b_rout = sb("w_rout", [LD, D]), sb("b_rout", [P, D])
        w_out0, b_out0 = sb("w_out0", [P, D]), sb("b_out0", [P, D])
        gate_l, gate_r = sb("gate_l", [P, HD]), sb("gate_r", [P, HD])
        w_qs = sb("w_qs", [P, D])
        gam_col, bet_col = sb("gam_col", [P, 1]), sb("bet_col", [P, 1])
        w_qkv1, b_qk1, b_v1 = sb("w_qkv1", [P, 3 * D]), sb("b_qk1", [P, 2 * D]), sb("b_v1", [P, D])
        w_out1, b_out1 = sb("w_out1", [P, D]), sb("b_out1", [P, D])
        w_sur, b_sur, thresh = sb("w_sur", [P, D]), sb("b_sur", [P, 1]), sb("thresh", [P, 1])
        w1t, w2t = sb("w1t", [P, HID]), sb("w2t", [P, HID])
        h1t, h2t = sb("h1t", [P, HC, HID]), sb("h2t", [P, HC, HID])
        s1, s2, g1, g2 = (sb(n, [P, HC]) for n in ("s1", "s2", "g1", "g2"))
        w3t = sb("w3t", [P, HC, D])
        mhalf, zero = sb("mhalf", [P, 2 * PRE]), sb("zero", [P, 1])
        minus1 = sb("minus1", [P, 1])
        ksign = sb("ksign", [P, BLK * 2 * H])

        zc, zs = sb("zc", [P, SCOLS]), sb("zs", [P, SCOLS])
        prob0 = sb("prob0", [P, SCOLS])
        w_tern, wn, wr, gam_row, bet_row, s3 = (prob0[:, n * D:(n + 1) * D] for n in range(6))
        half = PRE_CHUNKS // 2
        px = [z[:, 0:half * PRE * D].rearrange("p (c n d) -> p c n d", c=half, d=D) for z in (zc, zs)]
        borrowed = 6 * D

        def borrow(chunk_shape):
            nonlocal borrowed
            size = PRE_CHUNKS * int(np.prod(chunk_shape))
            ap = prob0[:, borrowed:borrowed + size].rearrange("p (c k f) -> p k c f", c=half, k=2)
            borrowed += size
            return [ap[:, k].rearrange("p c (n f) -> p c n f", n=chunk_shape[0]) for k in range(2)]

        pst, pmv = [sb(f"pst{k}", [P, PRE, 6]) for k in range(2)], [sb(f"pmv{k}", [P, PRE, 2]) for k in range(2)]
        pve, prs = sb("pve", [P, PRE]), sb("prs", [P, PRE])
        pscale, pneg = borrow([1, PRE]), borrow([1, PRE])
        pmost, pleast = borrow([1, D]), borrow([1, D])
        pall = prob0[:, borrowed:borrowed + 2 * D].rearrange("p (e d) -> p e d", e=2)
        gcol, gall = sb("gcol", [P, 1]), sb("gall", [P, 1])
        thr, nthr = sb("thr", [P, 1]), sb("nthr", [P, 1])
        wcol, wall = sb("wcol", [P, 1]), sb("wall", [P, 1])
        beta, rbeta = sb("beta", [P, 1]), sb("rbeta", [P, 1])

        x = sb("x", [P, BLK, D])
        xres = sb("xres", [P, BLK, D])
        st, mv = sb("st", [P, BLK, 6]), sb("mv", [P, BLK, 2])
        ve, rs = sb("ve", [P, BLK]), sb("rs", [P, BLK])
        ve2, rs2 = sb("ve2", [P, BLK]), sb("rs2", [P, BLK])
        xn, xf = sb("xn", [P, BLK, D]), sb("xf", [P, BLK, D])
        xn_t, xa_t, xq_t = sb("xn_t", [P, T]), sb("xa_t", [P, T]), sb("xq_t", [P, T])
        pooled = sb("pooled", [P, 2, NLAT])
        qk_t, resid = sb("qk_t", [P, 2 * T]), sb("resid", [P, 2 * T])
        parts = sb("parts", [P, 3, 2 * T], BF16)
        q_st = [sb(f"q_st{n}", [P, HP, 2, T], BF16) for n in range(2)]
        k_st = [sb(f"k_st{n}", [P, HP, T], BF16) for n in range(2)]
        v_st = [sb(f"v_st{n}", [P, BLK, H, 32]) for n in range(2)]
        rq_t, rk_t, rk_m = sb("rq_t", [LD, T]), sb("rk_t", [LD, NLAT]), sb("rk_m", [LD, LH, NLAT])
        rv, rv_st = sb("rv", [P, LD]), sb("rv_st", [P, LH // 2, 2 * LD])

        nmax = [sb("nmax0", [P, BLK, NM]), sb("nmax1", [P, BLK, H])]
        nmax2 = [sb(f"nmax2_{n}", [P, BLK, P], BF16) for n in range(2)]
        m_t = [sb(f"m_t{n}", [P, T], BF16) for n in range(2)]
        prob_l = sb("prob_l", [P, LH // 2, T])
        o_t = sb("o_t", [P, 4, T])
        rsum, rrec = sb("rsum", [P, BLK * H]), sb("rrec", [P, BLK * H])
        lo_t = sb("lo_t", [2 * LD, T])
        lsum, lrec = sb("lsum", [P, BLK, LH]), sb("lrec", [P, BLK, LH])
        local, lat = sb("local", [P, BLK, D]), sb("lat", [P, BLK, LD])
        lat_t = sb("lat_t", [LD, T])
        remote = sb("remote", [P, BLK, D])
        gl, gr = sb("gl", [P, BLK, D]), sb("gr", [P, BLK, D])
        glog, gexp, gate = (sb(n, [P, BLK * H]) for n in ("glog", "gexp", "gate"))
        mixed, out_t = gr, sb("out_t", [P, T])
        x1 = sb("x1", [P, BLK, D])
        st1, mv1 = sb("st1", [P, BLK, 6]), sb("mv1", [P, BLK, 2])
        ve1, rs1 = sb("ve1", [P, BLK]), sb("rs1", [P, BLK])
        xn1 = sb("xn1", [P, BLK, D])
        emb = sb("emb", [P, BLK, 2 * D])
        xs1 = emb[:, 0, :].rearrange("p (k d) -> p k d", k=BLK)
        imp, eimp = sb("imp", [P, BLK]), sb("eimp", [P, BLK])
        xn1_t = sb("xn1_t", [P, T])
        u_qk, u_sq = sb("u_qk", [P, BLK, 2 * D]), emb[:]
        v_new = sb("v_new", [P, BLK, D])
        NV = BLK * 2 * H
        mink, lnw, nom, rnom, epos, eneg = (sb(n, [P, NV]) for n in ("mink", "lnw", "nom", "rnom", "epos", "eneg"))
        ctime, sfac, wsmall, poly, small = (sb(n, [P, NV]) for n in ("ctime", "sfac", "wsmall", "poly", "small"))

        x1res, spike = sb("x1res", [P, BLK, D]), sb("spike", [P, BLK])
        zmin, zsq, zsr, zd = (sb(n, [P, BLK * H]) for n in ("zmin", "zsq", "zsr", "zd"))
        gated = zc[:, (UNITS - 1) * UNIT:UNITS * UNIT].rearrange("p (c t) -> p c t", c=HC)
        prob1 = zs
        y1 = local
        hid1, hid2, hid3 = (sb(n, [P, HC, T]) for n in ("hid1", "hid2", "hid3"))
        xatt, xold = sb("xatt", [P, BLK, D]), sb("xold", [P, BLK, D])

        scr = nc.dram_tensor("scr", [2, 2, P, len(SLOTS), T], BF16, kind="Internal").ap()

        pu = ctx.enter_context(nc.psum_tensor("pu", [P, 2, UNIT], F32))
        pav = ctx.enter_context(nc.psum_tensor("pav", [P, 2 * BANK], F32))
        pm = ctx.enter_context(nc.psum_tensor("pm", [P, 2, BANK], F32))
        F, M, L, E, O = "first", "middle", "last", "end", "out"
        MAX, MIN, EXP, COSH, SUB = ([f"{n}{u}" for u in range(UNITS)] for n in ("max", "min", "exp", "cosh", "sub"))
        uses = lambda stage, names: [(stage, n) for n in names]
        PAIRS = [use for u in range(UNITS) for use in ((M, EXP[u]), (L, COSH[u]))]
        UNIT_USES = [uses(M, MAX[1::2]) + uses(L, MIN[0::2]) + PAIRS[0::3] + uses(O, ["yffn"]) + uses(L, [SUB[0], SUB[3], SUB[5]]),
                     uses(M, MAX[0::2]) + uses(L, MIN[1::2]) + PAIRS[1::3] + uses(E, ["f3"]) + uses(L, [SUB[2], SUB[4]])]
        MISC_ORDER = uses(L, ["f1_2", "f1_3"]) + [
                      (F, "xT"), (M, "lmax"), (E, "yT"), (F, "qk"), (M, "mT"), (E, "y1"), (M, "lexp"), (M, "lo"), (M, "loT"), (M, "latT"),
                      (M, "rem"), (F, "v"), (F, "rqkv"), (M, "mixT"), (M, "y0"), (L, "mT1"),
                      (M, "x1T"), (M, "qkv1a"), (M, "qkv1b"), (L, "f2_0"), (L, "f2_1"), (M, "embT")]
        MISC_USES = [MISC_ORDER[0::2], MISC_ORDER[1::2]]
        AV_USES = uses(E, ["av1", "avT1"]) + PAIRS[2::3] + uses(M, ["av0", "avT0"]) + uses(L, [SUB[1]]) + uses(M, ["f1"])

        def buffer(name, ap, users):
            one = Buffer(ap, users, sem(name + "_full"), sig(name + "_free", start=1).sem)
            return {n: one for _, n in users}

        score_banks = buffer("unit0", pu[:, 0, :], UNIT_USES[0]) | buffer("unit1", pu[:, 1, :], UNIT_USES[1]) | buffer("av", pav[:, :], AV_USES)
        misc_banks = buffer("misc0", pm[:, 0, :], MISC_USES[0]) | buffer("misc1", pm[:, 1, :], MISC_USES[1])
        unit = avuse = lambda run, n: score_banks[n].use(run, n)
        misc = lambda run, n: misc_banks[n].use(run, n)

        loads = []
        consts_in, passed = sem("consts_in"), sem("passed")
        zeros_set = sem("zeros_set")
        pre_in = [sem("pre_in0"), sem("pre_in1")]
        pre_var, pre_scale, pre_normed = sem("pre_var"), sem("pre_scale"), sem("pre_normed")
        pool_pre = sem("pool_pre")
        cols_ready, all_ready = sem("cols_ready"), sem("all_ready")
        weights_ready = sem("weights_ready")
        pre_link = sem("pre_link")

        x_in = sig("x_in", 1, 16)
        var0, rstd0, var0b, rstd0b = sig("var0"), sig("rstd0"), sig("var0b"), sig("rstd0b")
        xn_ready, xres_ready, xf_ready = sig("xn_ready"), sig("xres_ready"), sig("xf_ready")
        xq_ready = sig("xq_ready", start=1)
        pooled_ready = sig("pooled_ready")
        hi_ready = [sig("hi_ready0"), sig("hi_ready1")]
        parts_ready = [sig("parts_ready0"), sig("parts_ready1")]
        scr_written = [sig("scr_written0", 6, 16), sig("scr_written1", 6, 16)]
        stacked = [sig("stacked0", 3, 16, start=1), sig("stacked1", 3, 16, start=1)]
        rq_ready, rk_ready, rv_ready = sig("rq_ready"), sig("rk_ready"), sig("rv_ready")
        nmax_ready = [sig("nmax_ready0"), sig("nmax_ready1")]
        masked0 = sig("masked0", UNITS + 1)
        gr_ready, glog_ready, gexp_ready = (sig(n) for n in ("gr_ready", "glog_ready", "gexp_ready"))
        mixed_ready = sig("mixed_ready")

        var1, rstd1, xn1_ready, x1res_ready = sig("var1"), sig("rstd1"), sig("xn1_ready"), sig("x1res_ready")
        imp_ready, eimp_ready = sig("imp_ready"), sig("eimp_ready")
        xs1_ready = sig("xs1_ready")
        mink_ready, exps_ready, emb_ready = (sig(n) for n in ("mink_ready", "exps_ready", "emb_ready"))
        v1_ready = sig("v1_ready")
        zmin_ready, zsr_ready, zsum_ready, zln_ready = (sig(n) for n in ("zmin_ready", "zsr_ready", "zsum_ready", "zln_ready"))
        sqrt_done, ln_done, exp1_done, masked1 = (sig(n, UNITS) for n in ("sqrt_done", "ln_done", "exp1_done", "masked1"))
        SQUARED_BY_POOL, SQUARED_BY_DVE, SUMMED_BY_POOL, SQUARED_LOG_BY_POOL = (1, 4), (5,), (3, 4, 5), (2, 3, 5)
        sum_done = [sig("sum_done_dve", UNITS - len(SUMMED_BY_POOL)), sig("sum_done_pool", len(SUMMED_BY_POOL))]
        squared = [sig(f"squared{n}") for n in range(UNITS)]
        hid2_ready, hid3_ready, xold_ready = sig("hid2_ready"), sig("hid3_ready"), sig("xold_ready")
        sq_done = [sig("sq_done_act", UNITS - len(SQUARED_LOG_BY_POOL)), sig("sq_done_pool", len(SQUARED_LOG_BY_POOL))]
        sil_ready, hid1_ready = sig("sil_ready"), sig("hid1_ready")
        out_done = sig("out_done", 1, 16, start=1)
        dve_link = {F: sig("dve_first", DVE_LINKS[F]), M: sig("dve_middle", DVE_LINKS[M]), L: sig("dve_last", DVE_LINKS[L]), E: sig("dve_end", DVE_LINKS[E])}
        act_link = {M: sig("act_middle", 2), L: sig("act_last", 1)}
        pool_link = {F: sig("pool_first", 5)}

        class Links:

            def __init__(self, eng, counter, seq):
                self.eng, self.counter, self.seq, self.n = eng, counter, seq, 0

            def __call__(self, ins, after=None):
                self.n += 1
                ins.then_inc(self.counter.sem, 1)
                self.eng.wait_ge(self.counter.sem, self.counter.at(self.seq, self.n))
                if after:
                    after(self.eng)

            def end(self):
                assert self.n == self.counter.per, (self.counter.sem, self.n)

        def links_of(eng, counters, run):
            seqs = {F: run.first, M: run.middle, L: run.last, E: run.end, O: run.out}
            return {n: Links(eng, c, seqs[n]) for n, c in counters.items() if seqs[n] is not None}

        def apart(eng):
            eng.sem_inc(passed, 1)

        def phases(eng, iteration):
            for phase in PHASES:
                if phase.trips == 1:
                    iteration(Run(phase, phase.t0))
                else:
                    with eng.Fori(phase.t0, phase.t0 + phase.trips) as t:
                        iteration(Run(phase, t))

        block = ctx.enter_context(nc.Block())

        def row(ap, n=P):
            return ap.rearrange("(o n) -> o n", o=1).to_broadcast([n, ap.shape[0]])

        def col(ap):
            return ap.rearrange("(p o) -> p o", o=1)

        for name, dst in (("ident", ident), ("ident_bf", ident_bf), ("win0", win0), ("win1", win1), ("cau0", cau0),
                          ("winl", winl), ("winl_t", winl_t), ("sel", sel), ("lat_cols", lat_cols), ("lat_rows", lat_rows),
                          ("lat_ones", rv_st)):
            loads.append((dst[:], A[name]))
        loads += [
            (w_qkv0[:], A["L0_attn_qkv_w"]), (b_qk0[:], A["b_qk0_cols"]),
            (b_v0[:], row(A["L0_attn_qkv_b"][2 * D:3 * D])), (w_rq[:], A["L0_attn_rq_w"]), (b_rq[:], col(A["L0_attn_rq_b"])),
            (w_rkv[:], A["L0_attn_rkv_w"]), (b_rk[:], col(A["L0_attn_rkv_b"][0:LD])), (b_rv[:], row(A["L0_attn_rkv_b"][LD:2 * LD])),
            (w_rout[:], A["L0_attn_rout_w"]), (b_rout[:], row(A["L0_attn_rout_b"])), (w_out0[:], A["L0_attn_out_w"]),
            (b_out0[:], row(A["L0_attn_out_b"])), (gate_l[:], row(A["L0_attn_gl_w"].rearrange("a o -> (a o)"))),
            (gate_r[:], row(A["L0_attn_gr_w"].rearrange("a o -> (a o)"))), (w_tern, A["L0_ffn_weight"]),
            (gam_row, row(A["L0_ffn_ln_gamma"])), (bet_row, row(A["L0_ffn_ln_beta"])),
            (gam_col[:], col(A["L0_ffn_ln_gamma"])), (bet_col[:], col(A["L0_ffn_ln_beta"])),
            (w_qkv1[:], A["L1_attn_W_qkv"]), (b_qk1[:], row(A["L1_attn_b_qkv"][0:2 * D])), (b_v1[:], row(A["L1_attn_b_qkv"][2 * D:3 * D])),
            (w_out1[:], A["L1_attn_W_out"]), (b_out1[:], row(A["L1_attn_b_out"])), (w_sur[:], row(A["L1_attn_w_sur"])),
            (b_sur[:], row(A["L1_attn_b_sur"])), (thresh[:], row(A["L1_attn_threshold"])),
            (w1t[:], A["w1t"]), (w2t[:], A["w2t"]), (h1t[:], A["h1t"].rearrange("(c p) n -> p c n", p=P)),
            (h2t[:], A["h2t"].rearrange("(c p) n -> p c n", p=P)), (w3t[:], A["w3t"].rearrange("(c p) n -> p c n", p=P)),
            (s3, row(A["L1_ffn_w3_s"])),
        ]
        for dst, name in ((s1, "L1_ffn_w1_s"), (s2, "L1_ffn_w2_s"), (g1, "L1_ffn_h1_s"), (g2, "L1_ffn_h2_s")):
            loads.append((dst[:], A[name + "_cols"]))

        x_seq = A["L0_attn_x"].rearrange("b (k p) d -> b p k d", p=P)
        out_seq = out.rearrange("b (k p) d -> b p k d", p=P)
        x_chunk = A["L0_attn_x"].rearrange("b t d -> (b t) d").rearrange("(c n p) d -> c p n d", p=P, n=PRE)

        @block.sync
        def _(sp):
            for s in ahead:
                sp.sem_inc(s.sem, s.start)
            sp.sem_inc(pre_in[0], 1)
            sp.sem_inc(pre_in[1], 1)
            for c in range(PRE_CHUNKS // 2):
                for k in range(2):
                    sp.wait_ge(pre_in[k], c * 16 + 1)
                    sp.dma_start(px[k][:, c], x_chunk[c * 2 + k]).then_inc(pre_in[k], 16)
            for dst, src in loads:
                sp.dma_start(dst, src).then_inc(consts_in, 16)
            def stack(layer, s, run):
                sp.wait_ge(stacked[layer].sem, stacked[layer].at(s, 0))
                apart(sp)
                sp.wait_ge(parts_ready[layer].sem, parts_ready[layer].at(s))
                apart(sp)
                for side, cols in enumerate((slice(0, T), slice(T, 2 * T))):
                    for part in range(3):
                        slots = [n for n, pair in enumerate(SLOTS) if pair[side] == part]
                        step = slots[1] - slots[0]
                        sp.dma_start(scr[layer, side, :, slots[0]:slots[-1] + 1:step, :],
                                     bc(parts[:, part:part + 1, cols], [P, len(slots), T])).then_inc(scr_written[layer].sem, 16)
                sp.wait_ge(scr_written[layer].sem, scr_written[layer].at(s))
                apart(sp)
                if layer == 0 and run.middle is not None:
                    unit(run, f"exp{UNITS - 1}").wait_full(sp)
                    apart(sp)
                if layer == 1 and run.last is not None:
                    unit(run, f"cosh{UNITS - 1}").wait_full(sp)
                    apart(sp)
                half = P // 2
                for e in range(2):
                    sp.dma_start(q_st[layer][e * half:(e + 1) * half, :, e, :],
                                 scr[layer, 0].rearrange("(p e d) s t -> e (d s) p t", e=2, d=HD)[e]).then_inc(stacked[layer].sem, 16)
                sp.dma_start(k_st[layer][:], scr[layer, 1].rearrange("(p r) s t -> (r s) p t", p=HP)).then_inc(stacked[layer].sem, 16)

            def load_x(i):
                sp.dma_start(x[:], x_seq[bass.ds(i, 1)].rearrange("o p k d -> p (o k) d")).then_inc(x_in.sem, 16)

            def iteration(run):
                f, m, o = run.first, run.middle, run.out
                if f:
                    stack(0, f, run)
                if o:
                    unit(run, "yffn").wait_drained(sp)
                    apart(sp)
                    sp.dma_start(out_seq[bass.ds(o.index(), 1)].rearrange("o p k d -> p (o k) d"), xold[:]).then_inc(out_done.sem, 16)
                if f and (run.phase.trips > 1 or run.t + 1 < NB):
                    sp.wait_ge(xn_ready.sem, xn_ready.at(f))
                    apart(sp)
                    sp.wait_ge(xres_ready.sem, xres_ready.at(f))
                    apart(sp)
                    load_x(f.index() + 1)
                if m:
                    stack(1, m, run)

            sp.wait_ge(zeros_set, 3)
            load_x(0)
            phases(sp, iteration)
            sp.wait_ge(out_done.sem, out_done.at(Sequence(NB - 1, 0)))

        @block.vector
        def _(dve):
            V = nc.vector
            n_pre = [0]

            def pre(ins):
                n_pre[0] += 1
                ins.then_inc(pre_link, 1)
                dve.wait_ge(pre_link, n_pre[0])

            V.memset(mhalf[:], -0.5)
            V.memset(minus1[:], -1.0)
            V.memset(ksign[:].rearrange("p (k s h) -> p k s h", k=BLK, s=2)[:, :, 0, :], 1.0)
            V.memset(ksign[:].rearrange("p (k s h) -> p k s h", k=BLK, s=2)[:, :, 1, :], -1.0)
            V.memset(zero[:], 0.0).then_inc(zeros_set, 1)
            with dve.Fori(0, PRE_CHUNKS // 2) as c:
                for k in range(2):
                    dve.wait_ge(pre_in[k], c * 16 + 17)
                    apart(dve)
                    for n in range(PRE):
                        last = V.bn_stats(pst[k][:, n, :], px[k][:, bass.ds(c, 1), n, :].rearrange("p o d -> p (o d)"))
                    last.then_inc(pre_link, 1)
                    dve.wait_ge(pre_link, c * 2 + k + 1)
                    apart(dve)
                    dve.wait_ge(pre_scale, c * 2 + k + 1)
                    apart(dve)
                    for n in range(PRE):
                        last = V.bn_aggr(pmv[k][:, n, :], pst[k][:, n, :])
                    last.then_inc(pre_var, 1)
            with dve.Fori(0, PRE_CHUNKS // 2) as c:
                for k in range(2):
                    dve.wait_ge(pre_normed, c * 2 + k + 1)
                    apart(dve)
                    chunk = px[k][:, bass.ds(c, 1)].rearrange("p o n d -> p d (o n)")
                    for dst, op in ((pmost, ALU.max), (pleast, ALU.min)):
                        V.tensor_reduce(out=dst[k][:, bass.ds(c, 1), 0, :].rearrange("p o d -> p (o d)"), in_=chunk, axis=AX_X,
                                        op=op).then_inc(pre_link, 1)
            dve.wait_ge(zeros_set, 3)
            dve.wait_ge(consts_in, 16 * len(loads))
            V.tensor_reduce(out=wcol[:], in_=w_tern, axis=AX_X, op=ALU.add, apply_absolute_value=True).then_inc(cols_ready, 1)
            V.tensor_tensor(w3t[:], w3t[:], bc(s3.unsqueeze(1), [P, HC, D]), ALU.mult)

            n_pre[0] = 3 * PRE_CHUNKS
            dve.wait_ge(pre_link, n_pre[0])
            everything = lambda halves: halves.rearrange("p c d -> p d c")
            pre(V.tensor_tensor(pmost[0], pmost[0], pmost[1], ALU.max))
            pre(V.tensor_tensor(pleast[0], pleast[0], pleast[1], ALU.min))
            V.tensor_reduce(out=pall[:, 0, :], in_=everything(pmost[0][:, :, 0, :]), axis=AX_X, op=ALU.max)
            pre(V.tensor_reduce(out=pall[:, 1, :], in_=everything(pleast[0][:, :, 0, :]), axis=AX_X, op=ALU.min))
            pre(V.tensor_tensor(pall, pall, bc(gam_row.unsqueeze(1), [P, 2, D]), ALU.mult))
            pre(V.tensor_tensor(pall, pall, bc(bet_row.unsqueeze(1), [P, 2, D]), ALU.add))
            V.tensor_reduce(out=gcol[:], in_=pall.rearrange("p e d -> p (e d)"), axis=AX_X, op=ALU.max,
                            apply_absolute_value=True).then_inc(cols_ready, 1)
            dve.wait_ge(all_ready, 2)
            lim = float(np.float32(QB - FFN_EPS)) / QB
            V.tensor_scalar(thr[:], gall[:], lim, None, ALU.mult)
            V.tensor_scalar(nthr[:], gall[:], -lim, None, ALU.mult)
            pre(V.tensor_scalar(beta[:], wall[:], 1.0 / (D * D), None, ALU.mult))
            pre(V.tensor_scalar(rbeta[:], beta[:], FFN_EPS, None, ALU.add))
            pre(V.reciprocal(rbeta[:], rbeta[:]))
            pre(V.tensor_scalar(wn, w_tern, rbeta[:], None, ALU.mult))
            pre(V.tensor_scalar(wr, wn, 4.0, -4.0, ALU.min, ALU.max))
            magic = 1.5 * 2.0 ** 23
            pre(V.tensor_scalar(wr, wr, magic, None, ALU.add))
            pre(V.tensor_scalar(wr, wr, -magic, None, ALU.add))
            pre(V.tensor_scalar(wr, wr, 1.0, -1.0, ALU.min, ALU.max))
            V.tensor_scalar(w_qs[:], wr, beta[:], None, ALU.mult).then_inc(weights_ready, 1)

            d4 = lambda a: a[:].rearrange("p k (h d) -> p (k h) d", d=HD)

            def moments(dst_st, dst_mv, dst_ve, src, eps, ready, link):
                for k in range(BLK):
                    last = V.bn_stats(dst_st[:, k, :], src[:, k, :])
                link(last, apart)
                for k in range(BLK):
                    last = V.bn_aggr(dst_mv[:, k, :], dst_st[:, k, :])
                link(last)
                V.tensor_scalar(dst_ve[:], dst_mv[:, :, 1], eps, None, ALU.add).then_inc(ready.sem, 1)

            def normed(dst, src, mvs, rstd, ready, s):
                dve.wait_ge(ready.sem, ready.at(s))
                for k in range(BLK):
                    last = V.tensor_scalar(dst[:, k, :], src[:, k, :], mvs[:, k, 0:1], rstd[:, k:k + 1], ALU.subtract, ALU.mult)
                return last

            def split1(m, link):
                dve.wait_ge(hi_ready[1].sem, hi_ready[1].at(m))
                link(V.tensor_tensor(resid[:], qk_t[:], parts[:, 0, :], ALU.subtract))
                link(V.tensor_copy(parts[:, 1, :], resid[:]))
                V.tensor_tensor(parts[:, 2, :], resid[:], parts[:, 1, :], ALU.subtract).then_inc(parts_ready[1].sem, 1)

            def head_norm(layer, use, dst, link, extra=None):
                use.wait_full(dve)
                t = use.ap.rearrange("p (n c) -> p n c", c=32)
                total, rec = rsum, rrec
                link(V.tensor_scalar(total[:].unsqueeze(2), t[:, :, HD:HD + 1], 0.5, None, ALU.max))
                link(V.reciprocal(rec[:], total[:]))
                if extra is not None:
                    r3 = rec[:].rearrange("p (k h) -> p k h", k=BLK)
                    link(V.tensor_tensor(r3, r3, bc(extra[:].unsqueeze(2), [P, BLK, H]), ALU.mult))
                V.tensor_tensor(dst[:].rearrange("p k (h d) -> p (k h) d", d=HD), t[:, :, 0:HD],
                                bc(rec[:].unsqueeze(2), [P, BLK * H, HD]), ALU.mult).then_inc(use.free, 1)

            def heads_reduced(u, n, blocks, op, negate):
                heads, width = (8, P) if n < 2 else (4, T)
                h = 8 * n if n < 2 else 4 * (n - 2)
                dst = blocks[0 if n < 2 else 1][:, h:h + heads]
                u.wait_full(dve)
                V.tensor_reduce(out=dst, in_=u.ap.rearrange("p (h k) -> p h k", k=width), axis=AX_X, op=op, negate=negate).then_inc(u.free, 1)

            def pool_tokens(run, f, link):
                misc(run, "xT").wait_drained(dve)
                link(V.tensor_reduce(out=pooled[:, 0, :], in_=xn_t[:].rearrange("p (l c) -> p l c", c=POOL), axis=AX_X, op=ALU.add))
                V.tensor_copy(pooled[:, 1, :], pooled[:, 0, :]).then_inc(pooled_ready.sem, 1)

            def latent_projections(run, f):
                u = misc(run, "rqkv")
                u.wait_full(dve)
                V.tensor_scalar(rq_t[:], u.ap[0:LD, 0:T], b_rq[:], None, ALU.add).then_inc(rq_ready.sem, 1)
                V.tensor_scalar(rk_t[:], u.ap[0:LD, T:T + NLAT], 1.0 / POOL, b_rk[:], ALU.mult, ALU.add)
                last = V.scalar_tensor_tensor(rv[:], u.ap[:, T + NLAT:T + NLAT + LD], 1.0 / POOL, b_rv[:], ALU.mult, ALU.add)
                last.then_inc(u.free, 1)
                u.wait_drained(dve)
                V.tensor_tensor(rk_m[:], bc(rk_t[:].unsqueeze(1), [LD, LH, NLAT]), bc(lat_rows[:].unsqueeze(2), [LD, LH, NLAT]), ALU.mult).then_inc(rk_ready.sem, 1)
                V.tensor_tensor(rv_st[:, :, 0:LD], bc(rv[:].unsqueeze(1), [P, LH // 2, LD]), lat_cols[:], ALU.mult).then_inc(rv_ready.sem, 1)

            def values0(run, f):
                u = misc(run, "v")
                u.wait_full(dve)
                V.tensor_tensor(v_st[0][:, :, :, 0:HD], u.ap[:, 0:T].rearrange("p (k h d) -> p k h d", k=BLK, d=HD),
                                bc(b_v0[:].rearrange("p (h d) -> p h d", d=HD).unsqueeze(1), [P, BLK, H, HD]), ALU.add).then_inc(u.free, 1)

            def latent_maxima(run, m, link):
                u = misc(run, "lmax")
                u.wait_full(dve)
                V.tensor_reduce(out=nmax[0][:, :, H:NM], in_=u.ap.rearrange("p (k h l) -> p k h l", k=BLK, l=NLAT), axis=AX_X, op=ALU.max,
                                negate=True).then_inc(u.free, 1)
                u.wait_drained(dve)
                link(V.tensor_copy(nmax2[0][:, :, 0:NM], nmax[0][:]))
                V.tensor_tensor(nmax2[0][:, :, MLO:MLO + NM], nmax[0][:], nmax2[0][:, :, 0:NM], ALU.subtract).then_inc(nmax_ready[0].sem, 1)

            def latent_out(run):
                u = misc(run, "lo")
                u.wait_full(dve)
                V.tensor_copy(lo_t[:], u.ap[0:2 * LD, 0:T]).then_inc(u.free, 1)

            def latent_norm(run, link):
                u = misc(run, "loT")
                u.wait_full(dve)
                t = u.ap[:, 0:2 * 2 * LD].rearrange("p (k c) -> p k c", k=BLK)
                link(V.tensor_scalar(lsum[:], t[:, :, LD:LD + LH], 0.5, None, ALU.max))
                link(V.reciprocal(lrec[:], lsum[:]))
                V.tensor_tensor(lat[:].rearrange("p k (h d) -> p k h d", h=LH), t[:, :, 0:LD].rearrange("p k (h d) -> p k h d", h=LH),
                                bc(lrec[:].unsqueeze(3), [P, BLK, LH, LD // LH]), ALU.mult).then_inc(u.free, 1)

            def remote_bias(run):
                u = misc(run, "rem")
                u.wait_full(dve)
                V.tensor_tensor(remote[:], u.ap[:, 0:T].rearrange("p (k d) -> p k d", k=BLK), bc(b_rout[:].unsqueeze(1), [P, BLK, D]), ALU.add).then_inc(u.free, 1)

            def attended(run):
                u = avuse(run, "av0")
                u.wait_full(dve)
                V.tensor_copy(o_t[:].rearrange("p v t -> p (v t)"), u.ap).then_inc(u.free, 1)

            def gate_logits(m, link):
                link(V.tensor_tensor(d4(gl), d4(local), bc(gate_l[:].unsqueeze(1), [P, BLK * H, HD]), ALU.mult))
                dve.wait_ge(gr_ready.sem, gr_ready.at(m))
                link(V.tensor_tensor(gl[:], gl[:], gr[:], ALU.add))
                V.tensor_reduce(out=glog[:], in_=d4(gl), axis=AX_X, op=ALU.add).then_inc(glog_ready.sem, 1)
                V.tensor_tensor(gr[:], local[:], remote[:], ALU.subtract)

            def mix(m, link):
                dve.wait_ge(gexp_ready.sem, gexp_ready.at(m))
                link(V.tensor_scalar(gexp[:], gexp[:], 1.0, None, ALU.add))
                link(V.reciprocal(gate[:], gexp[:]))
                link(V.tensor_tensor(d4(gr), d4(gr), bc(gate[:].unsqueeze(2), [P, BLK * H, HD]), ALU.mult))
                V.tensor_tensor(mixed[:], gr[:], remote[:], ALU.add).then_inc(mixed_ready.sem, 1)

            def layer0_out(run, m):
                u = misc(run, "y0")
                u.wait_full(dve)
                if run.last:
                    dve.wait_ge(x1res_ready.sem, x1res_ready.at(run.last))
                V.tensor_tensor(x1[:], u.ap[:, 0:T].rearrange("p (k d) -> p k d", k=BLK), xres[:], ALU.add).then_inc(u.free, 1)
                u.wait_drained(dve)

            def importance(l, link):
                dve.wait_ge(xs1_ready.sem, xs1_ready.at(l))
                link(V.tensor_reduce(out=imp[:], in_=xs1, axis=AX_X, op=ALU.add))
                V.tensor_scalar(imp[:], imp[:], b_sur[:], None, ALU.add).then_inc(imp_ready.sem, 1)

            def projections1(run, m, link):
                if run.last:
                    dve.wait_ge(v1_ready.sem, v1_ready.at(run.last))
                for k, name in enumerate(("qkv1a", "qkv1b")):
                    u = misc(run, name)
                    u.wait_full(dve)
                    V.tensor_tensor(v_new[:, k, :], u.ap[:, 2 * D:3 * D], b_v1[:], ALU.add)
                    V.tensor_tensor(u_qk[:, k, :], u.ap[:, 0:2 * D], b_qk1[:], ALU.add).then_inc(u.free, 1)
                u.wait_drained(dve)
                link(V.tensor_tensor(u_sq, u_qk[:], u_qk[:], ALU.mult))
                sq = u_sq.rearrange("p k (h d) -> p (k h) d", d=HD)
                link(V.tensor_reduce(out=mink[:], in_=sq[:, :, 1:HD], axis=AX_X, op=ALU.add))
                link(V.tensor_tensor(mink[:], mink[:], sq[:, :, 0], ALU.subtract))
                V.tensor_scalar(mink[:], mink[:], 1e-8, None, ALU.max).then_inc(mink_ready.sem, 1)

            def sinh_series(m, link):
                dve.wait_ge(mink_ready.sem, mink_ready.at(m))
                V.tensor_scalar(small[:].bitcast(I32), mink[:], 1.0, None, ALU.is_le)
                link(V.tensor_scalar(wsmall[:], mink[:], 1.0, None, ALU.min))
                coefficients = [1.0 / np.prod(np.arange(2, 2 * k + 2, dtype=np.float64)) for k in (5, 4, 3, 2, 1)]
                link(V.tensor_scalar(poly[:], wsmall[:], float(coefficients[0]), None, ALU.mult))
                for c in coefficients[1:]:
                    link(V.scalar_tensor_tensor(poly[:], poly[:], float(c), wsmall[:], ALU.add, ALU.mult))
                link(V.tensor_scalar(poly[:], poly[:], 1.0, None, ALU.add))

            def embedding(m, link):
                dve.wait_ge(exps_ready.sem, exps_ready.at(m))
                V.tensor_tensor(ctime[:], epos[:], eneg[:], ALU.add)
                link(V.tensor_tensor(sfac[:], epos[:], eneg[:], ALU.subtract))
                link(V.scalar_tensor_tensor(sfac[:], sfac[:], 0.5, rnom[:], ALU.mult, ALU.mult), apart)
                link(V.copy_predicated(sfac[:], small[:].bitcast(I32), poly[:]))
                link(V.tensor_tensor(sfac[:], sfac[:], ksign[:], ALU.mult))
                e3 = emb[:].rearrange("p k (h d) -> p (k h) d", d=HD)
                link(V.tensor_tensor(e3, u_qk[:].rearrange("p k (h d) -> p (k h) d", d=HD), bc(sfac[:].unsqueeze(2), [P, NV, HD]), ALU.mult))
                V.tensor_scalar(e3[:, :, 0:1], ctime[:].unsqueeze(2), 0.5, None, ALU.mult).then_inc(emb_ready.sem, 1)

            def spikes(e, link):
                dve.wait_ge(eimp_ready.sem, eimp_ready.at(e))
                link(V.tensor_scalar(eimp[:], eimp[:], 1.0, None, ALU.add))
                link(V.reciprocal(eimp[:], eimp[:]))
                link(V.tensor_scalar(spike[:], eimp[:], thresh[:], None, ALU.is_gt))

            def clamp_minima(run):
                unit(run, f"min{UNITS - 1}").wait_drained(dve)
                V.tensor_scalar(zmin[:], zmin[:], MIN_COSH, None, ALU.max).then_inc(zmin_ready.sem, 1)

            def clamp_cosh(run, n):
                u = unit(run, f"cosh{n}")
                u.wait_full(dve)
                if n == UNITS - 1:
                    dve.wait_ge(hid1_ready.sem, hid1_ready.at(run.last))
                V.tensor_scalar(zc[:, n * UNIT:(n + 1) * UNIT], u.ap, MIN_COSH, None, ALU.max).then_inc(u.free, 1)

            def square_cosh(run, l, n):
                c = slice(n * UNIT, (n + 1) * UNIT)
                unit(run, f"cosh{n}").wait_drained(dve)
                V.tensor_tensor(zs[:, c], zc[:, c], zc[:, c], ALU.mult).then_inc(squared[n].sem, 1)

            def sum_minima(l):
                dve.wait_ge(zsr_ready.sem, zsr_ready.at(l))
                V.tensor_tensor(zmin[:], zmin[:], zsr[:], ALU.add).then_inc(zsum_ready.sem, 1)

            def sum_cosh(l, n):
                c = slice(n * UNIT, (n + 1) * UNIT)
                dve.wait_ge(sqrt_done.sem, sqrt_done.at(l, n + 1))
                V.tensor_tensor(zc[:, c], zc[:, c], zs[:, c], ALU.add).then_inc(sum_done[0].sem, 1)

            def least_squares(l, link):
                dve.wait_ge(zln_ready.sem, zln_ready.at(l))
                z3 = zd[:].rearrange("p (k h) -> p k h", k=BLK)
                link(V.scalar_tensor_tensor(nmax[1][:], z3, -1.0, z3, ALU.mult, ALU.mult))
                link(V.tensor_copy(nmax2[1][:, :, 0:H], nmax[1][:]))
                V.tensor_tensor(nmax2[1][:, :, MLO:MLO + H], nmax[1][:], nmax2[1][:, :, 0:H], ALU.subtract).then_inc(nmax_ready[1].sem, 1)

            def shift(run, l, n):
                c = slice(n * UNIT, (n + 1) * UNIT)
                done = sq_done[n in SQUARED_LOG_BY_POOL]
                dve.wait_ge(done.sem, done.at(l, nth(n, SQUARED_LOG_BY_POOL)))
                u = unit(run, f"sub{n}")
                u.wait_full(dve)
                V.tensor_tensor(zc[:, c], zs[:, c], u.ap, ALU.add).then_inc(u.free, 1)

            def attention_out(run, e):
                u = misc(run, "y1")
                u.wait_full(dve)
                if run.out:
                    dve.wait_ge(xold_ready.sem, xold_ready.at(run.out))
                V.tensor_tensor(xatt[:], u.ap[:, 0:T].rearrange("p (k d) -> p k d", k=BLK), x1res[:], ALU.add).then_inc(u.free, 1)

            def output(run, o):
                u = unit(run, "yffn")
                dve.wait_ge(xold_ready.sem, xold_ready.at(o))
                u.wait_full(dve)
                V.tensor_tensor(xold[:], u.ap[:, 0:T].rearrange("p (k d) -> p k d", k=BLK), xold[:], ALU.add).then_inc(u.free, 1)

            def iteration(run):
                f, m, l, e, o = run.first, run.middle, run.last, run.end, run.out
                link = links_of(dve, dve_link, run)
                zblocks = [zmin[:, 0:H], zmin[:, H:2 * H]]
                nblocks = [nmax[0][:, 0, 0:H], nmax[0][:, 1, 0:H]]
                for n in range(UNITS):
                    if m:
                        heads_reduced(unit(run, f"max{n}"), n, nblocks, ALU.max, True)
                    if f and n == 1:
                        dve.wait_ge(x_in.sem, x_in.at(f))
                        moments(st, mv, ve, x, LN_EPS, var0, link[F])
                if e:
                    spikes(e, link[E])
                for n in range(UNITS):
                    if l:
                        heads_reduced(unit(run, f"min{n}"), n, zblocks, ALU.min, False)
                    if e and n == 1:
                        head_norm(1, avuse(run, "avT1"), y1, link[E], spike)
                    if m and n == 2:
                        latent_maxima(run, m, link[M])
                if l:
                    clamp_minima(run)
                if e:
                    attention_out(run, e)
                if f:
                    pool_tokens(run, f, link[F])
                for n in range(UNITS):
                    if l:
                        clamp_cosh(run, n)
                    if m and n == 2:
                        latent_out(run)
                    if m and n == 4:
                        latent_norm(run, link[M])
                if m:
                    remote_bias(run)
                if l:
                    for n in SQUARED_BY_DVE:
                        square_cosh(run, l, n)
                if l:
                    sum_minima(l)
                    sum_cosh(l, 0)
                    importance(l, link[L])
                if m:
                    attended(run)
                if f:
                    values0(run, f)
                if l:
                    sum_cosh(l, 1)
                if m:
                    head_norm(0, avuse(run, "avT0"), local, link[M])
                    avuse(run, "avT0").wait_drained(dve)
                    gate_logits(m, link[M])
                    mix(m, link[M])
                if f:
                    latent_projections(run, f)
                if l:
                    least_squares(l, link[L])
                if o:
                    output(run, o)
                if m:
                    layer0_out(run, m)
                    moments(st1, mv1, ve1, x1, LN_EPS, var1, link[M])
                if l:
                    sum_cosh(l, 2)
                if m:
                    normed(xn1, x1, mv1, rs1, rstd1, m).then_inc(xn1_ready.sem, 1)
                if l:
                    shift(run, l, 0)
                if l:
                    shift(run, l, 1)
                if m:
                    projections1(run, m, link[M])
                if m:
                    sinh_series(m, link[M])
                    embedding(m, link[M])
                if l:
                    shift(run, l, 2)
                    shift(run, l, 3)
                if m:
                    split1(m, link[M])
                if l:
                    shift(run, l, 4)
                    shift(run, l, 5)
                for one in link.values():
                    one.end()

            phases(dve, iteration)

        @block.gpsimd
        def _(pool):
            G = nc.gpsimd
            RMAX, RADD = bass.bass_isa.ReduceOp.max, bass.bass_isa.ReduceOp.add
            pool.wait_ge(zeros_set, 1)
            pool.sem_inc(pre_scale, 2)
            STEPS = 4
            with pool.Fori(0, PRE_CHUNKS // 2) as c:
                for k in range(2):
                    done = 0

                    def own(ins):
                        nonlocal done
                        done += 1
                        ins.then_inc(pool_pre, 1)
                        pool.wait_ge(pool_pre, c * (2 * STEPS) + (k * STEPS + done))
                        apart(pool)

                    pool.wait_ge(pre_var, c * 2 + k + 1)
                    apart(pool)
                    row = lambda a: a[k][:, bass.ds(c, 1), 0, :].rearrange("p o n -> p (o n)")
                    mean, var = pmv[k][:, :, 0], pmv[k][:, :, 1]
                    own(G.tensor_scalar(pve[:], var, LN_EPS, FFN_LN_EPS, ALU.add, ALU.mult))
                    own(G.tensor_tensor(pve[:], pve[:], var, ALU.add))
                    own(G.tensor_tensor(row(pscale), pve[:], mhalf[:, 0:PRE], ALU.pow))
                    own(G.tensor_tensor(prs[:], mean, bc(minus1[:], [P, PRE]), ALU.mult))
                    G.tensor_tensor(row(pneg), prs[:], row(pscale), ALU.mult).then_inc(pre_scale, 1)
                    assert done == STEPS
            pool.wait_ge(cols_ready, 1)
            G.partition_all_reduce(wall[:], wcol[:], P, RADD).then_inc(all_ready, 1)
            pool.wait_ge(cols_ready, 2)
            G.partition_all_reduce(gall[:], gcol[:], P, RMAX).then_inc(all_ready, 1)
            d4 = lambda a: a[:].rearrange("p k (h d) -> p (k h) d", d=HD)

            def power(dst, src, var, done, s):
                pool.wait_ge(var.sem, var.at(s))
                G.tensor_tensor(dst[:], src[:], mhalf[:, 0:BLK], ALU.pow).then_inc(done.sem, 1)

            def power_again(f, link):
                link(G.tensor_tensor(ve2[:], mv[:, :, 1], rs[:], ALU.mult))
                link(G.tensor_tensor(ve2[:], ve2[:], rs[:], ALU.mult), apart)
                link(G.tensor_scalar(ve2[:], ve2[:], FFN_LN_EPS, None, ALU.add))
                G.tensor_tensor(rs2[:], ve2[:], mhalf[:, 0:BLK], ALU.pow).then_inc(rstd0b.sem, 1)

            def normed(f):
                pool.wait_ge(rstd0.sem, rstd0.at(f))
                apart(pool)
                for k in range(BLK):
                    last = G.tensor_scalar(xn[:, k, :], x[:, k, :], mv[:, k, 0:1], rs[:, k:k + 1], ALU.subtract, ALU.mult)
                last.then_inc(xn_ready.sem, 1)

            def normed_again(f):
                pool.wait_ge(rstd0b.sem, rstd0b.at(f))
                apart(pool)
                pool.wait_ge(xn_ready.sem, xn_ready.at(f))
                apart(pool)
                for k in range(BLK):
                    last = G.tensor_scalar(xf[:, k, :], xn[:, k, :], rs2[:, k:k + 1], None, ALU.mult)
                last.then_inc(xf_ready.sem, 1)

            def hidden1(l):
                pool.wait_ge(sil_ready.sem, sil_ready.at(l))
                G.tensor_tensor(hid1[:], hid1[:], gated, ALU.mult).then_inc(hid1_ready.sem, 1)

            def split0(f, link):
                pool.wait_ge(hi_ready[0].sem, hi_ready[0].at(f))
                link(G.tensor_tensor(resid[:], qk_t[:], parts[:, 0, :], ALU.subtract))
                apart(pool)
                link(G.tensor_copy(parts[:, 1, :], resid[:]))
                G.tensor_tensor(parts[:, 2, :], resid[:], parts[:, 1, :], ALU.subtract).then_inc(parts_ready[0].sem, 1)

            def clip_input(run, f):
                if run.middle:
                    misc(run, "y0").wait_drained(pool)
                misc(run, "xT").wait_drained(pool)
                apart(pool)
                G.tensor_scalar(xq_t[:], xa_t[:], thr[:], nthr[:], ALU.min, ALU.max).then_inc(xq_ready.sem, 1)

            def importance_products(run, m):
                misc(run, "embT").wait_full(pool)
                G.tensor_tensor(xs1, xn1[:], bc(w_sur[:].unsqueeze(1), [P, BLK, D]), ALU.mult).then_inc(xs1_ready.sem, 1)

            def window(run, n):
                unit(run, f"exp{n}").wait_drained(pool)
                apart(pool)
                c = prob0[:, n * UNIT:(n + 1) * UNIT]
                if n < 4:
                    t = c.rearrange("p (h q) -> p h q", q=T)
                    G.affine_select(out=t[:, :, 0:P], in_=t[:, :, 0:P], compare_op=ALU.is_gt, fill=0.0, base=0,
                                    pattern=[[0, 4], [1, P]], channel_multiplier=-1)
                    G.affine_select(out=t[:, :, P:T], in_=t[:, :, P:T], compare_op=ALU.is_ge, fill=0.0, base=0,
                                    pattern=[[0, 4], [-1, P]], channel_multiplier=1).then_inc(masked0.sem, 1)
                else:
                    t = c.rearrange("p (h q) -> p h q", q=P)
                    G.affine_select(out=t, in_=t, compare_op=ALU.is_gt, fill=0.0, base=0,
                                    pattern=[[0, 8], [1, P]], channel_multiplier=-1).then_inc(masked0.sem, 1)

            def window_edge(m):
                pool.wait_ge(masked0.sem, masked0.at(m, UNITS - 2))
                apart(pool)
                edge = prob0[:, 0:H * T].rearrange("p (h q) -> p h q", q=T)[:, :, P:P + 1]
                G.affine_select(out=edge, in_=edge, compare_op=ALU.is_gt, fill=0.0, base=0, pattern=[[0, H], [0, 1]],
                                channel_multiplier=1).then_inc(masked0.sem, 1)

            def gate_remote(run):
                misc(run, "rem").wait_drained(pool)
                G.tensor_tensor(d4(gr), d4(remote), bc(gate_r[:].unsqueeze(1), [P, BLK * H, HD]), ALU.mult).then_inc(gr_ready.sem, 1)

            def sum_cosh(l, n):
                c = slice(n * UNIT, (n + 1) * UNIT)
                pool.wait_ge(sqrt_done.sem, sqrt_done.at(l, n + 1))
                G.tensor_tensor(zc[:, c], zc[:, c], zs[:, c], ALU.add).then_inc(sum_done[1].sem, 1)

            def square(l, n):
                c = slice(n * UNIT, (n + 1) * UNIT)
                pool.wait_ge(ln_done.sem, ln_done.at(l, n + 1))
                G.tensor_tensor(zs[:, c], zs[:, c], zs[:, c], ALU.mult).then_inc(sq_done[1].sem, 1)

            def square_cosh(run, l, n):
                c = slice(n * UNIT, (n + 1) * UNIT)
                unit(run, f"cosh{n}").wait_drained(pool)
                G.tensor_tensor(zs[:, c], zc[:, c], zc[:, c], ALU.mult).then_inc(squared[n].sem, 1)

            def causal(l, n):
                pool.wait_ge(exp1_done.sem, exp1_done.at(l, n + 1))
                apart(pool)
                c = prob1[:, n * UNIT:(n + 1) * UNIT]
                t = c.rearrange("p (h q) -> p h q", q=T)[:, :, 0:P] if n < 4 else c.rearrange("p (h q) -> p h q", q=P)
                G.affine_select(out=t, in_=t, compare_op=ALU.is_ge, fill=0.0, base=0, pattern=[[0, 4 if n < 4 else 8], [1, P]],
                                channel_multiplier=-1).then_inc(masked1.sem, 1)

            def iteration(run):
                f, m, l, e, o = run.first, run.middle, run.last, run.end, run.out
                link = links_of(pool, pool_link, run)
                if o:
                    pool.wait_ge(out_done.sem, out_done.at(o, 0))
                    apart(pool)
                    G.tensor_copy(xold[:], xatt[:]).then_inc(xold_ready.sem, 1)
                if f:
                    power(rs, ve, var0, rstd0, f)
                    normed(f)
                    power_again(f, link[F])
                    normed_again(f)
                if l:
                    if e:
                        avuse(run, "av1").wait_full(pool)
                    apart(pool)
                    G.tensor_copy(v_st[1][:, :, :, 0:HD], v_new[:].rearrange("p k (h d) -> p k h d", d=HD)).then_inc(v1_ready.sem, 1)
                if l:
                    hidden1(l)
                for n in range(UNITS):
                    if m:
                        window(run, n)
                    if m and n == UNITS - 3:
                        window_edge(m)
                    if l and n == SQUARED_BY_POOL[0]:
                        square_cosh(run, l, n)
                if m:
                    gate_remote(run)
                if l:
                    square_cosh(run, l, SQUARED_BY_POOL[1])
                if f:
                    split0(f, link[F])
                if l:
                    if e:
                        misc(run, "y1").wait_drained(pool)
                    G.tensor_tensor(x1res[:], x1[:], bc(b_out1[:].unsqueeze(1), [P, BLK, D]), ALU.add).then_inc(x1res_ready.sem, 1)
                if l:
                    sum_cosh(l, 3)
                    sum_cosh(l, 4)
                if m:
                    power(rs1, ve1, var1, rstd1, m)
                if l:
                    sum_cosh(l, 5)
                    square(l, 2)
                    square(l, 3)
                    causal(l, 0)
                if f:
                    clip_input(run, f)
                    pool.wait_ge(x_in.sem, x_in.at(f))
                    G.tensor_tensor(xres[:], x[:], bc(b_out0[:].unsqueeze(1), [P, BLK, D]), ALU.add).then_inc(xres_ready.sem, 1)
                if l:
                    square(l, 5)
                    causal(l, 1)
                    causal(l, 2)
                if m:
                    importance_products(run, m)
                if l:
                    causal(l, 3)
                    causal(l, 4)
                    causal(l, 5)
                for one in link.values():
                    one.end()

            phases(pool, iteration)

        @block.scalar
        def _(act):
            S = nc.scalar
            act.wait_ge(zeros_set, 1)
            zeros = lambda shape: bc(zero[:], shape)
            for n in range(2):
                S.activation(q_st[n][:].rearrange("p h e t -> p (h e t)"), zeros([P, HP * 2 * T]), ACT.Copy)
                S.activation(nmax2[n][:].rearrange("p k c -> p (k c)"), zeros([P, BLK * P]), ACT.Copy)
                last = S.activation(v_st[n][:].rearrange("p k h c -> p (k h c)"), zeros([P, BLK * H * 32]), ACT.Copy)
            last.then_inc(zeros_set, 1)
            act.wait_ge(zeros_set, 2)
            for n in range(2):
                last = S.activation(v_st[n][:].rearrange("p k h c -> p (k h) c")[:, :, HD], bc(minus1[:], [P, BLK * H]), ACT.Copy, scale=-1.0)
            last.then_inc(zeros_set, 1)
            with act.Fori(0, PRE_CHUNKS // 2) as c:
                for k in range(2):
                    act.wait_ge(pre_scale, c * 2 + k + 3)
                    apart(act)
                    tile = lambda n: px[k][:, bass.ds(c, 1), n, :].rearrange("p o d -> p (o d)")
                    for n in range(PRE):
                        last = S.activation(tile(n), tile(n), ACT.Identity, bias=pneg[k][:, bass.ds(c, 1), 0, n],
                                            scale=pscale[k][:, bass.ds(c, 1), 0, n])
                    last.then_inc(pre_normed, 1)
            act.wait_ge(weights_ready, 1)
            LOG_EXP, SILU = "natural_log_exp_and_others", "silu_and_others"

            def transposes0(run, f):
                u = misc(run, "xT")
                u.wait_full(act)
                S.activation(xn_t[:], u.ap[:, 0:T], ACT.Copy)
                act.wait_ge(xq_ready.sem, xq_ready.at(f, 0))
                S.activation(xa_t[:], u.ap[:, T:2 * T], ACT.Identity, bias=bet_col[:], scale=gam_col[:]).then_inc(u.free, 1)

            def hi_part(layer, other, s):
                if other:
                    act.wait_ge(scr_written[1 - layer].sem, scr_written[1 - layer].at(other))
                S.activation(parts[:, 0, :], qk_t[:], ACT.Copy).then_inc(hi_ready[layer].sem, 1)

            def operands0(run, f):
                u = misc(run, "qk")
                u.wait_full(act)
                if run.last:
                    act.wait_ge(parts_ready[1].sem, parts_ready[1].at(run.last))
                S.activation(qk_t[:, 0:T], u.ap[:, 0:T], ACT.Identity, bias=b_qk0[:, 0:1])
                S.activation(qk_t[:, T:2 * T], u.ap[:, T:2 * T], ACT.Identity, bias=b_qk0[:, 1:2]).then_inc(u.free, 1)
                u.wait_drained(act)
                hi_part(0, run.last, f)

            def copied(u, dst, src):
                u.wait_full(act)
                S.activation(dst, src, ACT.Copy).then_inc(u.free, 1)

            def latent_weights(run):
                u = misc(run, "lexp")
                u.wait_full(act)
                S.activation(prob_l[:].rearrange("p a q -> p (a q)"), u.ap, ACT.Exp, scale=SCALE).then_inc(u.free, 1)

            def weights0(run, n):
                u = unit(run, f"exp{n}")
                u.wait_full(act)
                S.activation(prob0[:, n * UNIT:(n + 1) * UNIT], u.ap, ACT.Exp, scale=SCALE).then_inc(u.free, 1)

            def gate_exp(m):
                act.wait_ge(glog_ready.sem, glog_ready.at(m))
                S.activation(gexp[:], glog[:], ACT.Exp, scale=-1.0).then_inc(gexp_ready.sem, 1)

            def importance_exp(l):
                act.wait_ge(imp_ready.sem, imp_ready.at(l))
                S.activation(eimp[:], imp[:], ACT.Exp, scale=-1.0).then_inc(eimp_ready.sem, 1)

            def norm_exps(m, link):
                act.wait_ge(mink_ready.sem, mink_ready.at(m))
                link(S.activation(lnw[:], mink[:], ACT.Ln))
                S.activation(rnom[:], lnw[:], ACT.Exp, scale=-0.5)
                link(S.activation(nom[:], lnw[:], ACT.Exp, scale=0.5))
                S.activation(epos[:], nom[:], ACT.Exp)
                S.activation(eneg[:], nom[:], ACT.Exp, scale=-1.0).then_inc(exps_ready.sem, 1)

            def operands1(run, m):
                u = misc(run, "embT")
                u.wait_full(act)
                if run.first:
                    act.wait_ge(parts_ready[0].sem, parts_ready[0].at(run.first))
                S.activation(qk_t[:], u.ap, ACT.Copy).then_inc(u.free, 1)
                u.wait_drained(act)
                hi_part(1, run.first, m)

            def silu(u, chunks):
                u.wait_full(act)
                for n, c in enumerate(chunks):
                    o = n * BANK
                    S.activation(gated[:, c, :], u.ap[:, o + T:o + 2 * T], ACT.Identity, scale=s2[:, c:c + 1])
                    last = S.activation(hid1[:, c, :], u.ap[:, o:o + T], ACT.Silu, scale=s1[:, c:c + 1])
                last.then_inc(u.free, 1)
                if chunks[-1] == HC - 1:
                    u.wait_drained(act)
                    act.sem_inc(sil_ready.sem, 1)

            def hidden(u, chunks, dst, g):
                u.wait_full(act)
                for n, c in enumerate(chunks):
                    last = S.activation(dst[:, c, :], u.ap[:, n * T:(n + 1) * T], ACT.Identity, scale=g[:, c:c + 1])
                last.then_inc(u.free, 1)

            def gelu(layer, done):
                flat = layer[:].rearrange("p c t -> p (c t)")
                S.activation(flat, flat, ACT.Gelu).then_inc(done.sem, 1)

            def square_cosh(run, n):
                c = slice(n * UNIT, (n + 1) * UNIT)
                unit(run, f"cosh{n}").wait_drained(act)
                S.activation(zs[:, c], zc[:, c], ACT.Square).then_inc(squared[n].sem, 1)

            def minima_root(l, link):
                act.wait_ge(zmin_ready.sem, zmin_ready.at(l))
                link(S.activation(zsq[:], zmin[:], ACT.Square))
                S.activation(zsr[:], zsq[:], ACT.Sqrt, bias=minus1[:]).then_inc(zsr_ready.sem, 1)

            def root(l, n):
                c = slice(n * UNIT, (n + 1) * UNIT)
                act.wait_ge(squared[n].sem, squared[n].at(l))
                S.activation(zs[:, c], zs[:, c], ACT.Sqrt, bias=minus1[:]).then_inc(sqrt_done.sem, 1)

            def minima_log(l):
                act.wait_ge(zsum_ready.sem, zsum_ready.at(l))
                S.activation(zd[:], zmin[:], ACT.Ln).then_inc(zln_ready.sem, 1)

            def log(l, n):
                c = slice(n * UNIT, (n + 1) * UNIT)
                done = sum_done[n in SUMMED_BY_POOL]
                act.wait_ge(done.sem, done.at(l, nth(n, SUMMED_BY_POOL)))
                S.activation(zs[:, c], zc[:, c], ACT.Ln).then_inc(ln_done.sem, 1)

            def square_log(l, n):
                c = slice(n * UNIT, (n + 1) * UNIT)
                act.wait_ge(ln_done.sem, ln_done.at(l, n + 1))
                S.activation(zs[:, c], zs[:, c], ACT.Square).then_inc(sq_done[0].sem, 1)

            def weights1(run, n):
                c = slice(n * UNIT, (n + 1) * UNIT)
                unit(run, f"sub{n}").wait_drained(act)
                S.activation(prob1[:, c], zc[:, c], ACT.Exp, scale=-SCALE).then_inc(exp1_done.sem, 1)

            def iteration(run):
                f, m, l, e, o = run.first, run.middle, run.last, run.end, run.out
                link = links_of(act, act_link, run)
                if l:
                    S.preload_act_table_set(SILU)
                    if e:
                        act.wait_ge(exp1_done.sem, exp1_done.at(e))
                    silu(unit(run.before(), "f1"), (0, 1))
                    silu(misc(run, "f1_2"), (2,))
                    silu(misc(run, "f1_3"), (3,))
                if o:
                    unit(run.before(), "f3").wait_drained(act)
                    gelu(hid3, hid3_ready)
                if e:
                    misc(run.before(), "f2_0").wait_drained(act)
                    misc(run.before(), "f2_1").wait_drained(act)
                    gelu(hid2, hid2_ready)
                if e:
                    copied(avuse(run, "av1"), o_t[:].rearrange("p v t -> p (v t)"), pav[:, :])
                if f:
                    transposes0(run, f)
                if e:
                    u = misc(run, "yT")
                    copied(u, out_t[:], u.ap[:, 0:T])
                if f:
                    operands0(run, f)
                if m:
                    u = misc(run, "mT")
                    copied(u, m_t[0][:], u.ap.bitcast(BF16)[:, 0:T])
                S.preload_act_table_set(LOG_EXP)
                if m:
                    latent_weights(run)
                for n in range(UNITS + 1):
                    if m and n < UNITS:
                        weights0(run, n)
                    if m and n == UNITS:
                        u = misc(run, "latT")
                        copied(u, lat_t[:], u.ap[0:LD, 0:T])
                    if l and n and n - 1 not in SQUARED_BY_POOL + SQUARED_BY_DVE:
                        square_cosh(run, n - 1)
                if l:
                    minima_root(l, link[L])
                    for n in range(UNITS):
                        root(l, n)
                S.preload_act_table_set(LOG_EXP)
                if l:
                    minima_log(l)
                if m:
                    gate_exp(m)
                if l:
                    log(l, 0)
                    square_log(l, 0)
                if m:
                    u = misc(run, "mixT")
                    copied(u, out_t[:], u.ap[:, 0:T])
                if l:
                    u = misc(run, "mT1")
                    copied(u, m_t[1][:], u.ap.bitcast(BF16)[:, 0:T])
                if l:
                    log(l, 1)
                    square_log(l, 1)
                    log(l, 2)
                if m:
                    u = misc(run, "x1T")
                    copied(u, xn1_t[:], u.ap[:, 0:T])
                if e:
                    hidden(unit(run, "f3"), range(HC), hid3, g2)
                if l:
                    log(l, 3)
                    importance_exp(l)
                    weights1(run, 0)
                    weights1(run, 1)
                    log(l, 4)
                if m:
                    norm_exps(m, link[M])
                if l:
                    square_log(l, 4)
                    log(l, 5)
                    hidden(misc(run, "f2_0"), (0, 1), hid2, g1)
                if m:
                    operands1(run, m)
                if l:
                    weights1(run, 2)
                    hidden(misc(run, "f2_1"), (2, 3), hid2, g1)
                    weights1(run, 3)
                    weights1(run, 4)
                    weights1(run, 5)
                for one in link.values():
                    one.end()

            phases(act, iteration)

        @block.tensor
        def _(pe):
            PE = nc.tensor
            pe.wait_ge(weights_ready, 1)

            def scores_by_query(u, layer, n, masks):
                u.wait_free(pe)
                per = 4 if n < 2 else 2
                width = BANK // per
                q = slice(0, P) if n < 2 else slice(P, T)
                for b in range(2):
                    bank = u.ap[:, b * BANK:(b + 1) * BANK]
                    for s in range(per):
                        h = (8 * n if n < 2 else 4 * (n - 2)) + per * b + s
                        PE.matmul(bank[:, s * width:(s + 1) * width], q_st[layer][:, h // 2, h % 2, q], k_st[layer][:, h // 2, 0:width],
                                  start=(s == 0), stop=False)
                    mask = masks[0 if n < 2 or layer else 1]
                    wide = mask.shape[1]
                    if n >= 2 and layer:
                        last = PE.matmul(bank.rearrange("p (h k) -> p h k", k=T)[:, :, P:T], ident_bf[:], masks[0][:, 0:2 * P], start=False, stop=True)
                        continue
                    for o in range(0, BANK, wide):
                        last = PE.matmul(bank[:, o:o + wide], ident_bf[:], mask[:], start=False, stop=(o + wide == BANK))
                last.then_inc(u.full, 1)

            def scores_by_key(u, layer, n, scores, shifts):
                u.wait_free(pe)
                for b in range(2):
                    if n < 4:
                        pairs, keys, queries, width = [2 * n + b], slice(0, P), slice(0, T), 2 * T
                    else:
                        pairs, keys, queries, width = [4 * (n - 4) + 2 * b, 4 * (n - 4) + 2 * b + 1], slice(P, T), slice(P, T), 2 * P
                    products = []
                    for s, hp in enumerate(pairs):
                        o, w = b * BANK + s * width, width // 2
                        if scores:
                            products.append((u.ap[:, o:o + width], k_st[layer][:, hp, keys], q_st[layer][:, hp, :, queries]))
                        if shifts:
                            products += [(u.ap[:, o + e * w:o + (e + 1) * w], sel[:, 2 * hp + e, :], m_t[layer][:, queries]) for e in range(2)]
                    for k, (dst, a, b_) in enumerate(products):
                        last = PE.matmul(dst, a, b_, start=(k == 0), stop=(k == len(products) - 1))
                last.then_inc(u.full, 1)

            def attend(use, layer, prob, groups=range(4)):
                if 0 in groups:
                    use.wait_free(pe)
                for v in groups:
                    for g in range(4):
                        h = 4 * v + g
                        PE.matmul(use.ap[32 * g:32 * g + 32, v * T:(v + 1) * T], v_st[layer][:, 0, h, :], prob[:, h * T:(h + 1) * T], start=True, stop=False)
                    for g in range(4):
                        h = 4 * v + g
                        last = PE.matmul(use.ap[32 * g:32 * g + 32, v * T + P:(v + 1) * T], v_st[layer][:, 1, h, :],
                                         prob[:, H * T + h * P:H * T + (h + 1) * P], start=False, stop=True)
                if 3 in groups:
                    last.then_inc(use.full, 1)

            def attended_t(use_t, layer):
                use_t.wait_free(pe)
                for k in range(BLK):
                    for v in range(4):
                        last = PE.transpose(use_t.ap[:, k * BANK + v * P:k * BANK + (v + 1) * P], o_t[:, v, k * P:(k + 1) * P], ident[:])
                last.then_inc(use_t.full, 1)

            def transposed(u, srcs):
                u.wait_free(pe)
                for n, src in enumerate(srcs):
                    last = PE.transpose(u.ap[:, n * P:(n + 1) * P], src, ident[:])
                last.then_inc(u.full, 1)

            def maxima_t(u, layer, s):
                pe.wait_ge(nmax_ready[layer].sem, nmax_ready[layer].at(s))
                u.wait_free(pe)
                for k in range(BLK):
                    last = PE.transpose(u.ap.bitcast(BF16)[:, k * P:(k + 1) * P], nmax2[layer][:, k, :], ident_bf[:])
                last.then_inc(u.full, 1)

            def project0(run):
                u = misc(run, "qk")
                misc(run, "xT").wait_drained(pe)
                u.wait_free(pe)
                PE.matmul(u.ap[:, 0:T], w_qkv0[:, 0:D], xn_t[:], start=True, stop=True)
                PE.matmul(u.ap[:, T:2 * T], w_qkv0[:, D:2 * D], xn_t[:], start=True, stop=True).then_inc(u.full, 1)

            def project_latent(run, f):
                u = misc(run, "rqkv")
                u.wait_free(pe)
                pe.wait_ge(pooled_ready.sem, pooled_ready.at(f))
                PE.matmul(u.ap[0:LD, 0:T], w_rq[:], xn_t[:], start=True, stop=True)
                PE.matmul(u.ap[0:LD, T:T + NLAT], w_rkv[:, 0:LD], pooled[:, 0, :], start=True, stop=True)
                PE.matmul(u.ap[:, T + NLAT:T + NLAT + LD], pooled[:].rearrange("p a l -> p (a l)"), w_rkv[:, LD:2 * LD], start=True, stop=True).then_inc(u.full, 1)

            def project_values0(run):
                u = misc(run, "v")
                u.wait_free(pe)
                for k in range(BLK):
                    last = PE.matmul(u.ap[:, k * P:(k + 1) * P], xn_t[:, k * P:(k + 1) * P], w_qkv0[:, 2 * D:3 * D], start=True, stop=True)
                last.then_inc(u.full, 1)

            def latent_scores(run, m):
                u = misc(run, "lmax")
                u.wait_free(pe)
                pe.wait_ge(rk_ready.sem, rk_ready.at(m))
                for k in range(BLK):
                    PE.matmul(u.ap[:, k * T:(k + 1) * T], rq_t[:, k * P:(k + 1) * P], rk_m[:].rearrange("p h l -> p (h l)"), start=(k == 0), stop=False)
                PE.matmul(u.ap, ident_bf[:], winl[:], start=False, stop=True).then_inc(u.full, 1)

            def latent_scores_t(run):
                u = misc(run, "lexp")
                misc(run, "mT").wait_drained(pe)
                u.wait_free(pe)
                for p in range(LH // 2):
                    PE.matmul(u.ap[:, p * T:(p + 1) * T], rk_m[:, 2 * p:2 * p + 2, :].rearrange("p h l -> p (h l)"), rq_t[:], start=(p == 0), stop=False)
                    PE.matmul(u.ap[:, p * T:(p + 1) * T], sel[:, H + p, :], m_t[0][:], start=False, stop=False)
                    last = PE.matmul(u.ap[:, p * T:(p + 1) * T], ident_bf[:], winl_t[:], start=False, stop=(p == LH // 2 - 1))
                last.then_inc(u.full, 1)

            def latent_attend(run, m):
                u = misc(run, "lo")
                u.wait_free(pe)
                misc(run, "lexp").wait_drained(pe)
                pe.wait_ge(rv_ready.sem, rv_ready.at(m))
                for p in range(LH // 2):
                    last = PE.matmul(u.ap[0:2 * LD, 0:T], rv_st[:, p, :], prob_l[:, p, :], start=(p == 0), stop=(p == LH // 2 - 1))
                last.then_inc(u.full, 1)

            def latent_tokens(run):
                misc(run, "lo").wait_drained(pe)
                u = misc(run, "loT")
                u.wait_free(pe)
                apart(pe)
                for k in range(BLK):
                    last = PE.transpose(u.ap[:, k * 2 * LD:(k + 1) * 2 * LD], lo_t[:, k * P:(k + 1) * P], ident[0:2 * LD, 0:2 * LD])
                last.then_inc(u.full, 1)

            def latent_back(run):
                misc(run, "loT").wait_drained(pe)
                u = misc(run, "latT")
                u.wait_free(pe)
                for k in range(BLK):
                    last = PE.transpose(u.ap[0:LD, k * P:(k + 1) * P], lat[:, k, :], ident[:])
                last.then_inc(u.full, 1)

            def latent_project(run):
                misc(run, "latT").wait_drained(pe)
                u = misc(run, "rem")
                u.wait_free(pe)
                for k in range(BLK):
                    last = PE.matmul(u.ap[:, k * D:(k + 1) * D], lat_t[:, k * P:(k + 1) * P], w_rout[:], start=True, stop=True)
                last.then_inc(u.full, 1)

            def mixed_t(run, m):
                pe.wait_ge(mixed_ready.sem, mixed_ready.at(m))
                transposed(misc(run, "mixT"), [mixed[:, 0, :], mixed[:, 1, :]])

            def layer0_out(run, m):
                misc(run, "mixT").wait_drained(pe)
                u = misc(run, "y0")
                u.wait_free(pe)
                pe.wait_ge(xq_ready.sem, xq_ready.at(m))
                for k in range(BLK):
                    c = slice(k * P, (k + 1) * P)
                    PE.matmul(u.ap[:, c], out_t[:, c], w_out0[:], start=True, stop=False)
                    last = PE.matmul(u.ap[:, c], xq_t[:, c], w_qs[:], start=False, stop=True)
                last.then_inc(u.full, 1)

            def project1(run):
                misc(run, "x1T").wait_drained(pe)
                for k, name in enumerate(("qkv1a", "qkv1b")):
                    u = misc(run, name)
                    u.wait_free(pe)
                    PE.matmul(u.ap[:, 0:3 * D], xn1_t[:, k * P:(k + 1) * P], w_qkv1[:], start=True, stop=True).then_inc(u.full, 1)

            def feed1(u, c, of):
                if c == of[0]:
                    u.wait_free(pe)
                w, o = slice(c * P, (c + 1) * P), (c - of[0]) * BANK
                PE.matmul(u.ap[:, o:o + T], w1t[:, w], xn1_t[:], start=True, stop=True)
                last = PE.matmul(u.ap[:, o + T:o + 2 * T], w2t[:, w], xn1_t[:], start=True, stop=True)
                if c == of[-1]:
                    last.then_inc(u.full, 1)

            def feed(u, w, src, chunks, of):
                if chunks[0] == of[0]:
                    u.wait_free(pe)
                for c in chunks:
                    for k in range(HC):
                        last = PE.matmul(u.ap[:, (c - of[0]) * T:(c - of[0] + 1) * T], w[:, k, c * P:(c + 1) * P], src[:, k, :], start=(k == 0), stop=(k == HC - 1))
                if chunks[-1] == of[-1]:
                    last.then_inc(u.full, 1)

            def feed_out(run, k):
                u = unit(run, "yffn")
                if k == 0:
                    u.wait_free(pe)
                c = slice(k * P, (k + 1) * P)
                for n in range(HC):
                    last = PE.matmul(u.ap[:, c], hid3[:, n, c], w3t[:, n, :], start=(n == 0), stop=(n == HC - 1))
                if k == BLK - 1:
                    last.then_inc(u.full, 1)

            def outputs_t(run):
                avuse(run, "avT1").wait_drained(pe)
                transposed(misc(run, "yT"), [y1[:, 0, :], y1[:, 1, :]])

            def output(run):
                misc(run, "yT").wait_drained(pe)
                u = misc(run, "y1")
                u.wait_free(pe)
                for k in range(BLK):
                    c = slice(k * P, (k + 1) * P)
                    last = PE.matmul(u.ap[:, c], out_t[:, c], w_out1[:], start=True, stop=True)
                last.then_inc(u.full, 1)

            def iteration(run):
                f, m, l, e, o = run.first, run.middle, run.last, run.end, run.out
                maxima = lambda *units: [scores_by_query(unit(run, f"max{n}"), 0, n, (win0, win1)) for n in units if m]
                minima = lambda *units: [scores_by_query(unit(run, f"min{n}"), 1, n, (cau0,)) for n in units if l]
                shifts = lambda *units: [scores_by_key(unit(run, f"sub{n}"), 1, n, False, True) for n in units if l]
                if m:
                    pe.wait_ge(stacked[0].sem, stacked[0].at(m))
                if l:
                    feed1(misc(run, "f1_2"), 2, (2,))
                maxima(0, 1)
                if l:
                    feed1(misc(run, "f1_3"), 3, (3,))
                maxima(2)
                if e:
                    pe.wait_ge(v1_ready.sem, v1_ready.at(e))
                    pe.wait_ge(masked1.sem, masked1.at(e))
                for v in range(4):
                    if v < 3:
                        maxima(v + 3)
                    if e:
                        attend(avuse(run, "av1"), 1, prob1, [v])
                if l:
                    pe.wait_ge(stacked[1].sem, stacked[1].at(l))
                minima(0)
                minima(1)
                if e:
                    attended_t(avuse(run, "avT1"), 1)
                if f:
                    pe.wait_ge(xf_ready.sem, xf_ready.at(f))
                    transposed(misc(run, "xT"), [xn[:, 0, :], xn[:, 1, :], xf[:, 0, :], xf[:, 1, :]])
                minima(2)
                if m:
                    latent_scores(run, m)
                if e:
                    outputs_t(run)
                minima(3)
                if f:
                    project0(run)
                if m:
                    maxima_t(misc(run, "mT"), 0, m)
                minima(4)
                if e:
                    output(run)
                minima(5)
                if m:
                    latent_scores_t(run)
                for n in range(UNITS):
                    if m:
                        scores_by_key(unit(run, f"exp{n}"), 0, n, True, True)
                    if l:
                        scores_by_key(unit(run, f"cosh{n}"), 1, n, True, False)
                    if m and n == 1:
                        latent_attend(run, m)
                    if m and n == 3:
                        latent_tokens(run)
                if o:
                    pe.wait_ge(hid3_ready.sem, hid3_ready.at(o))
                    feed_out(run, 0)
                if m:
                    latent_back(run)
                if o:
                    feed_out(run, 1)
                if m:
                    latent_project(run)
                if m:
                    pe.wait_ge(masked0.sem, masked0.at(m))
                    attend(avuse(run, "av0"), 0, prob0)
                if f:
                    project_values0(run)
                    project_latent(run, f)
                if m:
                    attended_t(avuse(run, "avT0"), 0)
                if e:
                    pe.wait_ge(hid2_ready.sem, hid2_ready.at(e))
                    feed(unit(run, "f3"), h2t, hid2, (0, 1, 2), range(HC))
                if m:
                    mixed_t(run, m)
                if m:
                    layer0_out(run, m)
                if l:
                    maxima_t(misc(run, "mT1"), 1, l)
                    misc(run, "mT1").wait_drained(pe)
                shifts(0, 1)
                if e:
                    feed(unit(run, "f3"), h2t, hid2, (3,), range(HC))
                if m:
                    pe.wait_ge(xn1_ready.sem, xn1_ready.at(m))
                    transposed(misc(run, "x1T"), [xn1[:, 0, :], xn1[:, 1, :]])
                if m:
                    project1(run)
                shifts(2, 3)
                if l:
                    pe.wait_ge(hid1_ready.sem, hid1_ready.at(l))
                    feed(misc(run, "f2_0"), h1t, hid1, (0, 1), (0, 1))
                    feed(misc(run, "f2_1"), h1t, hid1, (2,), (2, 3))
                if m:
                    feed1(unit(run, "f1"), 0, (0, 1))
                if m:
                    pe.wait_ge(emb_ready.sem, emb_ready.at(m))
                    transposed(misc(run, "embT"), [emb[:, 0, 0:D], emb[:, 1, 0:D], emb[:, 0, D:2 * D], emb[:, 1, D:2 * D]])
                if l:
                    feed(misc(run, "f2_1"), h1t, hid1, (3,), (2, 3))
                if m:
                    feed1(unit(run, "f1"), 1, (0, 1))
                shifts(4, 5)

            phases(pe, iteration)


_IN = ["L0_attn_x", "L0_attn_qkv_w", "L0_attn_qkv_b", "L0_attn_rq_w", "L0_attn_rq_b", "L0_attn_rkv_w", "L0_attn_rkv_b", "L0_attn_rout_w",
       "L0_attn_rout_b", "L0_attn_out_w", "L0_attn_out_b", "L0_attn_gl_w", "L0_attn_gr_w", "L0_ffn_weight", "L0_ffn_ln_gamma",
       "L0_ffn_ln_beta", "L1_attn_W_qkv", "L1_attn_b_qkv", "L1_attn_W_out", "L1_attn_b_out", "L1_attn_w_sur", "L1_attn_b_sur",
       "L1_attn_threshold", "L1_ffn_w1_s", "L1_ffn_w2_s", "L1_ffn_h1_s", "L1_ffn_h2_s", "L1_ffn_w3_s"]
_COLUMNS = ("L1_ffn_w1_s", "L1_ffn_w2_s", "L1_ffn_h1_s", "L1_ffn_h2_s")
_TRANSPOSED = {"w1t": "L1_ffn_w1_w", "w2t": "L1_ffn_w2_w", "h1t": "L1_ffn_h1_w", "h2t": "L1_ffn_h2_w", "w3t": "L1_ffn_w3_w"}


def kernel(**inputs):
    import concourse.bacc as bacc
    from concourse.bass_utils import run_bass_kernel_spmd

    nc = bacc.Bacc("TRN2", target_bir_lowering=False, num_devices=1)
    arrays, A = {}, {}
    laid = {n: np.ascontiguousarray(inputs[n]).reshape(inputs[n].shape or (1,)) for n in _IN}
    laid |= {n: np.ascontiguousarray(np.asarray(inputs[src]).T) for n, src in _TRANSPOSED.items()}
    laid["b_qk0_cols"] = np.ascontiguousarray(np.asarray(inputs["L0_attn_qkv_b"])[:2 * D].reshape(2, P).T)
    laid |= {n + "_cols": np.ascontiguousarray(laid.pop(n).reshape(HC, P).T) for n in _IN if n in _COLUMNS}
    laid |= shape_constants()
    for name, a in laid.items():
        arrays[f"in_{name}"] = a
        A[name] = nc.dram_tensor(f"in_{name}", list(a.shape), mybir.dt.from_np(a.dtype), kind="ExternalInput").ap()
    out = nc.dram_tensor("out_0", [NB, T, D], F32, kind="ExternalOutput").ap()
    build(nc, A, out)
    r = run_bass_kernel_spmd(nc, [arrays], core_ids=[0])
    return r.results[0]["out_0"]
```
